# Optimizing a Trainium2 kernel written in Bass

```python
import numpy as np
import jax
import jax.numpy as jnp

def _softmax(x, axis=-1):
    return jax.nn.softmax(x, axis=axis)

def _gelu(x):
    return jax.nn.gelu(x, approximate=True)

def _silu(x):
    return jax.nn.silu(x)

def _sigmoid(x):
    return jax.nn.sigmoid(x)

def _layernorm(x, axis=-1, eps=1e-05):
    m = jnp.mean(x, axis=axis, keepdims=True)
    v = jnp.var(x, axis=axis, keepdims=True)
    return (x - m) / jnp.sqrt(v + eps)

def _scatter_add(tgt, idx, src, axis=0):
    return tgt.at[idx].add(src)

def _segment_sum(src, seg, n):
    return jax.ops.segment_sum(src, seg, n)
kernel_name = 'mk_decoder_postln_d2_seqx_r4_32a2a8'

def setup_inputs(seed: int=0):
    np.random.seed(seed)
    _w = jnp.asarray

    def _rec_inputs():
        import jax
        import jax.numpy as jnp
        _rk = jax.random.key(seed)
        x = 7.22e-05 + 1 * jax.random.normal(jax.random.fold_in(_rk, 1), (8, 256, 256), jnp.float32)
        _lenS = 256 - jax.random.randint(jax.random.fold_in(_rk, 7), (8,), 0, max(1, 256 // 4) + 1, jnp.int32)
        _lenS2 = 256 - jax.random.randint(jax.random.fold_in(_rk, 8), (8,), 0, max(1, 256 // 4) + 1, jnp.int32)
        _ctx_1024P = jax.random.normal(jax.random.fold_in(_rk, 11), (8, 16, 256), jnp.float32)
        _ctx_1024c = jax.random.dirichlet(jax.random.fold_in(_rk, 511), 0.3 * jnp.ones((16,), jnp.float32), (8, 256))
        _ctx_1024t = jnp.einsum('bsk,bkd->bsd', _ctx_1024c, _ctx_1024P)
        _ctx_1024t = _ctx_1024t * jax.lax.rsqrt(jnp.mean(jnp.square(_ctx_1024t)) + 1e-12) * 0.953939
        ctx_1024 = 4.13588e-05 + 0.999923 * (_ctx_1024t + 0.3 * jax.random.normal(jax.random.fold_in(_rk, 611), (8, 256, 256), jnp.float32))
        return (x, ctx_1024)
    x, ctx_1024 = _rec_inputs()

    def _L0_attn_setup():
        import jax, jax.numpy as jnp
        import numpy as np
        DT_MIN, DT_MAX = (0.001, 0.1)
        DT_RANK, D_STATE = (64, 16)

        def _selective_scan(xp, delta, A, Bm, Cm):
            batch, L, d_inner = xp.shape
            d_state = A.shape[1]

            def step(h, inp):
                x_t, dt_t, B_t, C_t = inp
                A_bar = 1.0 + A[None] * dt_t[..., None]
                B_bar = B_t[:, None, :] * dt_t[..., None]
                h = A_bar * h + B_bar * x_t[..., None]
                y_t = jnp.sum(C_t[:, None, :] * h, axis=-1)
                return (h, y_t)
            h0 = jnp.zeros((batch, d_inner, d_state), xp.dtype)
            xs = (jnp.swapaxes(xp, 0, 1), jnp.swapaxes(delta, 0, 1), jnp.swapaxes(Bm, 0, 1), jnp.swapaxes(Cm, 0, 1))
            _, ys = jax.lax.scan(step, h0, xs)
            return jnp.swapaxes(ys, 0, 1)
        key = jax.random.key(seed)
        ks = jax.random.split(key, 8)
        B, L, D_MODEL, D_INNER = (2, 1024, 256, 512)
        s = 0.02
        return {'x': jax.random.normal(ks[0], (B, L, D_MODEL), jnp.float32), 'W_in': jax.random.normal(ks[1], (D_MODEL, 2 * D_INNER), jnp.float32) * s, 'W_xproj': jax.random.normal(ks[2], (D_INNER, DT_RANK + 2 * D_STATE), jnp.float32) * s, 'W_dt': jax.random.normal(ks[3], (DT_RANK, D_INNER), jnp.float32) * s, 'b_dt': jax.random.normal(ks[4], (D_INNER,), jnp.float32) * s, 'A_log': jnp.log(jax.random.uniform(ks[5], (D_INNER, D_STATE), jnp.float32) + 0.5), 'D': jnp.ones((D_INNER,), jnp.float32), 'W_out': jax.random.normal(ks[6], (D_INNER, D_MODEL), jnp.float32) * s}
    _L0_attn_all = _L0_attn_setup()
    _L0_attn_in = {k: v for k, v in _L0_attn_all.items() if k in ('W_in', 'W_xproj', 'W_dt', 'b_dt', 'A_log', 'D', 'W_out')}
    del _L0_attn_all

    def _L0_xattn_setup():
        import jax, jax.numpy as jnp
        import numpy as np
        from jax import lax
        NUM_HEADS = 16
        DIM = 256
        BATCH = 4
        SEQ = 512
        key = jax.random.key(seed)
        ks = jax.random.split(key, 12)
        f32 = jnp.float32
        q = jax.random.normal(ks[0], (BATCH, SEQ, DIM), dtype=f32)
        k = jax.random.normal(ks[1], (BATCH, SEQ, DIM), dtype=f32)
        v = jax.random.normal(ks[2], (BATCH, SEQ, DIM), dtype=f32)
        lim = 1.0 / np.sqrt(DIM)
        Wi = jax.random.uniform(ks[3], (DIM, DIM), minval=-lim, maxval=lim, dtype=f32)
        bi = jax.random.uniform(ks[4], (DIM,), minval=-lim, maxval=lim, dtype=f32)
        Wg = jax.random.uniform(ks[5], (DIM, DIM), minval=-lim, maxval=lim, dtype=f32)
        bg = jax.random.uniform(ks[6], (DIM,), minval=-lim, maxval=lim, dtype=f32)
        Wo = jax.random.uniform(ks[7], (DIM, DIM), minval=-lim, maxval=lim, dtype=f32)
        bo = jax.random.uniform(ks[8], (DIM,), minval=-lim, maxval=lim, dtype=f32)
        A = jax.random.normal(ks[9], (DIM, DIM), dtype=f32) * 0.1
        Bm = jax.random.normal(ks[10], (DIM, DIM), dtype=f32) * 0.1
        decay = jnp.full((1, NUM_HEADS, 1), 0.9, dtype=f32)
        return dict(q=q, k=k, v=v, Wi=Wi, bi=bi, Wg=Wg, bg=bg, A=A, Bm=Bm, Wo=Wo, bo=bo, decay=decay)
    _L0_xattn_all = _L0_xattn_setup()
    _L0_xattn_in = {k: v for k, v in _L0_xattn_all.items() if k in ('Wi', 'bi', 'Wg', 'bg', 'A', 'Bm', 'Wo', 'bo', 'decay')}
    del _L0_xattn_all

    def _L0_ffn_setup():
        import jax, jax.numpy as jnp
        import numpy as np
        HIDDEN = 256
        INNER = 1024

        def _weight_quant(w):
            scale = 1.0 / jnp.clip(jnp.mean(jnp.abs(w)), 1e-05)
            wq = jnp.clip(jnp.round(w * scale), -1.0, 1.0) / scale
            return w + jax.lax.stop_gradient(wq - w)

        def _act_quant(x):
            scale = 127.0 / jnp.clip(jnp.max(jnp.abs(x), axis=-1, keepdims=True), 1e-05)
            xq = jnp.clip(jnp.round(x * scale), -128.0, 127.0) / scale
            return x + jax.lax.stop_gradient(xq - x)

        def _bitlinear(x, w):
            return jnp.einsum('bsi,oi->bso', _act_quant(x), _weight_quant(w))
        key = jax.random.key(seed)
        k0, k1, k2, k3 = jax.random.split(key, 4)
        x = jax.random.normal(k0, (4, 512, HIDDEN), dtype=jnp.float32)
        w_gate = jax.random.normal(k1, (INNER, HIDDEN), dtype=jnp.float32) / np.sqrt(HIDDEN)
        w_up = jax.random.normal(k2, (INNER, HIDDEN), dtype=jnp.float32) / np.sqrt(HIDDEN)
        w_down = jax.random.normal(k3, (HIDDEN, INNER), dtype=jnp.float32) / np.sqrt(INNER)
        return {'x': x, 'w_gate': w_gate, 'w_up': w_up, 'w_down': w_down}
    _L0_ffn_all = _L0_ffn_setup()
    _L0_ffn_in = {k: v for k, v in _L0_ffn_all.items() if k in ('w_gate', 'w_up', 'w_down')}
    del _L0_ffn_all

    def _L1_attn_setup():
        import jax, jax.numpy as jnp
        import numpy as np
        H = 256
        NH = 16
        HD = H // NH
        B, S = (2, 512)
        key = jax.random.key(seed)
        ks = jax.random.split(key, 6)
        std = 0.02
        x = jax.random.normal(ks[0], (B, S, H), dtype=jnp.float32)
        w_qkv = jax.random.normal(ks[1], (3 * H, H), dtype=jnp.float32) * std
        b_qkv = jnp.zeros((3 * H,), dtype=jnp.float32)
        ln_g = jnp.ones((H,), dtype=jnp.float32)
        ln_b = jnp.zeros((H,), dtype=jnp.float32)
        w_ent = jax.random.normal(ks[2], (1, H), dtype=jnp.float32) * std
        b_ent = jnp.zeros((1,), dtype=jnp.float32)
        w_out = jax.random.normal(ks[3], (H, H), dtype=jnp.float32) * std
        b_out = jnp.zeros((H,), dtype=jnp.float32)
        return {'x': x, 'ln_g': ln_g, 'ln_b': ln_b, 'w_qkv': w_qkv, 'b_qkv': b_qkv, 'w_ent': w_ent, 'b_ent': b_ent, 'w_out': w_out, 'b_out': b_out}
    _L1_attn_all = _L1_attn_setup()
    _L1_attn_in = {k: v for k, v in _L1_attn_all.items() if k in ('ln_g', 'ln_b', 'w_qkv', 'b_qkv', 'w_ent', 'b_ent', 'w_out', 'b_out')}
    del _L1_attn_all

    def _L1_xattn_setup():
        import jax, jax.numpy as jnp
        import numpy as np
        DIM = 256
        NUM_HEADS = 16
        DIM_HEAD = 64
        INNER = NUM_HEADS * DIM_HEAD
        SCALE = DIM_HEAD ** (-0.5)

        def _layernorm(x, gamma, beta, eps=1e-05):
            mu = jnp.mean(x, axis=-1, keepdims=True)
            var = jnp.mean(jnp.square(x - mu), axis=-1, keepdims=True)
            return (x - mu) * jax.lax.rsqrt(var + eps) * gamma + beta
        key = jax.random.key(seed)
        ks = jax.random.split(key, 8)
        B, SQ, SK = (2, 512, 1024)
        x = jax.random.normal(ks[0], (B, SQ, DIM), dtype=jnp.float32)
        context = jax.random.normal(ks[1], (B, SK, DIM), dtype=jnp.float32)
        ln_gamma = jnp.ones((DIM,), jnp.float32)
        ln_beta = jnp.zeros((DIM,), jnp.float32)
        w_q = jax.random.normal(ks[2], (DIM, INNER), dtype=jnp.float32) / np.sqrt(DIM)
        w_kv = jax.random.normal(ks[3], (DIM, 2 * INNER), dtype=jnp.float32) / np.sqrt(DIM)
        w_out = jax.random.normal(ks[4], (INNER, DIM), dtype=jnp.float32) / np.sqrt(INNER)
        b_out = jnp.zeros((DIM,), jnp.float32)
        gate = jnp.array([0.5], jnp.float32)
        return {'x': x, 'context': context, 'ln_gamma': ln_gamma, 'ln_beta': ln_beta, 'w_q': w_q, 'w_kv': w_kv, 'w_out': w_out, 'b_out': b_out, 'gate': gate}
    _L1_xattn_all = _L1_xattn_setup()
    _L1_xattn_in = {k: v for k, v in _L1_xattn_all.items() if k in ('ln_gamma', 'ln_beta', 'w_q', 'w_kv', 'w_out', 'b_out', 'gate')}
    del _L1_xattn_all

    def _L1_ffn_setup():
        import jax, jax.numpy as jnp
        import numpy as np
        H = 256
        I = 1024
        E = 4
        LN_EPS = 1e-12

        def _layer_norm(x, gamma, beta, eps=LN_EPS):
            mu = jnp.mean(x, axis=-1, keepdims=True)
            var = jnp.mean(jnp.square(x - mu), axis=-1, keepdims=True)
            return (x - mu) * jax.lax.rsqrt(var + eps) * gamma + beta
        key = jax.random.key(seed)
        ks = jax.random.split(key, 8)
        B, S = (4, 128)
        scale = 0.02
        return {'hidden_states': jax.random.normal(ks[0], (B, S, H), jnp.float32), 'W_router': jax.random.normal(ks[1], (H, E), jnp.float32) * scale, 'W1': jax.random.normal(ks[2], (E, H, I), jnp.float32) * scale, 'b1': jax.random.normal(ks[3], (E, I), jnp.float32) * scale, 'Wo': jax.random.normal(ks[4], (I, H), jnp.float32) * scale, 'bo': jax.random.normal(ks[5], (H,), jnp.float32) * scale, 'ln_gamma': jnp.ones((H,), jnp.float32), 'ln_beta': jnp.zeros((H,), jnp.float32)}
    _L1_ffn_all = _L1_ffn_setup()
    _L1_ffn_in = {k: v for k, v in _L1_ffn_all.items() if k in ('W_router', 'W1', 'b1', 'Wo', 'bo', 'ln_gamma', 'ln_beta')}
    del _L1_ffn_all
    return {'x': x, 'ctx_1024': ctx_1024, 'L0_attn_W_in': _L0_attn_in['W_in'], 'L0_attn_W_xproj': _L0_attn_in['W_xproj'], 'L0_attn_W_dt': _L0_attn_in['W_dt'], 'L0_attn_b_dt': _L0_attn_in['b_dt'], 'L0_attn_A_log': _L0_attn_in['A_log'], 'L0_attn_D': _L0_attn_in['D'], 'L0_attn_W_out': _L0_attn_in['W_out'], 'L0_xattn_Wi': _L0_xattn_in['Wi'], 'L0_xattn_bi': _L0_xattn_in['bi'], 'L0_xattn_Wg': _L0_xattn_in['Wg'], 'L0_xattn_bg': _L0_xattn_in['bg'], 'L0_xattn_A': _L0_xattn_in['A'], 'L0_xattn_Bm': _L0_xattn_in['Bm'], 'L0_xattn_Wo': _L0_xattn_in['Wo'], 'L0_xattn_bo': _L0_xattn_in['bo'], 'L0_xattn_decay': _L0_xattn_in['decay'], 'L0_ffn_w_gate': _L0_ffn_in['w_gate'], 'L0_ffn_w_up': _L0_ffn_in['w_up'], 'L0_ffn_w_down': _L0_ffn_in['w_down'], 'L1_attn_ln_g': _L1_attn_in['ln_g'], 'L1_attn_ln_b': _L1_attn_in['ln_b'], 'L1_attn_w_qkv': _L1_attn_in['w_qkv'], 'L1_attn_b_qkv': _L1_attn_in['b_qkv'], 'L1_attn_w_ent': _L1_attn_in['w_ent'], 'L1_attn_b_ent': _L1_attn_in['b_ent'], 'L1_attn_w_out': _L1_attn_in['w_out'], 'L1_attn_b_out': _L1_attn_in['b_out'], 'L1_xattn_ln_gamma': _L1_xattn_in['ln_gamma'], 'L1_xattn_ln_beta': _L1_xattn_in['ln_beta'], 'L1_xattn_w_q': _L1_xattn_in['w_q'], 'L1_xattn_w_kv': _L1_xattn_in['w_kv'], 'L1_xattn_w_out': _L1_xattn_in['w_out'], 'L1_xattn_b_out': _L1_xattn_in['b_out'], 'L1_xattn_gate': _L1_xattn_in['gate'], 'L1_ffn_W_router': _L1_ffn_in['W_router'], 'L1_ffn_W1': _L1_ffn_in['W1'], 'L1_ffn_b1': _L1_ffn_in['b1'], 'L1_ffn_Wo': _L1_ffn_in['Wo'], 'L1_ffn_bo': _L1_ffn_in['bo'], 'L1_ffn_ln_gamma': _L1_ffn_in['ln_gamma'], 'L1_ffn_ln_beta': _L1_ffn_in['ln_beta']}

def reference(x, ctx_1024, L0_attn_W_in, L0_attn_W_xproj, L0_attn_W_dt, L0_attn_b_dt, L0_attn_A_log, L0_attn_D, L0_attn_W_out, L0_xattn_Wi, L0_xattn_bi, L0_xattn_Wg, L0_xattn_bg, L0_xattn_A, L0_xattn_Bm, L0_xattn_Wo, L0_xattn_bo, L0_xattn_decay, L0_ffn_w_gate, L0_ffn_w_up, L0_ffn_w_down, L1_attn_ln_g, L1_attn_ln_b, L1_attn_w_qkv, L1_attn_b_qkv, L1_attn_w_ent, L1_attn_b_ent, L1_attn_w_out, L1_attn_b_out, L1_xattn_ln_gamma, L1_xattn_ln_beta, L1_xattn_w_q, L1_xattn_w_kv, L1_xattn_w_out, L1_xattn_b_out, L1_xattn_gate, L1_ffn_W_router, L1_ffn_W1, L1_ffn_b1, L1_ffn_Wo, L1_ffn_bo, L1_ffn_ln_gamma, L1_ffn_ln_beta):
    import jax
    import jax.numpy as jnp

    def _L0_attn_ref(x, W_in, W_xproj, W_dt, b_dt, A_log, D, W_out):
        import jax, jax.numpy as jnp
        import numpy as np
        DT_MIN, DT_MAX = (0.001, 0.1)
        DT_RANK, D_STATE = (64, 16)

        def _selective_scan(xp, delta, A, Bm, Cm):
            batch, L, d_inner = xp.shape
            d_state = A.shape[1]

            def step(h, inp):
                x_t, dt_t, B_t, C_t = inp
                A_bar = 1.0 + A[None] * dt_t[..., None]
                B_bar = B_t[:, None, :] * dt_t[..., None]
                h = A_bar * h + B_bar * x_t[..., None]
                y_t = jnp.sum(C_t[:, None, :] * h, axis=-1)
                return (h, y_t)
            h0 = jnp.zeros((batch, d_inner, d_state), xp.dtype)
            xs = (jnp.swapaxes(xp, 0, 1), jnp.swapaxes(delta, 0, 1), jnp.swapaxes(Bm, 0, 1), jnp.swapaxes(Cm, 0, 1))
            _, ys = jax.lax.scan(step, h0, xs)
            return jnp.swapaxes(ys, 0, 1)
        xz = x @ W_in
        xp, z = jnp.split(xz, 2, axis=-1)
        x_dbl = xp @ W_xproj
        dlt, Bm, Cm = jnp.split(x_dbl, [DT_RANK, DT_RANK + D_STATE], axis=-1)
        delta = jnp.clip(jax.nn.softplus(dlt @ W_dt + b_dt), DT_MIN, DT_MAX)
        A = -jnp.exp(A_log)
        y = _selective_scan(xp, delta, A, Bm, Cm)
        y = y + D[None, None, :] * xp
        y = y * jax.nn.silu(z)
        return y @ W_out

    def _L0_xattn_ref(q, k, v, Wi, bi, Wg, bg, A, Bm, Wo, bo, decay):
        import jax, jax.numpy as jnp
        import numpy as np
        from jax import lax
        NUM_HEADS = 16
        DIM = 256
        BATCH = 4
        SEQ = 512
        B, S, D = q.shape
        H = decay.shape[1]
        hd = D // H
        qh = jnp.moveaxis(q.reshape(B, S, H, hd), 1, 0)
        kh = jnp.moveaxis(k.reshape(B, S, H, hd), 1, 0)
        vh = jnp.moveaxis(v.reshape(B, S, H, hd), 1, 0)

        def step(carry, xs):
            r, state = carry
            qt, kt, vt = xs
            r = decay * r + kt * vt
            retained = (qt * r).reshape(B, D)
            inp = retained @ Wi.T + bi
            gate = jax.nn.sigmoid(inp @ Wg.T + bg)
            blended = gate * state + (1.0 - gate) * inp
            state = jnp.tanh(blended @ A.T + inp @ Bm.T)
            out = state @ Wo.T + bo
            return ((r, state), out)
        r0 = jnp.zeros((B, H, hd), dtype=q.dtype)
        s0 = jnp.zeros((B, D), dtype=q.dtype)
        _, outs = lax.scan(step, (r0, s0), (qh, kh, vh))
        return jnp.moveaxis(outs, 0, 1)

    def _L0_ffn_ref(x, w_gate, w_up, w_down):
        import jax, jax.numpy as jnp
        import numpy as np
        HIDDEN = 256
        INNER = 1024

        def _weight_quant(w):
            scale = 1.0 / jnp.clip(jnp.mean(jnp.abs(w)), 1e-05)
            wq = jnp.clip(jnp.round(w * scale), -1.0, 1.0) / scale
            return w + jax.lax.stop_gradient(wq - w)

        def _act_quant(x):
            scale = 127.0 / jnp.clip(jnp.max(jnp.abs(x), axis=-1, keepdims=True), 1e-05)
            xq = jnp.clip(jnp.round(x * scale), -128.0, 127.0) / scale
            return x + jax.lax.stop_gradient(xq - x)

        def _bitlinear(x, w):
            return jnp.einsum('bsi,oi->bso', _act_quant(x), _weight_quant(w))
        gate = jax.nn.silu(_bitlinear(x, w_gate))
        up = _bitlinear(x, w_up)
        return _bitlinear(gate * up, w_down)

    def _L1_attn_ref(x, ln_g, ln_b, w_qkv, b_qkv, w_ent, b_ent, w_out, b_out):
        import jax, jax.numpy as jnp
        import numpy as np
        H = 256
        NH = 16
        HD = H // NH
        B, S = (2, 512)
        b, s, h = x.shape
        scale = 1.0 / jnp.sqrt(jnp.float32(HD))
        TEMP = 0.1
        mu = jnp.mean(x, axis=-1, keepdims=True)
        var = jnp.mean(jnp.square(x - mu), axis=-1, keepdims=True)
        xn = (x - mu) / jnp.sqrt(var + 1e-06) * ln_g + ln_b
        qkv = xn @ w_qkv.T + b_qkv
        qkv = qkv.reshape(b, s, 3, NH, HD).transpose(2, 0, 3, 1, 4)
        q, k, v = (qkv[0], qkv[1], qkv[2])
        scores = jnp.einsum('bhqd,bhkd->bhqk', q, k) * scale
        causal = jnp.tril(jnp.ones((s, s), dtype=bool))
        scores = jnp.where(causal[None, None], scores, -jnp.inf)
        probs = jax.nn.softmax(scores / TEMP, axis=-1)
        gate = jax.nn.sigmoid(xn @ w_ent.T + b_ent)
        gate = jnp.clip(gate, 0.1, 2.0)[:, None, None, :, 0]
        probs = probs * gate
        out = jnp.einsum('bhqk,bhkd->bhqd', probs, v)
        out = out.transpose(0, 2, 1, 3).reshape(b, s, h)
        return (out @ w_out.T + b_out) * 0.1

    def _L1_xattn_ref(x, context, ln_gamma, ln_beta, w_q, w_kv, w_out, b_out, gate):
        import jax, jax.numpy as jnp
        import numpy as np
        DIM = 256
        NUM_HEADS = 16
        DIM_HEAD = 64
        INNER = NUM_HEADS * DIM_HEAD
        SCALE = DIM_HEAD ** (-0.5)

        def _layernorm(x, gamma, beta, eps=1e-05):
            mu = jnp.mean(x, axis=-1, keepdims=True)
            var = jnp.mean(jnp.square(x - mu), axis=-1, keepdims=True)
            return (x - mu) * jax.lax.rsqrt(var + eps) * gamma + beta
        B, SQ, _ = x.shape
        SK = context.shape[1]
        xn = _layernorm(x, ln_gamma, ln_beta)
        q = (xn @ w_q).reshape(B, SQ, NUM_HEADS, DIM_HEAD)
        kv = context @ w_kv
        k, v = jnp.split(kv, 2, axis=-1)
        k = k.reshape(B, SK, NUM_HEADS, DIM_HEAD)
        v = v.reshape(B, SK, NUM_HEADS, DIM_HEAD)
        scores = jnp.einsum('bqhd,bkhd->bhqk', q * SCALE, k)
        attn = jax.nn.softmax(scores, axis=-1)
        out = jnp.einsum('bhqk,bkhd->bqhd', attn, v).reshape(B, SQ, INNER)
        out = out @ w_out + b_out
        return out * jnp.tanh(gate[0])

    def _L1_ffn_ref(hidden_states, W_router, W1, b1, Wo, bo, ln_gamma, ln_beta):
        import jax, jax.numpy as jnp
        import numpy as np
        H = 256
        I = 1024
        E = 4
        LN_EPS = 1e-12

        def _layer_norm(x, gamma, beta, eps=LN_EPS):
            mu = jnp.mean(x, axis=-1, keepdims=True)
            var = jnp.mean(jnp.square(x - mu), axis=-1, keepdims=True)
            return (x - mu) * jax.lax.rsqrt(var + eps) * gamma + beta
        B, S, _ = hidden_states.shape
        x = hidden_states.reshape(-1, H)
        logits = x @ W_router
        expert_idx = jnp.argmax(logits, axis=-1)
        h = jnp.einsum('th,ehi->tei', x, W1) + b1
        h = jax.nn.gelu(h, approximate=False)
        onehot = jax.nn.one_hot(expert_idx, E, dtype=x.dtype)
        intermediate = jnp.einsum('te,tei->ti', onehot, h)
        y = intermediate @ Wo + bo + x
        y = _layer_norm(y, ln_gamma, ln_beta)
        return y.reshape(B, S, H)
    x = _layernorm(x + _L0_attn_ref(x, L0_attn_W_in, L0_attn_W_xproj, L0_attn_W_dt, L0_attn_b_dt, L0_attn_A_log, L0_attn_D, L0_attn_W_out), axis=-1)
    x = _layernorm(x + _L0_xattn_ref(x, ctx_1024, ctx_1024, L0_xattn_Wi, L0_xattn_bi, L0_xattn_Wg, L0_xattn_bg, L0_xattn_A, L0_xattn_Bm, L0_xattn_Wo, L0_xattn_bo, L0_xattn_decay), axis=-1)
    x = _layernorm(x + _L0_ffn_ref(x, L0_ffn_w_gate, L0_ffn_w_up, L0_ffn_w_down), axis=-1)
    x = _layernorm(x + _L1_attn_ref(x, L1_attn_ln_g, L1_attn_ln_b, L1_attn_w_qkv, L1_attn_b_qkv, L1_attn_w_ent, L1_attn_b_ent, L1_attn_w_out, L1_attn_b_out), axis=-1)
    x = _layernorm(x + _L1_xattn_ref(x, ctx_1024, L1_xattn_ln_gamma, L1_xattn_ln_beta, L1_xattn_w_q, L1_xattn_w_kv, L1_xattn_w_out, L1_xattn_b_out, L1_xattn_gate), axis=-1)
    x = _layernorm(x + _L1_ffn_ref(x, L1_ffn_W_router, L1_ffn_W1, L1_ffn_b1, L1_ffn_Wo, L1_ffn_bo, L1_ffn_ln_gamma, L1_ffn_ln_beta), axis=-1)
    return x

_drawn_inputs = setup_inputs


def setup_inputs(seed=0):
    import zlib

    import numpy as np

    out = dict(_drawn_inputs(seed))
    spreads = {'L0_attn_D': (1.0, 0.2),
     'L0_xattn_decay': (0.8999999761581421, 0.2),
     'L1_attn_ln_g': (1.0, 0.6),
     'L1_attn_ln_b': (0.0, 0.8),
     'L1_attn_b_qkv': (0.0, 0.8),
     'L1_attn_b_out': (0.0, 0.651),
     'L1_xattn_ln_gamma': (1.0, 0.6),
     'L1_xattn_ln_beta': (0.0, 0.702),
     'L1_xattn_b_out': (0.0, 0.1),
     'L1_ffn_ln_gamma': (1.0, 0.2),
     'L1_ffn_ln_beta': (0.0, 0.1)}
    factors = {'L0_attn_W_xproj': 2.801,
     'L0_attn_A_log': 6.008,
     'L0_xattn_bi': 8.0,
     'L0_xattn_bg': 8.0,
     'L1_attn_w_qkv': 8.0,
     'L1_attn_w_ent': 8.0,
     'L1_attn_w_out': 8.0,
     'L1_ffn_b1': 8.0,
     'L1_ffn_bo': 5.335}
    for name, (base, spread) in spreads.items():
        noise = np.random.default_rng([zlib.crc32(name.encode()), seed]).standard_normal(out[name].shape)
        drawn = base * np.exp(spread * noise) if base else spread * noise
        out[name] = jnp.asarray(drawn.astype(out[name].dtype))
    for name, factor in factors.items():
        out[name] = (out[name] * factor).astype(out[name].dtype)
    return out
```

```python
from contextlib import ExitStack

import concourse.bass as bass
from concourse import mybir

P = 128
F32 = mybir.dt.float32
BF16 = mybir.dt.bfloat16
FP16 = mybir.dt.float16
ALU = mybir.AluOpType
ACT = mybir.ActivationFunctionType
AX = mybir.AxisListType

B, S, D = 8, 256, 256
T = B * S
KD = D // P
NCH = 4
TC = S // NCH
CC = B * TC
DI = 512
ND = DI // P
NS = 16
DTR = 64
NH = 16
HG = NH // 2
XI = 1024
NP = NH // 2
F = 1024
NF = F // P
NE = 4
MAGIC = 1.5 * 2.0 ** 23
TINY = 1e-5
SOFT = 2.5
GSC = 1024.0

COLS = {}
_at = 0
for _name, _n in (("b_dt", 4), ("A_log", 64), ("Dskip", 4), ("bi", 2), ("bg", 2), ("decay", 2),
                  ("ln_g", 2), ("ln_b", 2), ("bq", 2), ("bk", 2), ("gam", 2), ("bet", 2),
                  ("b_ent", 1), ("gate", 1)):
    COLS[_name] = (_at, _at + _n)
    _at += _n
NCOLS = _at
ROWS = ["bo", "b_out", "bv", "b_out2", "bo_ffn", "lng", "lnb"]


class Own:

    def __init__(self, eng, sem):
        self.eng, self.sem, self.base, self.n = eng, sem, 0, 0

    def did(self, ins):
        ins.then_inc(self.sem, 1)
        self.n += 1

    def wait(self):
        self.eng.wait_ge(self.sem, self.base + self.n)

    def enter(self, i, per):
        self.start, self.per = self.base + self.n, per
        self.base, self.n = self.start + i * per, 0

    def leave(self, count):
        assert self.n == self.per, (self.n, self.per)
        self.base, self.n = self.start + count * self.per, 0


class Plan:

    def __init__(self, full, free, base, uses, trips):
        self.full, self.free, self.base, self.bank, self.pos = full, free, list(base), {}, {}
        self.per = [0] * 8
        for key, bank in uses:
            self.bank[key], self.pos[key] = bank, self.per[bank]
            self.per[bank] += 1
        self.end = [a + trips * n for a, n in zip(self.base, self.per)]

    def count(self, key, i):
        b = self.bank[key]
        return self.base[b] + i * self.per[b] + self.pos[key]

    def wait_full(self, eng, key, i):
        eng.wait_ge(self.full[self.bank[key]], self.count(key, i) + 1)

    def wait_free(self, eng, key, i):
        eng.wait_ge(self.free[self.bank[key]], self.count(key, i) + 1)

    def wait_freed(self, eng, key, i):
        eng.wait_ge(self.free[self.bank[key]], self.count(key, i) + 2)

    def fills(self, ins, key):
        ins.then_inc(self.full[self.bank[key]], 1)

    def frees(self, ins, key):
        ins.then_inc(self.free[self.bank[key]], 1)


def build_program(nc, dr):
    ctx = ExitStack()
    with ctx:
        def sb(name, shape, dt=F32):
            return ctx.enter_context(nc.sbuf_tensor(name, shape, dt))

        def ps(name, shape, dt=F32):
            return ctx.enter_context(nc.psum_tensor(name, shape, dt))

        def sem(name):
            return ctx.enter_context(nc.semaphore(name))

        cols = sb("cols", [P, NCOLS])
        rows = sb("rows", [P, len(ROWS), D])
        ident = sb("ident", [P, P])
        identb = sb("identb", [P, P], BF16)
        causal = sb("causal", [P, P], BF16)
        headm = sb("headm", [P, 8])
        x_tok = sb("x_tok", [P, 16, D])

        def col(name, j=0):
            a = COLS[name][0]
            return cols[:, a + j:a + j + 1]

        def row(name):
            return rows[:, ROWS.index(name), :]

        front = ExitStack()
        fsb = lambda name, shape, dt=F32: front.enter_context(nc.sbuf_tensor(name, shape, dt))
        w_in = fsb("w_in", [P, KD, 2 * DI])
        w_xp = fsb("w_xp", [P, ND, 96])
        w_dt = fsb("w_dt", [DTR, DI])
        w_o0 = fsb("w_o0", [P, ND, D])
        w_ch = fsb("w_ch", [P, 5, KD, D])
        wi_t, wg_t, a_t, bm_t, wo_t = (w_ch[:, j] for j in range(5))
        a_neg = fsb("a_neg", [P, KD, D])
        a_parts = [fsb(f"a_part{j}", [P, KD, D], BF16) for j in range(3)]
        a_coef = fsb("a_coef", [P, NS * ND])
        d_diag = fsb("d_diag", [P, ND, P])
        causal_f = fsb("causal_f", [P, P])
        ctxT = fsb("ctxT", [P, KD, T])
        work4 = fsb("work4", [P, 4, KD * CC])
        kv = work4[:, :, :].rearrange("p (k a) c -> p k (a c)", k=KD)
        ret = work4[:, 0, :].rearrange("p (k c) -> p k c", k=KD)
        inp = work4[:, 1, :].rearrange("p (k c) -> p k c", k=KD)
        gate = work4[:, 2, :].rearrange("p (k c) -> p k c", k=KD)
        gsc = work4[:, 3, :].rearrange("p (t c) -> p t c", t=TC)
        xTc = fsb("xTc", [P, 2, KD, CC])
        xtk = fsb("xtk", [P, 2, 4, D])
        xp = fsb("xp", [P, ND, CC])
        zs = fsb("zs", [P, ND, CC])
        xd = fsb("xd", [96, CC])
        ee = fsb("ee", [P, ND, CC])
        um = fsb("um", [P, ND, CC])
        bc = fsb("bc", [P, 2, 2, CC])
        abar = fsb("abar", [P, 2, B, TC + 1])
        dbx = fsb("dbx", [P, 2, B, TC + 1])
        scan_out = fsb("scan_out", [P, 2 * B * (TC + 1) + 2 * CC])
        hh = scan_out[:, 0:2 * B * (TC + 1)].rearrange("p (a b t) -> p a b t", a=2, b=B)
        hc = scan_out[:, 2 * B * (TC + 1):].rearrange("p (a c) -> p a c", a=2)
        lnu = scan_out[:, 0:ND * CC].rearrange("p (d c) -> p d c", d=ND)
        hstate = fsb("hstate", [P, NS * ND, B])
        pf = fsb("pf", [P, TC, KD * B])
        pparts = fsb("pparts", [P, TC, 3, KD * B], BF16)
        states = fsb("states", [P, KD * B, TC])
        s_cur = fsb("s_cur", [P, 2, KD * B])
        gsf = fsb("gsf", [P, KD * B])
        gs2 = fsb("gs2", [P, 2, KD * B], FP16)
        x1 = fsb("x1", [P, 2, 4, D])
        res = fsb("res", [P, 4, D])
        x2c = fsb("x2c", [P, 2, 4, D])
        st6 = fsb("st6", [P, 4, 6])
        mv = fsb("mv", [P, 4, 2])
        lu = fsb("lu", [P, 4])
        lr = fsb("lr", [P, 4])
        l1 = fsb("l1", [P, 4])
        l2 = fsb("l2", [P, 4])

        front.close()

        ones = sb("ones", [P, P])
        prio = sb("prio", [P, 2, NE])
        wg_q = sb("wg_q", [P, KD, F], BF16)
        wu_q = sb("wu_q", [P, KD, F], BF16)
        wd_q = sb("wd_q", [P, NF, D], BF16)
        wsum = sb("wsum", [P, 3])
        wmean = sb("wmean", [P, 3])
        wrec = sb("wrec", [P, 3])
        w_qk = sb("w_qk", [P, KD, 2 * D])
        w_v = sb("w_v", [P, KD, D])
        w_ent = sb("w_ent", [P, KD])
        w_o1 = sb("w_o1", [P, KD, D])
        w_xq = sb("w_xq", [P, KD, XI])
        w_xkv = sb("w_xkv", [P, KD, 2 * XI])
        w_o2 = sb("w_o2", [P, NP, D])
        w_1 = sb("w_1", [P, NE * KD, F])
        w_raw = w_1[:, 0:6, :].rearrange("p (a k) n -> p a (k n)", a=3)
        b_1 = sb("b_1", [P, F])
        w_o3 = sb("w_o3", [P, NF, D])
        w_r = sb("w_r", [P, KD, NE])
        bk_m = sb("bk_m", [P, NH])
        bq_s = sb("bq_s", [P, KD])
        tg = sb("tg", [P, 1])
        nb_ent = sb("nb_ent", [P, 1])
        stats6 = sb("stats6", [P, 2, 6])
        mvb = sb("mvb", [P, 2, 2])
        lub = sb("lub", [P, 2])
        lrb = sb("lrb", [P, 2])
        l1b = sb("l1b", [P, 2])
        l2b = sb("l2b", [P, 2])
        resb = sb("resb", [P, 2, D])
        qv = sb("qv", [P, 12, 2])

        def work(fn):
            with ExitStack() as region:
                return fn(lambda name, shape, dt=F32: region.enter_context(nc.sbuf_tensor(name, shape, dt)))

        f_b = work(lambda w: dict(tmp=w("f_tmp", [P, 2, F]), xq=w("f_xq", [P, 2, D], BF16), xqT=w("f_xqT", [P, 2, KD, P], BF16),
                                  sg=w("f_sg", [P, 2, F]), hv=w("f_hv", [P, 2, F]), hq=w("f_hq", [P, 2, F], BF16),
                                  hqT=w("f_hqT", [P, 2, NF, P], BF16)))
        a_b = work(lambda w: dict(xn=w("a_xn", [P, 2, D]), xnT=w("a_xnT", [P, KD, S]), qT=w("a_qT", [P, KD, S]),
                                  km=w("a_km", [P, NH, S]), vm=w("a_vm", [P, 2, 2, HG * (P + 16)]), nm=w("a_nm", [P, NH, 2]),
                                  sm=w("a_sm", [P, NH, 2]), rr=w("a_rr", [P, NH, 2]), e=w("a_e", [P, 4, 384]),
                                  pt=w("a_pt", [P, 4, 384]), oT=w("a_oT", [P, KD, S]), gt=w("a_gt", [P, 4, 2])))
        x_b = work(lambda w: dict(xn=w("x_xn", [P, 2, D]), xnT=w("x_xnT", [P, KD, S]), cT=w("x_cT", [P, KD, S]),
                                  qT=w("x_qT", [P, NP, S]), kz=w("x_kz", [P, NH, S]), v=w("x_v", [P, 2, XI]),
                                  nm=w("x_nm", [P, NH, 2]), sm=w("x_sm", [P, NH, 2]), rr=w("x_rr", [P, NH, 2]),
                                  e=w("x_e", [P, 4, 2 * S]), pt=w("x_pt", [P, 2, 2 * S]), oT=w("x_oT", [P, NP, S])))
        m_b = work(lambda w: dict(xs=w("m_xs", [P, 2, D]), xT=w("m_xT", [P, KD, S]), lg=w("m_lg", [P, 2, NE]),
                                  oh=w("m_oh", [P, 2, NE]), mx=w("m_mx", [P, 4, 2]), xm=w("m_xm", [P, 2, NE, D]),
                                  xmT=w("m_xmT", [P, NE, KD, S]), ohT=w("m_ohT", [P, S]), hT=w("m_hT", [P, NF, S]),
                                  y=w("m_y", [P, 2, D]), o=w("m_o", [P, 2, D])))

        ybank = [ps(f"ybank{d}", [P, 512]) for d in range(4)]
        cbank = [ps(f"cbank{j}", [P, 512]) for j in range(2)]
        gbank = [ps(f"gbank{j}", [P, 512]) for j in range(2)]
        banks = ybank + cbank + gbank

        in_w = sem("in_w")
        in_w2 = sem("in_w2")
        in_ctx = sem("in_ctx")
        in_xT = [sem(f"in_xT{j}") for j in range(2)]
        in_xtk = [sem(f"in_xtk{j}") for j in range(2)]
        setup_dve = sem("setup_dve")
        setup_act = sem("setup_act")
        dve_own = sem("dve_own")
        act_own = sem("act_own")
        g_full = [sem(f"g_full{j}") for j in range(2)]
        g_free = [sem(f"g_free{j}") for j in range(2)]
        xd_ready = sem("xd_ready")
        xp_ready = sem("xp_ready")
        zs_ready = sem("zs_ready")
        bc_stored = sem("bc_stored")
        bc_loaded = [sem(f"bc_loaded{j}") for j in range(2)]
        e_ready = sem("e_ready")
        ec_ready = sem("ec_ready")
        lnu_ready = sem("lnu_ready")
        dt_ready = sem("dt_ready")
        seeded = sem("seeded")
        abar_ready = sem("abar_ready")
        scans = sem("scans")
        h_saved = sem("h_saved")
        hc_ready = sem("hc_ready")
        h_in = sem("h_in")
        hc_used = sem("hc_used")
        gs_ready = sem("gs_ready")
        chain_mm = sem("chain_mm")
        tanh_done = sem("tanh_done")
        y_ready = sem("y_ready")
        ln_u = sem("ln_u")
        ln_r = sem("ln_r")
        x1_ready = sem("x1_ready")
        ret_ready = sem("ret_ready")
        inp_ready = sem("inp_ready")
        gate_ready = sem("gate_ready")
        om_ready = sem("om_ready")
        pf_ready = sem("pf_ready")
        p_ready = sem("p_ready")
        st_copied = sem("st_copied")
        x2_ready = sem("x2_ready")
        x2_moved = [sem(f"x2_moved{j}") for j in range(2)]
        b_full = [sem(f"b_full{j}") for j in range(8)]
        b_free = [sem(f"b_free{j}") for j in range(8)]
        in_b1 = sem("in_b1")
        in_b2 = sem("in_b2")
        in_b3 = sem("in_b3")
        front_done = sem("front_done")
        w_summed = sem("w_summed")
        w_total = sem("w_total")
        w_ready = sem("w_ready")
        act_set = sem("act_set")
        dve_set = sem("dve_set")
        pool_set = sem("pool_set")
        stats_seen = sem("stats_seen")
        b_lnu = sem("b_lnu")
        b_lnr = sem("b_lnr")
        f_xq = sem("f_xq")
        f_xqT = sem("f_xqT")
        f_sg = sem("f_sg")
        f_hq = sem("f_hq")
        f_hqT = sem("f_hqT")
        a_xn = sem("a_xn")
        a_xnT = sem("a_xnT")
        a_qk = sem("a_qk")
        a_v = sem("a_v")
        a_gate = sem("a_gate")
        a_max = sem("a_max")
        a_exp = sem("a_exp")
        a_norm = sem("a_norm")
        a_ptA = sem("a_ptA")
        a_ptD = sem("a_ptD")
        a_oT = sem("a_oT")
        x_xn = sem("x_xn")
        x_xnT = sem("x_xnT")
        x_ctx = sem("x_ctx")
        x_q = sem("x_q")
        x_k = sem("x_k")
        x_v = sem("x_v")
        x_max = sem("x_max")
        x_exp = sem("x_exp")
        x_norm = sem("x_norm")
        x_ptA = sem("x_ptA")
        x_ptD = sem("x_ptD")
        x_oT = sem("x_oT")
        m_xs = sem("m_xs")
        m_xT = sem("m_xT")
        m_lg = sem("m_lg")
        m_oh = sem("m_oh")
        m_ohT = sem("m_ohT")
        m_xmT = sem("m_xmT")
        m_hT = sem("m_hT")
        m_out = sem("m_out")
        stored = sem("stored")

        uses = []
        for s in range(NCH + 1):
            if s < NCH:
                uses += [("xz", s, m) for m in range(5)] + [("xd", s, 0)]
                uses += [("xz", s, m) for m in range(5, 8)] + [("dt", s, m) for m in range(4)]
                uses += [("o1", s, j) for j in range(4)] + [("xt", s, k) for k in range(KD)]
                uses += [(what, s, m) for what in ("inp", "gate", "pp") for m in range(KD)]
            if s:
                uses += [("o2", s - 1, j) for j in range(4)]
        use_at = {key: n for n, key in enumerate(uses)}

        def before_loop(key, s):
            what, c, _ = key
            return c < s - (what == "o2") or (c == s and what in ("xz", "xd", "dt"))

        def bank_of(*key):
            return gbank[use_at[key] % 2]

        def wait_full(eng, *key):
            n = use_at[key]
            eng.wait_ge(g_full[n % 2], n // 2 + 1)

        def wait_free(eng, *key):
            n = use_at[key]
            if n >= 2:
                eng.wait_ge(g_free[n % 2], n // 2)

        def fills(ins, *key):
            ins.then_inc(g_full[use_at[key] % 2], 1)

        def frees(ins, *key):
            ins.then_inc(g_free[use_at[key] % 2], 1)

        def btc(ap):
            return ap.rearrange("p (b t) -> p b t", b=B)

        def in_chunk(ap, s):
            return ap.rearrange("p (b c t) -> p c b t", b=B, c=NCH)[:, s]

        def lncount(kind, s):
            order = []
            for q in range(NCH + 1):
                order += [("a", q)] * (q < NCH) + [("b", q - 1)] * (q > 0)
            return order.index((kind, s))

        plan_f = Plan(b_full, b_free, [0] * 7 + [1],
                      [use for h in range(2) for use in
                       ((("xt", h), 4), (("g", h, 0), 0), (("g", h, 1), 1), (("u", h, 0), 2), (("u", h, 1), 3))]
                      + [use for h in range(2) for use in ((("ht", h), 5), (("dn", h), 6 + h))], B)
        uses_a = [("xt", 6), ("q", 0), ("k", 1), ("v", 2), ("ge", 3)]
        heads = lambda p: (2 * p, 2 * p + 1)
        uses_a += [(("s", n), n % 4) for p in (0, 1) for n in heads(p)]
        for p in range(NP):
            uses_a += [(("t", n), 4 + n % 2) for n in heads(p)]
            if p + 2 < NP:
                uses_a += [(("s", n), n % 4) for n in heads(p + 2)]
            if p % 4 == 0:
                uses_a += [(("o", p // 4), 6 + p // 4)]
        uses_a += [("out", 0)]
        plan_a = Plan(b_full, b_free, plan_f.end, uses_a, B)
        uses_x = [("xt", 6)] + [(("k", m), m) for m in range(4)] + [(("v", m), 4 + m) for m in range(4)]
        uses_x += [(("q", m), m) for m in range(4)]
        uses_x += [(("s", n), n % 4) for p in (0, 1) for n in heads(p)]
        for p in range(NP):
            uses_x += [(("t", n), 4 + n % 2) for n in heads(p)]
            if p + 2 < NP:
                uses_x += [(("s", n), n % 4) for n in heads(p + 2)]
            uses_x += [(("o", p), 6 + p % 2)]
        uses_x += [("out", 0)]
        plan_x = Plan(b_full, b_free, plan_a.end, uses_x, B)
        uses_m = [("xt", 0), ("lg", 1), ("oh", 2)] + [(("xm", e), 3 + e) for e in range(NE)]
        uses_m += [(("h", m), m % 3) for m in range(NF // 2)] + [("out", 7)]
        plan_m = Plan(b_full, b_free, plan_x.end, uses_m, B)

        LN_BASE = {"f": (0, 1), "a": (B, 2), "x": (3 * B, 2), "m": (5 * B, 2)}

        def ln_at(phase, n, i):
            base, per = LN_BASE[phase]
            return base + i * per + n + 1

        block = ctx.enter_context(nc.Block())

        @block.sync
        def _(sp):
            sp.sem_inc(stored, 16)
            for b in range(8):
                sp.sem_inc(b_free[b], 1)
            for dst, src in ((w_in[:, :, :], dr["w_in"]), (w_xp[:, :, :], dr["w_xp"]), (w_dt[:, :], dr["w_dt"]),
                             (cols[:, :], dr["cols"]), (ident[:, :], dr["ident"])):
                sp.dma_start(dst, src).then_inc(in_w, 16)
            sp.dma_start(xTc[:, 0], dr["xT"][:, 0]).then_inc(in_xT[0], 16)
            for dst, src in ((w_o0[:, :, :], dr["w_o0"]), (w_ch[:, :, :, :], dr["w_ch"]),
                             (causal_f[:, :], dr["causal"]), (headm[:, :], dr["headm"]),
                             (rows[:, :, :].rearrange("p a b -> p (a b)"), dr["rows"].broadcast_to([P, len(ROWS) * D]))):
                sp.dma_start(dst, src).then_inc(in_w2, 16)
            sp.dma_start(ctxT[:, :, :], dr["ctxT"]).then_inc(in_ctx, 16)
            sp.dma_start(xtk[:, 0], dr["x_tok"][0]).then_inc(in_xtk[0], 16)
            for s in range(NCH + 1):
                if s < NCH:
                    if s + 1 < NCH:
                        if s:
                            sp.wait_ge(zs_ready, s)
                            sp.wait_ge(x1_ready, s)
                        sp.dma_start(xTc[:, (s + 1) % 2], dr["xT"][:, s + 1]).then_inc(in_xT[(s + 1) % 2], 16)
                        sp.dma_start(xtk[:, (s + 1) % 2], dr["x_tok"][s + 1]).then_inc(in_xtk[(s + 1) % 2], 16)
                    sp.wait_ge(xd_ready, s + 1)
                    sp.dma_start(dr["bcd"][s], xd[DTR:96, :]).then_inc(bc_stored, 16)
                    sp.wait_ge(bc_stored, 16 * (s + 1))
                    src = dr["bcd"][s].rearrange("(a n) t -> n a t", a=2)
                    with sp.Fori(0, NS // 2) as i:
                        for u in range(2):
                            sp.wait_ge(hc_ready, 4 * (NS * s + 2 * i + u) + 1)
                            sp.dma_start(bc[:, u], src[bass.ds(2 * i + u, 1)].broadcast_to([P, 2, CC]))\
                              .then_inc(bc_loaded[u], 16)
                if s:
                    sp.wait_ge(x2_ready, s)
                    c = s - 1
                    for j in range(4):
                        for b2 in range(2):
                            sp.dma_start(x_tok[(c % 2) * TC:(c % 2 + 1) * TC, (2 * j + b2) * 2 + c // 2, :],
                                         x2c[b2 * TC:(b2 + 1) * TC, c % 2, j, :]).then_inc(x2_moved[c % 2], 16)
            for j in range(2):
                sp.wait_ge(x2_moved[j], 16 * 8 * NCH // 2)
            sp.wait_ge(front_done, 1)
            for a, name in enumerate(("w_gate", "w_up", "w_down")):
                sp.dma_start(w_raw[:, a, :], dr[name].rearrange("p k n -> p (k n)")).then_inc(in_b1, 16)
            sp.dma_start(prio[:, :, :], dr["prio"]).then_inc(in_b1, 16)
            for dst, name in ((w_qk, "w_qk"), (w_v, "w_v"), (w_o1, "w_o1"), (w_xq, "w_xq"), (w_xkv, "w_xkv"), (w_o2, "w_o2")):
                sp.dma_start(dst[:, :, :], dr[name]).then_inc(in_b2, 16)
            sp.dma_start(w_ent[:, :], dr["w_ent"]).then_inc(in_b2, 16)
            sp.dma_start(w_o3[:, :, :], dr["w_o3"]).then_inc(in_b3, 16)
            sp.dma_start(w_r[:, :, :], dr["w_r"]).then_inc(in_b3, 16)
            sp.wait_ge(pool_set, 1)
            sp.dma_start(b_1[0:NE, :], dr["b_1"]).then_inc(in_b3, 16)
            sp.wait_ge(w_ready, 1)
            sp.dma_start(w_1[:, :, :], dr["w_1"]).then_inc(in_b3, 16)
            ctx_b = dr["ctxT"].rearrange("p k (b c) -> p b k c", b=B)
            cT = x_b["cT"]
            sp.wait_ge(x_xn, 1)
            sp.dma_start(cT[:, :, :], ctx_b[:, 0]).then_inc(x_ctx, 16)
            with sp.Fori(0, B - 1) as i:
                plan_x.wait_full(sp, ("v", 3), i)
                sp.dma_start(cT[:, :, :], ctx_b[:, bass.ds(i + 1, 1)].rearrange("p o k c -> p (o k) c")).then_inc(x_ctx, 16)
            o_rows = dr["out"].rearrange("b (h p) d -> b p h d", h=2)
            with sp.Fori(0, B) as i:
                sp.wait_ge(m_out, i + 1)
                sp.dma_start(o_rows[bass.ds(i, 1)].rearrange("o p h d -> (o p) h d"), m_b["o"][:, :, :]).then_inc(stored, 16)
            sp.wait_ge(stored, 16 * (B + 1))

        @block.scalar
        def _(act):
            own = Own(act, act_own)
            act.sem_inc(tanh_done, 1)
            act.wait_ge(in_w, 16 * 5)
            a0, a1 = COLS["A_log"]
            act.activation(a_coef[:, :], cols[:, a0:a1], ACT.Exp).then_inc(setup_act, 1)
            for s in range(NCH + 1):
                if s < NCH:
                    if s:
                        act.wait_ge(y_ready, s)
                    for m in range(8):
                        wait_full(act, "xz", s, m)
                        if m < 4:
                            ins = act.activation(xp[:, m, :], bank_of("xz", s, m)[:, :], ACT.Copy)
                        else:
                            ins = act.activation(zs[:, m - 4, :], bank_of("xz", s, m)[:, :], ACT.Silu)
                        frees(ins, "xz", s, m)
                        if m == 4:
                            act.wait_ge(g_free[use_at["xz", s, 3] % 2], use_at["xz", s, 3] // 2 + 1)
                            act.sem_inc(xp_ready, 1)
                    for m in range(4):
                        wait_full(act, "dt", s, m)
                        own.did(act.activation(ee[:, m, :], bank_of("dt", s, m)[:, :], ACT.Exp, bias=col("b_dt", m)))
                        own.wait()
                        act.sem_inc(g_free[use_at["dt", s, m] % 2], 1)
                        act.sem_inc(e_ready, 1)
                    act.sem_inc(zs_ready, 1)
                    act.wait_ge(ec_ready, s + 1)
                    act.activation(lnu[:, :, :], ee[:, :, :], ACT.Ln, bias=1.0).then_inc(lnu_ready, 1)
                    act.wait_ge(dt_ready, s + 1)
                if s:
                    act.wait_ge(p_ready, s)

                def decay_of(j, u):
                    act.wait_ge(scans, 64 * s + j + 1)
                    act.activation(abar[:, u % 2, :, 1:], btc(ee[:, u % 4, :]), ACT.Identity,
                                   scale=a_coef[:, bass.ds(j, 1)], bias=1.0).then_inc(abar_ready, 1)

                def steps(i, last):
                    for u in range(8):
                        j = 8 * i + u
                        if s < NCH:
                            if not (last and u == 7):
                                decay_of(j + 1, u + 1)
                            act.wait_ge(scans, 64 * s + j + 3)
                            act.activation(hstate[:, bass.ds(j, 1), :], hh[:, u % 2, :, TC:TC + 1].rearrange("p b o -> p o b"),
                                           ACT.Copy).then_inc(h_saved, 1)
                        if s:
                            tt = 64 * (s - 1) + j
                            act.wait_ge(chain_mm, tt + 1)
                            act.wait_ge(st_copied, tt + 1)
                            act.activation(s_cur[:, u % 2, :], cbank[u % 2][:, 0:16], ACT.Tanh,
                                           scale=1.0 / GSC).then_inc(tanh_done, 1)

                act.preload_act_table_set("sigmoid_and_others")
                if s < NCH:
                    decay_of(0, 0)
                with act.Fori(0, NS // 2 - 1) as i:
                    steps(i, False)
                steps(NS // 2 - 1, True)
                if s < NCH:
                    act.wait_ge(ln_u, lncount("a", s) + 1)
                    own.did(act.activation(l1[:, :], lu[:, :], ACT.Ln))
                    own.wait()
                    act.activation(lr[:, :], l1[:, :], ACT.Exp, scale=-0.5).then_inc(ln_r, 1)
                    for m in range(KD):
                        wait_full(act, "inp", s, m)
                        own.did(act.activation(inp[:, m, :], bank_of("inp", s, m)[:, :], ACT.Identity, bias=col("bi", m)))
                        own.wait()
                        act.sem_inc(g_free[use_at["inp", s, m] % 2], 1)
                        act.sem_inc(inp_ready, 1)
                    for m in range(KD):
                        wait_full(act, "gate", s, m)
                        own.did(act.activation(gate[:, m, :], bank_of("gate", s, m)[:, :], ACT.Sigmoid, bias=col("bg", m)))
                        own.wait()
                        act.sem_inc(g_free[use_at["gate", s, m] % 2], 1)
                        act.sem_inc(gate_ready, 1)
                    for m in range(KD):
                        wait_full(act, "pp", s, m)
                        own.did(act.activation(pf[:, :, m * B:(m + 1) * B], btc(bank_of("pp", s, m)[:, :]).rearrange("p b t -> p t b"),
                                               ACT.Copy, scale=GSC))
                        own.wait()
                        act.sem_inc(g_free[use_at["pp", s, m] % 2], 1)
                        act.sem_inc(pf_ready, 1)
                if s:
                    act.wait_ge(ln_u, lncount("b", s - 1) + 1)
                    own.did(act.activation(l1[:, :], lu[:, :], ACT.Ln))
                    own.wait()
                    act.activation(lr[:, :], l1[:, :], ACT.Exp, scale=-0.5).then_inc(ln_r, 1)

            act.wait_ge(front_done, 1)
            act.activation(tg[:, :], col("gate"), ACT.Tanh).then_inc(act_set, 1)

            def inverse_root(phase, n, i):
                act.wait_ge(b_lnu, ln_at(phase, n, i))
                own.did(act.activation(l2b[:, :], lub[:, :], ACT.Ln))
                own.wait()
                act.activation(lrb[:, :], l2b[:, :], ACT.Exp, scale=-0.5).then_inc(b_lnr, 1)

            pl, w = plan_f, f_b
            with act.Fori(0, B) as i:
                own.enter(i, 1)
                for h in range(2):
                    pl.wait_full(act, ("xt", h), i)
                    act.activation(w["xqT"][:, h].rearrange("p k t -> p (k t)"), banks[4][:, 0:P].bitcast(BF16), ACT.Copy)\
                        .then_inc(f_xqT, 1)
                    act.wait_ge(f_xqT, 2 * i + h + 1)
                    act.sem_inc(b_free[4], 1)
                    for q in range(2):
                        pl.wait_full(act, ("g", h, q), i)
                        pl.frees(act.activation(w["sg"][:, h, q * 512:(q + 1) * 512], banks[q][:, :], ACT.Silu,
                                                scale=qv[:, 4, h:h + 1]), ("g", h, q))
                for h in range(2):
                    pl.wait_full(act, ("ht", h), i)
                    act.activation(w["hqT"][:, h].rearrange("p k t -> p (k t)"), banks[5][:, :].bitcast(BF16), ACT.Copy)\
                        .then_inc(f_hqT, 1)
                    act.wait_ge(f_hqT, 2 * i + h + 1)
                    act.sem_inc(b_free[5], 1)
                inverse_root("f", 0, i)
                own.leave(B)

            act.preload_act_table_set("natural_log_exp_and_others")
            pl, w = plan_a, a_b

            def attention(i, pl, w, widths, s_max, s_exp, s_norm, s_pt, copy_o):
                def exps(p):
                    for n in heads(p):
                        act.wait_ge(s_max, NH * i + n + 1)
                        if p >= 2:
                            pl.wait_full(act, ("t", n - 4), i)
                        for h in range(2):
                            a, b = widths[h]
                            own.did(act.activation(w["e"][:, n % 4, a:b], banks[n % 4][:, a:b], ACT.Exp,
                                                   bias=w["nm"][:, n, h:h + 1], accum_out=w["sm"][:, n, h:h + 1]))
                        own.wait()
                        act.sem_inc(b_free[n % 4], 1)
                        act.sem_inc(s_exp, 1)

                exps(0)
                for p in range(NP):
                    if p + 1 < NP:
                        exps(p + 1)
                    n = 2 * p
                    pl.wait_full(act, ("t", n), i)
                    slot = w["pt"].shape[1]
                    own.did(act.activation(w["pt"][:, n % slot, 0:widths[1][1]], banks[4][:, 0:widths[1][1]], ACT.Copy))
                    own.wait()
                    act.sem_inc(b_free[4], 1)
                    act.sem_inc(s_pt, 1)
                    copy_o(p)

            with act.Fori(0, B) as i:
                own.enter(i, 64)
                inverse_root("a", 0, i)
                pl.wait_full(act, "xt", i)
                for k in range(KD):
                    own.did(act.activation(w["xnT"][:, k, :], banks[6][:, k * S:(k + 1) * S], ACT.Identity,
                                           scale=col("ln_g", k), bias=col("ln_b", k)))
                own.wait()
                act.sem_inc(b_free[6], 1)
                act.sem_inc(a_xnT, 1)
                pl.wait_full(act, "q", i)
                for m in range(KD):
                    own.did(act.activation(w["qT"][:, m, :], banks[0][:, m * S:(m + 1) * S], ACT.Identity, scale=SOFT,
                                           bias=bq_s[:, m:m + 1]))
                own.wait()
                act.sem_inc(b_free[0], 1)
                pl.wait_full(act, "k", i)
                for n in range(NH):
                    m = n // HG
                    own.did(act.activation(w["km"][:, n, :], banks[1][:, m * S:(m + 1) * S], ACT.Identity,
                                           scale=headm[:, n % HG:n % HG + 1], bias=bk_m[:, n:n + 1]))
                own.wait()
                act.sem_inc(b_free[1], 1)
                act.sem_inc(a_qk, 1)
                pl.wait_full(act, "ge", i)
                act.activation(w["gt"][:, 0, :], banks[3][:, 0:2], ACT.Exp, scale=-1.0, bias=nb_ent[:, :]).then_inc(b_free[3], 1)

                def copy_o(p):
                    if p % 4 == 3:
                        g = p // 4
                        pl.wait_full(act, ("o", g), i)
                        own.did(act.activation(w["oT"][:, g, :], banks[6 + g][:, 0:S], ACT.Copy))
                        own.wait()
                        act.sem_inc(b_free[6 + g], 1)
                        act.sem_inc(a_oT, 1)

                attention(i, pl, w, ((0, P), (P, 3 * P)), a_max, a_exp, a_norm, a_ptA, copy_o)
                inverse_root("a", 1, i)
                own.leave(B)

            pl, w = plan_x, x_b
            with act.Fori(0, B) as i:
                own.enter(i, 64)
                inverse_root("x", 0, i)
                pl.wait_full(act, "xt", i)
                for k in range(KD):
                    own.did(act.activation(w["xnT"][:, k, :], banks[6][:, k * S:(k + 1) * S], ACT.Identity,
                                           scale=col("gam", k), bias=col("bet", k)))
                own.wait()
                act.sem_inc(b_free[6], 1)
                act.sem_inc(x_xnT, 1)
                for m in range(4):
                    pl.wait_full(act, ("k", m), i)
                    for half in range(2):
                        r = slice(64 * half, 64 * half + 64)
                        own.did(act.activation(w["kz"][r, 4 * m + half:4 * m + half + 3:2, :],
                                               banks[m][r, :].rearrange("p (a c) -> p a c", a=2), ACT.Copy))
                    own.wait()
                    act.sem_inc(b_free[m], 1)
                act.sem_inc(x_k, 1)
                for m in range(4):
                    pl.wait_full(act, ("q", m), i)
                    own.did(act.activation(w["qT"][:, 2 * m:2 * m + 2, :].rearrange("p a c -> p (a c)"), banks[m][:, :],
                                           ACT.Copy, scale=0.125))
                    own.wait()
                    act.sem_inc(b_free[m], 1)
                act.sem_inc(x_q, 1)

                def copy_o(p):
                    pl.wait_full(act, ("o", p), i)
                    own.did(act.activation(w["oT"][:, p, :], banks[6 + p % 2][:, 0:S], ACT.Copy))
                    own.wait()
                    act.sem_inc(b_free[6 + p % 2], 1)
                    act.sem_inc(x_oT, 1)

                attention(i, pl, w, ((0, S), (S, 2 * S)), x_max, x_exp, x_norm, x_ptA, lambda p: copy_o(p - 1) if p else None)
                copy_o(NP - 1)
                inverse_root("x", 1, i)
                own.leave(B)

            pl, w = plan_m, m_b
            with act.Fori(0, B) as i:
                own.enter(i, 9)
                pl.wait_full(act, "xt", i)
                own.did(act.activation(w["xT"][:, :, :].rearrange("p k c -> p (k c)"), banks[0][:, :], ACT.Copy))
                own.wait()
                act.sem_inc(b_free[0], 1)
                act.sem_inc(m_xT, 1)
                for e in range(NE):
                    pl.wait_full(act, ("xm", e), i)
                    if e % 2 == 0:
                        own.did(act.activation(w["xmT"][:, e].rearrange("p k c -> p (k c)"), banks[3 + e][:, :], ACT.Copy))
                        own.wait()
                        act.sem_inc(b_free[3 + e], 1)
                        act.sem_inc(m_xmT, 1)
                for m in range(NF // 2):
                    pl.wait_full(act, ("h", m), i)
                    own.did(act.activation(w["hT"][:, 2 * m:2 * m + 2, :].rearrange("p a c -> p (a c)"), banks[m % 3][:, :], ACT.Gelu))
                    own.wait()
                    act.sem_inc(b_free[m % 3], 1)
                    act.sem_inc(m_hT, 1)
                inverse_root("m", 0, i)
                inverse_root("m", 1, i)
                own.leave(B)

        @block.vector
        def _(dve):
            own = Own(dve, dve_own)
            dve.sem_inc(scans, 2)
            dve.sem_inc(hc_ready, 5)

            def link(ins):
                own.did(ins)
                own.wait()

            dve.memset(abar[:, :, :, 0:1], 0.0).then_inc(setup_dve, 1)
            dve.memset(hstate[:, :, :], 0.0).then_inc(setup_dve, 1)
            dve.memset(s_cur[:, :, :], 0.0).then_inc(setup_dve, 1)
            dve.wait_ge(in_w, 16 * 5)
            dve.wait_ge(in_w2, 16 * 5)
            dve.wait_ge(setup_act, 1)
            link(dve.tensor_scalar(a_coef[:, :], a_coef[:, :], -1.0, None, ALU.mult))
            for d in range(ND):
                own.did(dve.tensor_scalar(d_diag[:, d, :], ident[:, :], col("Dskip", d), None, ALU.mult))
            own.did(dve.tensor_copy(identb[:, :], ident[:, :]))
            own.did(dve.tensor_copy(causal[:, :], causal_f[:, :]))
            own.did(dve.tensor_scalar(a_neg[:, :, :], a_t, -1.0, None, ALU.mult))
            link(dve.tensor_copy(a_parts[0][:, :, :], a_t))
            link(dve.tensor_tensor(ret[:, 0, :].rearrange("p (k n) -> p k n", k=2), a_t, a_parts[0][:, :, :], ALU.subtract))
            link(dve.tensor_copy(a_parts[1][:, :, :], ret[:, 0, :].rearrange("p (k n) -> p k n", k=2)))
            own.did(dve.tensor_tensor(a_parts[2][:, :, :], ret[:, 0, :].rearrange("p (k n) -> p k n", k=2),
                                      a_parts[1][:, :, :], ALU.subtract))
            own.wait()
            dve.sem_inc(setup_dve, 1)
            dve.wait_ge(in_ctx, 16)
            link(dve.tensor_tensor(kv[:, :, :], ctxT[:, :, :], ctxT[:, :, :], ALU.mult))
            for k in range(KD):
                for b in range(B):
                    own.did(dve.tensor_tensor_scan(ctxT[:, k, b * S:(b + 1) * S], col("decay", k).to_broadcast([P, S]),
                                                   kv[:, k, b * S:(b + 1) * S], 0.0, ALU.mult, ALU.add))
            own.wait()

            def norm_stats(n_ln, eps, tiles):
                for j in tiles:
                    own.did(dve.bn_stats(st6[:, j, :], res[:, j, :]))
                own.wait()
                for j in tiles:
                    own.did(dve.bn_aggr(mv[:, j, :], st6[:, j, :]))
                own.wait()
                dve.tensor_scalar(lu[:, :], mv[:, :, 1], eps, None, ALU.add).then_inc(ln_u, 1)
                dve.wait_ge(ln_u, n_ln + 1)
                dve.wait_ge(ln_r, n_ln + 1)
                link(dve.tensor_tensor(l1[:, :], lr[:, :], lr[:, :], ALU.mult))
                link(dve.scalar_tensor_tensor(l2[:, :], l1[:, :], -0.5, lu[:, :], ALU.mult, ALU.mult))
                link(dve.scalar_tensor_tensor(l1[:, :], l2[:, :], 1.5, lr[:, :], ALU.add, ALU.mult))

            for s in range(NCH + 1):
                if s < NCH:
                    wait_full(dve, "xd", s, 0)
                    if s:
                        dve.wait_ge(bc_stored, 16 * s)
                    own.did(dve.tensor_copy(xd[:, :], bank_of("xd", s, 0)[0:96, :]))
                    own.wait()
                    dve.sem_inc(g_free[use_at["xd", s, 0] % 2], 1)
                    dve.sem_inc(xd_ready, 1)
                    dve.wait_ge(e_ready, 4 * (s + 1))
                    own.did(dve.tensor_scalar(ee[:, :, :], ee[:, :, :], 2.0 ** -11, 1.0, ALU.max, ALU.min))
                    own.wait()
                    dve.sem_inc(ec_ready, 1)
                    link(dve.tensor_scalar(um[:, :, :], ee[:, :, :], 1.0, 1.0, ALU.add, ALU.subtract))
                    link(dve.reciprocal(um[:, :, :], um[:, :, :]))
                    dve.wait_ge(lnu_ready, s + 1)
                    link(dve.tensor_tensor(um[:, :, :], um[:, :, :], ee[:, :, :], ALU.mult))
                    link(dve.tensor_tensor(ee[:, :, :], um[:, :, :], lnu[:, :, :], ALU.mult))
                    link(dve.tensor_scalar(ee[:, :, :], ee[:, :, :], 0.001, 0.1, ALU.max, ALU.min))
                    own.did(dve.tensor_tensor(um[:, :, :], ee[:, :, :], xp[:, :, :], ALU.mult))
                    own.wait()
                    dve.sem_inc(dt_ready, 1)

                def drive(u):
                    own.did(dve.tensor_tensor(dbx[:, u % 2, :, 1:], btc(um[:, u % 4, :]), btc(bc[:, u // 4 % 2, 0, :]), ALU.mult))

                def steps(i, last):
                    for u in range(8):
                        j = 8 * i + u
                        if s:
                            dve.wait_ge(tanh_done, 64 * (s - 1) + j + 1)
                            g = gsc[:, bass.ds(j, 1), :].rearrange("p o c -> p (o c)")
                            own.did(dve.tensor_tensor(gsf[:, :], g, s_cur[:, (u + 1) % 2, :], ALU.mult))
                            own.did(dve.tensor_tensor(gs2[:, 0, :], g, s_cur[:, (u + 1) % 2, :], ALU.mult))
                            own.wait()
                            dve.tensor_tensor(gs2[:, 1, :], gsf[:, :], gs2[:, 0, :], ALU.subtract).then_inc(gs_ready, 1)
                        if s < NCH:
                            jj = 64 * s + j
                            dve.wait_ge(abar_ready, jj + 1)
                            dve.wait_ge(h_in, jj + 1)
                            dve.wait_ge(h_saved, jj + 1)
                            own.wait()
                            dve.tensor_tensor_scan(hh[:, u % 2].rearrange("p b t -> p (b t)"),
                                                   abar[:, u % 2].rearrange("p b t -> p (b t)"),
                                                   dbx[:, u % 2].rearrange("p b t -> p (b t)"), 0.0,
                                                   ALU.mult, ALU.add).then_inc(scans, 1)
                        if s < NCH:
                            if not (last and u == 7):
                                if u % 4 == 3:
                                    dve.wait_ge(bc_loaded[(u // 4 + 1) % 2], 16 * ((NS // 2) * s + i + 1 + (u == 7)))
                                drive(u + 1)
                            dve.wait_ge(scans, jj + 3)
                            dve.wait_ge(hc_used, jj + 1)
                            dve.tensor_tensor(btc(hc[:, u % 2, :]), hh[:, u % 2, :, 1:], btc(bc[:, u // 4, 1, :]),
                                              ALU.mult).then_inc(hc_ready, 1)

                if s < NCH:
                    dve.wait_ge(bc_loaded[0], 16 * ((NS // 2) * s + 1))
                    drive(0)
                with dve.Fori(0, NS // 2 - 1) as i:
                    own.enter(i, 8 * (2 * (s > 0) + (s < NCH)))
                    steps(i, False)
                    own.leave(NS // 2 - 1)
                steps(NS // 2 - 1, True)
                if s < NCH:
                    dve.wait_ge(hc_used, 64 * (s + 1) + 2)
                    for d in range(ND):
                        own.did(dve.tensor_tensor(zs[:, d, :], ybank[d][:, :], zs[:, d, :], ALU.mult))
                    own.wait()
                    dve.sem_inc(y_ready, 1)
                    dve.wait_ge(in_xtk[s % 2], 16 * (s // 2 + 1))
                    for j in range(4):
                        wait_full(dve, "o1", s, j)
                        own.did(dve.tensor_tensor(res[:, j, :], bank_of("o1", s, j)[:, 0:D], xtk[:, s % 2, j, :], ALU.add))
                        own.wait()
                        dve.sem_inc(g_free[use_at["o1", s, j] % 2], 1)
                    norm_stats(lncount("a", s), 1e-5, range(4))
                    for j in range(4):
                        own.did(dve.tensor_scalar(x1[:, s % 2, j, :], res[:, j, :], mv[:, j, 0:1], l1[:, j:j + 1],
                                                  ALU.subtract, ALU.mult))
                    own.wait()
                    dve.sem_inc(x1_ready, 1)
                    for k in range(KD):
                        wait_full(dve, "xt", s, k)
                        own.did(dve.tensor_tensor(btc(ret[:, k, :]), btc(bank_of("xt", s, k)[:, :]), in_chunk(ctxT[:, k, :], s), ALU.mult))
                        own.wait()
                        dve.sem_inc(g_free[use_at["xt", s, k] % 2], 1)
                        dve.sem_inc(ret_ready, 1)
                    for m in range(KD):
                        dve.wait_ge(gate_ready, KD * s + m + 1)
                        own.did(dve.scalar_tensor_tensor(ret[:, m, :], gate[:, m, :], 1.0, inp[:, m, :], ALU.subtract, ALU.mult))
                        own.did(dve.tensor_scalar(gsc[:, :, m * B:(m + 1) * B], btc(gate[:, m, :]).rearrange("p b t -> p t b"),
                                                  GSC, None, ALU.mult))
                        own.wait()
                        dve.sem_inc(om_ready, 1)
                    dve.wait_ge(pf_ready, KD * (s + 1))
                    link(dve.tensor_copy(pparts[:, :, 0, :], pf[:, :, :]))
                    link(dve.tensor_tensor(pf[:, :, :], pf[:, :, :], pparts[:, :, 0, :], ALU.subtract))
                    link(dve.tensor_copy(pparts[:, :, 1, :], pf[:, :, :]))
                    own.did(dve.tensor_tensor(pparts[:, :, 2, :], pf[:, :, :], pparts[:, :, 1, :], ALU.subtract))
                    own.wait()
                    dve.sem_inc(p_ready, 1)
                if s:
                    c = s - 1
                    for j in range(4):
                        wait_full(dve, "o2", c, j)
                        own.did(dve.tensor_tensor(res[:, j, :], bank_of("o2", c, j)[:, 0:D], x1[:, c % 2, j, :], ALU.add))
                        own.wait()
                        dve.sem_inc(g_free[use_at["o2", c, j] % 2], 1)
                    for j in range(4):
                        own.did(dve.tensor_tensor(res[:, j, :], res[:, j, :], row("bo"), ALU.add))
                    own.wait()
                    norm_stats(lncount("b", c), 1e-5, range(4))
                    if c >= 2:
                        dve.wait_ge(x2_moved[c % 2], 16 * 8 * (c // 2))
                    for j in range(4):
                        own.did(dve.tensor_scalar(x2c[:, c % 2, j, :], res[:, j, :], mv[:, j, 0:1], l1[:, j:j + 1],
                                                  ALU.subtract, ALU.mult))
                    own.wait()
                    dve.sem_inc(x2_ready, 1)

            for j in range(2):
                dve.wait_ge(x2_moved[j], 16 * 8 * NCH // 2)
            dve.wait_ge(st_copied, TC * NCH + 2)
            dve.sem_inc(front_done, 1)
            own.did(dve.memset(ones[:, :], 1.0))
            for n in range(NH):
                own.did(dve.tensor_scalar(bk_m[:, n:n + 1], headm[:, n % HG:n % HG + 1], col("bk", n // HG), None, ALU.mult))
            a0 = COLS["bq"][0]
            own.did(dve.tensor_scalar(bq_s[:, :], cols[:, a0:a0 + KD], SOFT, None, ALU.mult))
            own.did(dve.tensor_scalar(nb_ent[:, :], col("b_ent"), -1.0, None, ALU.mult))
            own.wait()
            dve.sem_inc(dve_set, 1)
            dve.wait_ge(in_b1, 16 * 4)
            for a in range(3):
                own.did(dve.tensor_reduce(wsum[:, a:a + 1], w_raw[:, a, :], AX.X, ALU.add, apply_absolute_value=True))
            own.wait()
            dve.sem_inc(w_summed, 1)
            dve.wait_ge(b_full[7], 1)
            own.did(dve.tensor_scalar(wmean[:, :], banks[7][:, 0:3], 1.0 / (D * F), TINY, ALU.mult, ALU.max))
            own.wait()
            dve.sem_inc(b_free[7], 1)
            link(dve.reciprocal(wrec[:, :], wmean[:, :]))
            for a, q in enumerate((wg_q, wu_q, wd_q)):
                qf = q[:, :, :].rearrange("p k n -> p (k n)")
                link(dve.tensor_scalar(w_raw[:, a, :], w_raw[:, a, :], wrec[:, a:a + 1], MAGIC, ALU.mult, ALU.add))
                link(dve.tensor_scalar(w_raw[:, a, :], w_raw[:, a, :], MAGIC, 1.0, ALU.subtract, ALU.min))
                link(dve.tensor_scalar(qf, w_raw[:, a, :], -1.0, None, ALU.max))
            dve.sem_inc(w_ready, 1)

            def tiles(i):
                return x_tok[:, bass.ds(2 * i, 2), :]

            def tile(i, h):
                return x_tok[:, bass.ds(2 * i + h, 1), :].rearrange("p o d -> p (o d)")

            def root(phase, n, i, src, eps):
                for h in range(2):
                    own.did(dve.bn_stats(stats6[:, h, :], src[h]))
                own.wait()
                dve.sem_inc(stats_seen, 1)
                for h in range(2):
                    own.did(dve.bn_aggr(mvb[:, h, :], stats6[:, h, :]))
                own.wait()
                dve.tensor_scalar(lub[:, :], mvb[:, :, 1], eps, None, ALU.add).then_inc(b_lnu, 1)
                dve.wait_ge(b_lnu, ln_at(phase, n, i))
                dve.wait_ge(b_lnr, ln_at(phase, n, i))
                link(dve.tensor_tensor(l1b[:, :], lrb[:, :], lrb[:, :], ALU.mult))
                link(dve.scalar_tensor_tensor(l2b[:, :], l1b[:, :], -0.5, lub[:, :], ALU.mult, ALU.mult))
                link(dve.scalar_tensor_tensor(l1b[:, :], l2b[:, :], 1.5, lrb[:, :], ALU.add, ALU.mult))

            def normalise(dst, src):
                for h in range(2):
                    own.did(dve.tensor_scalar(dst[h], src[h], mvb[:, h, 0:1], l1b[:, h:h + 1], ALU.subtract, ALU.mult))
                own.wait()

            def quantise(src, amax, tmp, dst, h):
                link(dve.tensor_scalar(tmp, src, amax, MAGIC, ALU.mult, ALU.add))
                own.did(dve.tensor_scalar(dst, tmp, MAGIC, None, ALU.subtract))

            pl, w = plan_f, f_b
            with dve.Fori(0, B) as i:
                own.enter(i, 39)
                link(dve.tensor_reduce(qv[:, 0, :], tiles(i), AX.X, ALU.max, apply_absolute_value=True))
                link(dve.tensor_scalar(qv[:, 1, :], qv[:, 0, :], TINY, None, ALU.max))
                link(dve.reciprocal(qv[:, 2, :], qv[:, 1, :]))
                own.did(dve.tensor_scalar(qv[:, 3, :], qv[:, 2, :], 127.0, None, ALU.mult))
                own.did(dve.tensor_scalar(qv[:, 4, :], qv[:, 1, :], 1.0 / 127.0, wmean[:, 0:1], ALU.mult, ALU.mult))
                link(dve.tensor_scalar(qv[:, 5, :], qv[:, 1, :], 1.0 / 127.0, wmean[:, 1:2], ALU.mult, ALU.mult))
                for h in range(2):
                    quantise(tile(i, h), qv[:, 3, h:h + 1], w["tmp"][:, h, 0:D], w["xq"][:, h, :], h)
                    own.wait()
                    dve.sem_inc(f_xq, 1)
                for h in range(2):
                    for q in range(2):
                        c = slice(q * 512, (q + 1) * 512)
                        pl.wait_full(dve, ("u", h, q), i)
                        pl.wait_freed(dve, ("g", h, q), i)
                        own.did(dve.scalar_tensor_tensor(w["hv"][:, h, c], banks[2 + q][:, :], qv[:, 5, h:h + 1],
                                                         w["sg"][:, h, c], ALU.mult, ALU.mult))
                        own.wait()
                        dve.sem_inc(b_free[2 + q], 1)
                    link(dve.tensor_reduce(qv[:, 6, h:h + 1], w["hv"][:, h, :], AX.X, ALU.max, apply_absolute_value=True))
                    link(dve.tensor_scalar(qv[:, 7, h:h + 1], qv[:, 6, h:h + 1], TINY, None, ALU.max))
                    link(dve.reciprocal(qv[:, 8, h:h + 1], qv[:, 7, h:h + 1]))
                    own.did(dve.tensor_scalar(qv[:, 9, h:h + 1], qv[:, 8, h:h + 1], 127.0, None, ALU.mult))
                    link(dve.tensor_scalar(qv[:, 10, h:h + 1], qv[:, 7, h:h + 1], 1.0 / 127.0, wmean[:, 2:3], ALU.mult, ALU.mult))
                    quantise(w["hv"][:, h, :], qv[:, 9, h:h + 1], w["tmp"][:, h, :], w["hq"][:, h, :], h)
                    own.wait()
                    dve.sem_inc(f_hq, 1)
                for h in range(2):
                    pl.wait_full(dve, ("dn", h), i)
                    own.did(dve.scalar_tensor_tensor(resb[:, h, :], banks[6 + h][:, 0:D], qv[:, 10, h:h + 1], tile(i, h),
                                                     ALU.mult, ALU.add))
                    own.wait()
                    dve.sem_inc(b_free[6 + h], 1)
                root("f", 0, i, [resb[:, h, :] for h in range(2)], 1e-5)
                normalise([tile(i, h) for h in range(2)], [resb[:, h, :] for h in range(2)])
                own.leave(B)

            def attention(i, pl, w, maxima, widths, s_max, s_exp, s_norm, s_pt):
                def top(p):
                    for n in heads(p):
                        pl.wait_full(dve, ("s", n), i)
                        maxima(n)
                        own.wait()
                        dve.sem_inc(s_max, 1)

                top(0)
                for p in range(NP):
                    if p + 1 < NP:
                        top(p + 1)
                    dve.wait_ge(s_exp, NH * i + 2 * p + 2)
                    n2 = slice(2 * p, 2 * p + 2)
                    link(dve.reciprocal(w["rr"][:, n2, :], w["sm"][:, n2, :]))
                    for n in heads(p):
                        for h in range(2):
                            a, b = widths[h]
                            own.did(dve.tensor_scalar(w["e"][:, n % 4, a:b], w["e"][:, n % 4, a:b], w["rr"][:, n, h:h + 1],
                                                      None, ALU.mult))
                        own.wait()
                        dve.sem_inc(s_norm, 1)
                    n = 2 * p + 1
                    pl.wait_full(dve, ("t", n), i)
                    slot = w["pt"].shape[1]
                    own.did(dve.tensor_copy(w["pt"][:, n % slot, 0:widths[1][1]], banks[5][:, 0:widths[1][1]]))
                    own.wait()
                    dve.sem_inc(b_free[5], 1)
                    dve.sem_inc(s_pt, 1)

            pl, w = plan_a, a_b
            link(dve.memset(w["vm"][:, :, :, :], 0.0))
            with dve.Fori(0, B) as i:
                own.enter(i, 109)
                root("a", 0, i, [tile(i, h) for h in range(2)], 1e-6)
                normalise([w["xn"][:, h, :] for h in range(2)], [tile(i, h) for h in range(2)])
                dve.sem_inc(a_xn, 1)
                pl.wait_freed(dve, "ge", i)
                gt = w["gt"]
                link(dve.tensor_scalar(gt[:, 1, :], gt[:, 0, :], 1.0, None, ALU.add))
                link(dve.reciprocal(gt[:, 2, :], gt[:, 1, :]))
                own.did(dve.tensor_scalar(gt[:, 3, :], gt[:, 2, :], 0.1, 2.0, ALU.max, ALU.min))
                pl.wait_full(dve, "v", i)
                vh = [w["vm"][:, h].rearrange("p g (j c) -> p g j c", c=P + 16)[:, :, :, 0:16] for h in range(2)]
                for h in range(2):
                    own.did(dve.tensor_tensor(vh[h], banks[2][:, h * D:(h + 1) * D].rearrange("p (g j c) -> p g j c", g=2, c=16),
                                              row("bv").rearrange("p (g j c) -> p g j c", g=2, c=16), ALU.add))
                own.wait()
                dve.sem_inc(b_free[2], 1)
                for h in range(2):
                    own.did(dve.tensor_scalar(vh[h], vh[h], gt[:, 3, h:h + 1], None, ALU.mult))
                own.wait()
                dve.sem_inc(a_v, 1)

                def maxima(n):
                    for h, (a, b) in enumerate(((0, P), (P, 3 * P))):
                        own.did(dve.tensor_reduce(w["nm"][:, n, h:h + 1], banks[n % 4][:, a:b], AX.X, ALU.max, negate=True))

                attention(i, pl, w, maxima, ((0, P), (P, 3 * P)), a_max, a_exp, a_norm, a_ptD)
                pl.wait_full(dve, "out", i)
                for h in range(2):
                    own.did(dve.tensor_tensor(resb[:, h, :], banks[0][:, h * D:(h + 1) * D], row("b_out"), ALU.add))
                own.wait()
                dve.sem_inc(b_free[0], 1)
                for h in range(2):
                    own.did(dve.scalar_tensor_tensor(resb[:, h, :], resb[:, h, :], 0.1, tile(i, h), ALU.mult, ALU.add))
                own.wait()
                root("a", 1, i, [resb[:, h, :] for h in range(2)], 1e-5)
                normalise([tile(i, h) for h in range(2)], [resb[:, h, :] for h in range(2)])
                own.leave(B)

            pl, w = plan_x, x_b
            link(dve.memset(w["kz"][:, :, :], 0.0))
            with dve.Fori(0, B) as i:
                own.enter(i, 90)
                root("x", 0, i, [tile(i, h) for h in range(2)], 1e-5)
                normalise([w["xn"][:, h, :] for h in range(2)], [tile(i, h) for h in range(2)])
                dve.sem_inc(x_xn, 1)
                for m in range(4):
                    pl.wait_full(dve, ("v", m), i)
                    own.did(dve.tensor_copy(w["v"][:, m // 2, (m % 2) * 512:(m % 2 + 1) * 512], banks[4 + m][:, :]))
                    own.wait()
                    dve.sem_inc(b_free[4 + m], 1)
                dve.sem_inc(x_v, 1)

                def maxima(n):
                    own.did(dve.tensor_reduce(w["nm"][:, n, :], banks[n % 4][:, :].rearrange("p (h c) -> p h c", h=2),
                                              AX.X, ALU.max, negate=True))

                attention(i, pl, w, maxima, ((0, S), (S, 2 * S)), x_max, x_exp, x_norm, x_ptD)
                pl.wait_full(dve, "out", i)
                for h in range(2):
                    own.did(dve.tensor_tensor(resb[:, h, :], banks[0][:, h * D:(h + 1) * D], row("b_out2"), ALU.add))
                own.wait()
                dve.sem_inc(b_free[0], 1)
                for h in range(2):
                    own.did(dve.scalar_tensor_tensor(resb[:, h, :], resb[:, h, :], tg[:, :], tile(i, h), ALU.mult, ALU.add))
                own.wait()
                root("x", 1, i, [resb[:, h, :] for h in range(2)], 1e-5)
                normalise([tile(i, h) for h in range(2)], [resb[:, h, :] for h in range(2)])
                own.leave(B)

            pl, w = plan_m, m_b
            link(dve.memset(w["ohT"][:, :], 0.0))
            with dve.Fori(0, B) as i:
                own.enter(i, 49)
                for h in range(2):
                    own.did(dve.tensor_copy(w["xs"][:, h, :], tile(i, h)))
                own.wait()
                dve.sem_inc(m_xs, 1)
                pl.wait_full(dve, "lg", i)
                own.did(dve.tensor_copy(w["lg"][:, :, :].rearrange("p h e -> p (h e)"), banks[1][:, 0:2 * NE]))
                own.wait()
                dve.sem_inc(b_free[1], 1)
                mx, lg, oh = w["mx"], w["lg"], w["oh"]
                link(dve.tensor_reduce(mx[:, 0, :], lg[:, :, :], AX.X, ALU.max))
                for h in range(2):
                    own.did(dve.tensor_scalar(oh[:, h, :], lg[:, h, :], mx[:, 0, h:h + 1], None, ALU.is_ge))
                own.wait()
                link(dve.tensor_tensor(lg[:, :, :], oh[:, :, :], prio[:, :, :], ALU.mult))
                link(dve.tensor_reduce(mx[:, 1, :], lg[:, :, :], AX.X, ALU.max))
                for h in range(2):
                    own.did(dve.tensor_scalar(oh[:, h, :], lg[:, h, :], mx[:, 1, h:h + 1], None, ALU.is_ge))
                own.wait()
                for h in range(2):
                    for e in range(NE):
                        own.did(dve.tensor_scalar(w["xm"][:, h, e, :], w["xs"][:, h, :], oh[:, h, e:e + 1], None, ALU.mult))
                own.wait()
                dve.sem_inc(m_oh, 1)
                pl.wait_full(dve, "oh", i)
                own.did(dve.tensor_copy(w["ohT"][0:NE, :], banks[2][0:NE, 0:S]))
                own.wait()
                dve.sem_inc(b_free[2], 1)
                dve.sem_inc(m_ohT, 1)
                for e in (1, 3):
                    pl.wait_full(dve, ("xm", e), i)
                    own.did(dve.tensor_copy(w["xmT"][:, e].rearrange("p k c -> p (k c)"), banks[3 + e][:, :]))
                    own.wait()
                    dve.sem_inc(b_free[3 + e], 1)
                    dve.sem_inc(m_ohT, 1)
                pl.wait_full(dve, "out", i)
                for h in range(2):
                    own.did(dve.tensor_tensor(resb[:, h, :], banks[7][:, h * D:(h + 1) * D], row("bo_ffn"), ALU.add))
                own.wait()
                dve.sem_inc(b_free[7], 1)
                for h in range(2):
                    own.did(dve.tensor_tensor(resb[:, h, :], resb[:, h, :], w["xs"][:, h, :], ALU.add))
                own.wait()
                root("m", 0, i, [resb[:, h, :] for h in range(2)], 1e-12)
                y = [w["y"][:, h, :] for h in range(2)]
                normalise(y, [resb[:, h, :] for h in range(2)])
                for h in range(2):
                    own.did(dve.tensor_tensor(y[h], y[h], row("lng"), ALU.mult))
                own.wait()
                for h in range(2):
                    own.did(dve.tensor_tensor(y[h], y[h], row("lnb"), ALU.add))
                own.wait()
                for h in range(2):
                    own.did(dve.tensor_tensor(resb[:, h, :], y[h], w["xs"][:, h, :], ALU.add))
                own.wait()
                root("m", 1, i, [resb[:, h, :] for h in range(2)], 1e-5)
                dve.wait_ge(stored, 16 * (i + 1))
                normalise([w["o"][:, h, :] for h in range(2)], [resb[:, h, :] for h in range(2)])
                dve.sem_inc(m_out, 1)
                own.leave(B)

        @block.gpsimd
        def _(pool):
            pool.sem_inc(st_copied, 2)
            for s in range(NCH + 1):
                def carry_in(j, u):
                    pool.wait_ge(scans, 64 * s + j + 1)
                    pool.tensor_copy(dbx[:, u % 2, :, 0:1], hstate[:, bass.ds(j, 1), :].rearrange("p o b -> p b o")).then_inc(h_in, 1)

                def steps(i, last):
                    for u in range(8):
                        j = 8 * i + u
                        if s < NCH and not (last and u == 7):
                            carry_in(j + 1, u + 1)
                        if s:
                            pool.wait_ge(tanh_done, TC * (s - 1) + j + 2)
                            pool.tensor_copy(states[:, :, bass.ds(j, 1)].rearrange("p c o -> p (c o)"), s_cur[:, u % 2, :])\
                                .then_inc(st_copied, 1)

                if s > 1:
                    pool.wait_ge(x2_ready, s - 1)
                if s < NCH:
                    pool.wait_ge(setup_dve, 4)
                    pool.wait_ge(h_saved, 64 * s + 2)
                    carry_in(0, 0)
                with pool.Fori(0, NS // 2 - 1) as i:
                    steps(i, False)
                steps(NS // 2 - 1, True)
            pool.wait_ge(front_done, 1)
            pool.memset(b_1[:, :], 0.0).then_inc(pool_set, 1)

        @block.tensor
        def _(pe):
            def product(out, pairs, start=True, stop=True, skip=False):
                n = len(pairs)
                for q, (lhs, rhs) in enumerate(pairs):
                    ins = pe.matmul(out, lhs, rhs, start=start and q == 0, stop=stop and q == n - 1, skip_group_check=skip)
                return ins

            pe.sem_inc(hc_used, 2)
            pe.sem_inc(h_saved, 2)
            pe.wait_ge(in_w, 16 * 5)
            pe.wait_ge(in_w2, 16 * 5)
            for s in range(NCH + 1):
                if s < NCH:
                    pe.wait_ge(in_xT[s % 2], 16 * (s // 2 + 1))

                    def xz(m):
                        wait_free(pe, "xz", s, m)
                        fills(product(bank_of("xz", s, m)[:, :],
                                      [(w_in[:, k, m * P:(m + 1) * P], xTc[:, s % 2, k, :]) for k in range(KD)]), "xz", s, m)

                    for m in range(5):
                        xz(m)
                    wait_free(pe, "xd", s, 0)
                    pe.wait_ge(xp_ready, s + 1)
                    fills(product(bank_of("xd", s, 0)[0:96, :], [(w_xp[:, k, :], xp[:, k, :]) for k in range(ND)]), "xd", s, 0)
                    for m in range(5, 8):
                        xz(m)
                    pe.wait_ge(xd_ready, s + 1)
                    for m in range(4):
                        wait_free(pe, "dt", s, m)
                        fills(product(bank_of("dt", s, m)[:, :], [(w_dt[:, m * P:(m + 1) * P], xd[0:DTR, :])]), "dt", s, m)
                    pe.wait_ge(setup_dve, 4)
                    if s:
                        pe.wait_ge(y_ready, s)
                    for d in range(ND):
                        pe.matmul(ybank[d][:, :], d_diag[:, d, :], xp[:, d, :], start=True, stop=True)
                if s:
                    pe.wait_ge(p_ready, s)
                for j in range(2):
                    pe.wait_ge(g_free[j], sum(1 for key, n in use_at.items() if n % 2 == j and before_loop(key, s)))
                with pe.Fori(0, NS // 2) as i:
                    for u in range(8):
                        d = u % 4
                        j = 8 * i + u
                        if s:
                            cb = cbank[u % 2]
                            for q in range(3):
                                pe.matmul(cb[:, 0:16], identb[:, :], pparts[:, bass.ds(j, 1), q, :].rearrange("p o c -> p (o c)"),
                                          start=q == 0, stop=False, skip_group_check=True)
                            pe.matmul(gbank[0][:, :], identb[:, :], a_parts[0][:, :, :].rearrange("p k n -> p (k n)"),
                                      start=True, stop=True)
                            pe.wait_ge(gs_ready, 64 * (s - 1) + j + 1)
                            for m in range(KD):
                                for k in range(KD):
                                    for a, g in ((0, 0), (0, 1), (1, 0), (1, 1), (2, 0)):
                                        ins = pe.matmul(cb[:, m * B:(m + 1) * B], a_parts[a][:, k, m * P:(m + 1) * P],
                                                        gs2[:, g, k * B:(k + 1) * B], start=False,
                                                        stop=(k == KD - 1 and a == 2), skip_group_check=True)
                            ins.then_inc(chain_mm, 1)
                        if s < NCH:
                            jj = 64 * s + j
                            pe.wait_ge(hc_ready, jj + 6)
                            pe.matmul(ybank[d][:, :], ident[:, :], hc[:, u % 2, :], start=False, stop=True,
                                      skip_group_check=True).then_inc(hc_used, 1)
                if s < NCH:
                    pe.wait_ge(y_ready, s + 1)
                    for j in range(4):
                        wait_free(pe, "o1", s, j)
                        fills(product(bank_of("o1", s, j)[:, 0:D],
                                      [(zs[:, d, j * P:(j + 1) * P], w_o0[:, d, :]) for d in range(ND)]), "o1", s, j)
                    pe.wait_ge(x1_ready, s + 1)
                    for k in range(KD):
                        wait_free(pe, "xt", s, k)
                        for j in range(4):
                            ins = pe.transpose(bank_of("xt", s, k)[:, j * P:(j + 1) * P], x1[:, s % 2, j, k * P:(k + 1) * P], ident[:, :])
                        fills(ins, "xt", s, k)
                    pe.wait_ge(ret_ready, KD * (s + 1))
                    for m in range(KD):
                        wait_free(pe, "inp", s, m)
                        fills(product(bank_of("inp", s, m)[:, :],
                                      [(wi_t[:, k, m * P:(m + 1) * P], ret[:, k, :]) for k in range(KD)]), "inp", s, m)
                    pe.wait_ge(inp_ready, KD * (s + 1))
                    for m in range(KD):
                        wait_free(pe, "gate", s, m)
                        fills(product(bank_of("gate", s, m)[:, :],
                                      [(wg_t[:, k, m * P:(m + 1) * P], inp[:, k, :]) for k in range(KD)]), "gate", s, m)
                    pe.wait_ge(om_ready, KD * (s + 1))
                    for m in range(KD):
                        wait_free(pe, "pp", s, m)
                        fills(product(bank_of("pp", s, m)[:, :],
                                      [(a_neg[:, k, m * P:(m + 1) * P], ret[:, k, :]) for k in range(KD)]
                                      + [(bm_t[:, k, m * P:(m + 1) * P], inp[:, k, :]) for k in range(KD)]), "pp", s, m)
                if s:
                    c = s - 1
                    pe.wait_ge(st_copied, TC * s + 2)
                    for j in range(4):
                        wait_free(pe, "o2", c, j)
                        lhs = [states[:, k * B + 2 * j:k * B + 2 * j + 2, :].rearrange("p b t -> p (b t)") for k in range(KD)]
                        fills(product(bank_of("o2", c, j)[:, 0:D], [(lhs[k], wo_t[:, k, :]) for k in range(KD)]), "o2", c, j)

            pe.wait_ge(dve_set, 1)
            pe.wait_ge(w_summed, 1)
            product(banks[7][:, 0:3], [(ones[:, :], wsum[:, :])]).then_inc(b_full[7], 1)
            pe.wait_ge(w_ready, 1)
            pl, w = plan_f, f_b
            with pe.Fori(0, B) as i:
                for h in range(2):
                    pe.wait_ge(f_xq, 2 * i + h + 1)
                    pl.wait_free(pe, ("xt", h), i)
                    xt = banks[4][:, 0:P].bitcast(BF16)
                    for k in range(KD):
                        ins = pe.transpose(xt[:, k * P:(k + 1) * P], w["xq"][:, h, k * P:(k + 1) * P], identb[:, :])
                    pl.fills(ins, ("xt", h))
                    pe.wait_ge(f_xqT, 2 * i + h + 1)
                    for name, wq, b0 in (("g", wg_q, 0), ("u", wu_q, 2)):
                        for q in range(2):
                            pl.wait_free(pe, (name, h, q), i)
                            pl.fills(product(banks[b0 + q][:, :], [(w["xqT"][:, h, k, :], wq[:, k, q * 512:(q + 1) * 512])
                                                                   for k in range(KD)]), (name, h, q))
                for h in range(2):
                    pe.wait_ge(f_hq, 2 * i + h + 1)
                    pl.wait_free(pe, ("ht", h), i)
                    ht = banks[5][:, :].bitcast(BF16)
                    for m in range(NF):
                        ins = pe.transpose(ht[:, m * P:(m + 1) * P], w["hq"][:, h, m * P:(m + 1) * P], identb[:, :])
                    pl.fills(ins, ("ht", h))
                    pe.wait_ge(f_hqT, 2 * i + h + 1)
                    pl.wait_free(pe, ("dn", h), i)
                    pl.fills(product(banks[6 + h][:, 0:D], [(w["hqT"][:, h, m, :], wd_q[:, m, :]) for m in range(NF)]), ("dn", h))

            pe.wait_ge(in_b2, 16 * 7)
            pl, w = plan_a, a_b
            qk_w = w_qk

            def transposed(key, bank, i, src):
                pl.wait_free(pe, key, i)
                for k in range(KD):
                    for h in range(2):
                        ins = pe.transpose(bank[:, k * S + h * P:k * S + (h + 1) * P], src[:, h, k * P:(k + 1) * P], ident[:, :])
                pl.fills(ins, key)

            with pe.Fori(0, B) as i:
                pe.wait_ge(a_xn, i + 1)
                transposed("xt", banks[6], i, w["xn"])
                pe.wait_ge(a_xnT, i + 1)
                xnT, qT, km, vm = w["xnT"], w["qT"], w["km"], w["vm"]
                for j, key in enumerate(("q", "k")):
                    pl.wait_free(pe, key, i)
                    for m in range(KD):
                        c = j * D + m * P
                        ins = product(banks[j][:, m * S:(m + 1) * S], [(w_qk[:, k, c:c + P], xnT[:, k, :]) for k in range(KD)])
                    pl.fills(ins, key)
                pl.wait_free(pe, "v", i)
                for h in range(2):
                    ins = product(banks[2][:, h * D:(h + 1) * D], [(xnT[:, k, h * P:(h + 1) * P], w_v[:, k, :]) for k in range(KD)])
                pl.fills(ins, "v")
                pl.wait_free(pe, "ge", i)
                for h in range(2):
                    ins = product(banks[3][:, h:h + 1], [(xnT[:, k, h * P:(h + 1) * P], w_ent[:, k:k + 1]) for k in range(KD)])
                pl.fills(ins, "ge")
                pe.wait_ge(a_qk, i + 1)

                def scores(p):
                    for n in heads(p):
                        pl.wait_free(pe, ("s", n), i)
                        m, bank = n // HG, banks[n % 4]
                        for h, (a, b) in enumerate(((0, P), (P, 3 * P))):
                            pe.matmul(bank[:, a:b], qT[:, m, h * P:(h + 1) * P], km[:, n, 0:b - a], start=True, stop=False)
                            ins = pe.matmul(bank[:, b - P:b], identb[:, :], causal[:, :], start=False, stop=True)
                        pl.fills(ins, ("s", n))

                scores(0)
                scores(1)
                pe.wait_ge(a_v, i + 1)
                for p in range(NP):
                    for n in heads(p):
                        pe.wait_ge(a_norm, NH * i + n + 1)
                        pl.wait_free(pe, ("t", n), i)
                        bank, e = banks[4 + n % 2], w["e"]
                        pe.transpose(bank[:, 0:P], e[:, n % 4, 0:P], ident[:, :])
                        pe.transpose(bank[:, P:2 * P], e[:, n % 4, P:2 * P], ident[:, :])
                        pl.fills(pe.transpose(bank[:, 2 * P:3 * P], e[:, n % 4, 2 * P:3 * P], ident[:, :]), ("t", n))
                    if p + 2 < NP:
                        scores(p + 2)
                    g = p // 4
                    if p % 4 == 0:
                        pl.wait_free(pe, ("o", g), i)
                    for n in heads(p):
                        pe.wait_ge((a_ptA, a_ptD)[n % 2], NP * i + p + 1)
                        j = n % HG
                        lhs = [vm[:, h, g, j * P:(j + 1) * P] for h in range(2)]
                        pe.matmul(banks[6 + g][:, 0:S], lhs[0], w["pt"][:, n % 4, 0:S], start=j == 0, stop=False)
                        ins = pe.matmul(banks[6 + g][:, P:S], lhs[1], w["pt"][:, n % 4, S:S + P], start=False, stop=j == HG - 1)
                    if p % 4 == 3:
                        pl.fills(ins, ("o", g))
                pe.wait_ge(a_oT, 2 * i + 2)
                pl.wait_free(pe, "out", i)
                for h in range(2):
                    ins = product(banks[0][:, h * D:(h + 1) * D], [(w["oT"][:, k, h * P:(h + 1) * P], w_o1[:, k, :]) for k in range(KD)])
                pl.fills(ins, "out")

            pl, w = plan_x, x_b
            with pe.Fori(0, B) as i:
                pe.wait_ge(x_xn, i + 1)
                transposed("xt", banks[6], i, w["xn"])
                xnT, cT, qT, kz, v = w["xnT"], w["cT"], w["qT"], w["kz"], w["v"]
                pe.wait_ge(x_ctx, 16 * (i + 1))
                for m in range(4):
                    pl.wait_free(pe, ("k", m), i)
                    for a in range(2):
                        c = (2 * m + a) * P
                        ins = product(banks[m][:, a * S:(a + 1) * S], [(w_xkv[:, k, c:c + P], cT[:, k, :]) for k in range(KD)])
                    pl.fills(ins, ("k", m))
                for m in range(4):
                    pl.wait_free(pe, ("v", m), i)
                    c, h = XI + (m % 2) * 512, m // 2
                    pl.fills(product(banks[4 + m][:, :], [(cT[:, k, h * P:(h + 1) * P], w_xkv[:, k, c:c + 512])
                                                          for k in range(KD)]), ("v", m))
                pe.wait_ge(x_xnT, i + 1)
                for m in range(4):
                    pl.wait_free(pe, ("q", m), i)
                    for a in range(2):
                        c = (2 * m + a) * P
                        ins = product(banks[m][:, a * S:(a + 1) * S], [(w_xq[:, k, c:c + P], xnT[:, k, :]) for k in range(KD)])
                    pl.fills(ins, ("q", m))
                pe.wait_ge(x_k, i + 1)
                pe.wait_ge(x_q, i + 1)

                def scores(p):
                    for n in heads(p):
                        pl.wait_free(pe, ("s", n), i)
                        for h in range(2):
                            ins = pe.matmul(banks[n % 4][:, h * S:(h + 1) * S], qT[:, p, h * P:(h + 1) * P], kz[:, n, :],
                                            start=True, stop=True)
                        pl.fills(ins, ("s", n))

                scores(0)
                scores(1)
                pe.wait_ge(x_v, i + 1)
                for p in range(NP):
                    for n in heads(p):
                        pe.wait_ge(x_norm, NH * i + n + 1)
                        pl.wait_free(pe, ("t", n), i)
                        for kt in range(2):
                            for h in range(2):
                                ins = pe.transpose(banks[4 + n % 2][:, kt * S + h * P:kt * S + (h + 1) * P],
                                                   w["e"][:, n % 4, h * S + kt * P:h * S + (kt + 1) * P], ident[:, :])
                        pl.fills(ins, ("t", n))
                    if p + 2 < NP:
                        scores(p + 2)
                    pl.wait_free(pe, ("o", p), i)
                    for n in heads(p):
                        pe.wait_ge((x_ptA, x_ptD)[n % 2], NP * i + p + 1)
                        r = slice(64 * (n % 2), 64 * (n % 2) + 64)
                        ins = product(banks[6 + p % 2][r, 0:S], [(v[:, kt, n * 64:(n + 1) * 64], w["pt"][:, n % 2, kt * S:(kt + 1) * S])
                                                                 for kt in range(2)])
                    pl.fills(ins, ("o", p))
                pe.wait_ge(x_oT, NP * (i + 1))
                pl.wait_free(pe, "out", i)
                for h in range(2):
                    ins = product(banks[0][:, h * D:(h + 1) * D], [(w["oT"][:, p, h * P:(h + 1) * P], w_o2[:, p, :]) for p in range(NP)])
                pl.fills(ins, "out")

            pe.wait_ge(in_b3, 16 * 4)
            pl, w = plan_m, m_b
            with pe.Fori(0, B) as i:
                pe.wait_ge(m_xs, i + 1)
                transposed("xt", banks[0], i, w["xs"])
                pe.wait_ge(m_xT, i + 1)
                pl.wait_free(pe, "lg", i)
                for h in range(2):
                    ins = product(banks[1][:, h * NE:(h + 1) * NE], [(w["xT"][:, k, h * P:(h + 1) * P], w_r[:, k, :]) for k in range(KD)])
                pl.fills(ins, "lg")
                pe.wait_ge(m_oh, i + 1)
                pl.wait_free(pe, "oh", i)
                for h in range(2):
                    ins = pe.transpose(banks[2][0:NE, h * P:(h + 1) * P], w["oh"][:, h, :], ident[:, :])
                pl.fills(ins, "oh")
                for e in range(NE):
                    transposed(("xm", e), banks[3 + e], i, w["xm"][:, :, e])
                pe.wait_ge(m_ohT, 3 * (i + 1))
                pe.wait_ge(m_xmT, 2 * (i + 1))
                for m in range(NF // 2):
                    pl.wait_free(pe, ("h", m), i)
                    for a in range(2):
                        c = slice((2 * m + a) * P, (2 * m + a + 1) * P)
                        ins = product(banks[m % 3][:, a * S:(a + 1) * S],
                                      [(w_1[:, e * KD + k, c], w["xmT"][:, e, k, :]) for e in range(NE) for k in range(KD)]
                                      + [(b_1[:, c], w["ohT"][:, :])])
                    pl.fills(ins, ("h", m))
                pe.wait_ge(m_hT, 4 * (i + 1))
                pl.wait_free(pe, "out", i)
                for h in range(2):
                    ins = product(banks[7][:, h * D:(h + 1) * D], [(w["hT"][:, m, h * P:(h + 1) * P], w_o3[:, m, :]) for m in range(NF)])
                pl.fills(ins, "out")


def _layout(inp):
    import numpy as np

    f = lambda a: np.ascontiguousarray(np.asarray(a), dtype=None)

    def ktiles(w):
        k, n = w.shape
        return w.reshape(k // P, P, n).transpose(1, 0, 2)

    def fcols(v):
        return v.reshape(-1, P).T

    a = {k: np.asarray(v) for k, v in inp.items()}
    x, c = a["x"], a["ctx_1024"]
    out = {}
    out["w_in"] = ktiles(a["L0_attn_W_in"])
    out["w_xp"] = ktiles(a["L0_attn_W_xproj"])
    out["w_dt"] = a["L0_attn_W_dt"]
    out["w_o0"] = ktiles(a["L0_attn_W_out"])
    out["w_ch"] = np.stack([ktiles(a[f"L0_xattn_{n}"].T) for n in ("Wi", "Wg", "A", "Bm", "Wo")], axis=1)
    alog = a["L0_attn_A_log"].reshape(ND, P, NS).transpose(1, 2, 0).reshape(P, NS * ND)
    bqkv = a["L1_attn_b_qkv"]
    one = lambda v: np.broadcast_to(v.reshape(1, 1), (P, 1))
    out["cols"] = np.concatenate([
        fcols(a["L0_attn_b_dt"]), alog, fcols(a["L0_attn_D"]), fcols(a["L0_xattn_bi"]), fcols(a["L0_xattn_bg"]),
        fcols(np.repeat(a["L0_xattn_decay"].reshape(-1), D // 16)),
        fcols(a["L1_attn_ln_g"]), fcols(a["L1_attn_ln_b"]), fcols(bqkv[:D]), fcols(bqkv[D:2 * D]),
        fcols(a["L1_xattn_ln_gamma"]), fcols(a["L1_xattn_ln_beta"]),
        one(a["L1_attn_b_ent"]), one(a["L1_xattn_gate"])], axis=1)
    out["rows"] = np.concatenate([a["L0_xattn_bo"], a["L1_attn_b_out"], bqkv[2 * D:], a["L1_xattn_b_out"],
                                  a["L1_ffn_bo"], a["L1_ffn_ln_gamma"], a["L1_ffn_ln_beta"]]).reshape(1, -1)
    out["xT"] = x.reshape(B, NCH, TC, KD, P).transpose(4, 1, 3, 0, 2).reshape(P, NCH, KD, CC)
    out["x_tok"] = x.reshape(4, 2, NCH, TC, D).transpose(2, 1, 3, 0, 4).reshape(NCH, P, 4, D)
    out["ctxT"] = ktiles(c.reshape(T, D).T)
    out["ident"] = np.eye(P, dtype=np.float32)
    q, k = np.arange(P)[:, None], np.arange(P)[None, :]
    out["causal"] = np.where(k > q, np.float32(-1e30), np.float32(0)).astype(np.float32)
    out["w_gate"] = ktiles(a["L0_ffn_w_gate"].T)
    out["w_up"] = ktiles(a["L0_ffn_w_up"].T)
    out["w_down"] = ktiles(a["L0_ffn_w_down"].T)
    wqkv = a["L1_attn_w_qkv"].T
    out["w_qk"] = ktiles(wqkv[:, :2 * D])
    out["w_v"] = ktiles(wqkv[:, 2 * D:])
    out["w_ent"] = fcols(a["L1_attn_w_ent"])
    out["w_o1"] = ktiles(a["L1_attn_w_out"].T)
    out["w_xq"] = ktiles(a["L1_xattn_w_q"])
    out["w_xkv"] = ktiles(a["L1_xattn_w_kv"])
    out["w_o2"] = ktiles(a["L1_xattn_w_out"])
    out["w_r"] = ktiles(a["L1_ffn_W_router"])
    out["w_1"] = ktiles(a["L1_ffn_W1"].reshape(NE * D, F))
    out["b_1"] = a["L1_ffn_b1"]
    out["w_o3"] = ktiles(a["L1_ffn_Wo"])
    out["prio"] = np.broadcast_to(np.arange(NE, 0, -1, dtype=np.float32), (P, 2, NE))
    out["headm"] = (np.arange(P)[:, None] // 16 == np.arange(8)[None, :]).astype(np.float32)
    return {k: f(v) for k, v in out.items()}


def build(nc, arrays):
    dr = {n: nc.dram_tensor("in_" + n, list(a.shape), F32, kind="ExternalInput").ap() for n, a in arrays.items()}
    dr["bcd"] = nc.dram_tensor("bcd", [NCH, 32, CC], F32, kind="Internal").ap()
    dr["out"] = nc.dram_tensor("out", [B, S, D], F32, kind="ExternalOutput").ap()
    build_program(nc, dr)


def kernel(**inputs):
    import concourse.bacc as _bacc
    from concourse.bass_utils import run_bass_kernel_spmd as _run

    nc = _bacc.Bacc("TRN2", target_bir_lowering=False, num_devices=1)
    arrays = _layout(inputs)
    build(nc, arrays)
    r = _run(nc, [{"in_" + n: v for n, v in arrays.items()}], core_ids=[0])
    return r.results[0]["out"]
```

```python
from contextlib import ExitStack

import concourse.bass as bass
from concourse import mybir

P = 128
F32 = mybir.dt.float32
BF16 = mybir.dt.bfloat16
FP16 = mybir.dt.float16
ALU = mybir.AluOpType
ACT = mybir.ActivationFunctionType
AX = mybir.AxisListType

B, S, D = 8, 256, 256
T = B * S
KD = D // P
NCH = 4
TC = S // NCH
CC = B * TC
DI = 512
ND = DI // P
NS = 16
DTR = 64
NH = 16
HG = NH // 2
XI = 1024
NP = NH // 2
F = 1024
NF = F // P
NE = 4
MAGIC = 1.5 * 2.0 ** 23
TINY = 1e-5
SOFT = 2.5
GSC = 1024.0

COLS = {}
_at = 0
for _name, _n in (("b_dt", 4), ("A_log", 64), ("Dskip", 4), ("bi", 2), ("bg", 2), ("decay", 2),
                  ("ln_g", 2), ("ln_b", 2), ("bq", 2), ("bk", 2), ("gam", 2), ("bet", 2),
                  ("b_ent", 1), ("gate", 1)):
    COLS[_name] = (_at, _at + _n)
    _at += _n
NCOLS = _at
ROWS = ["bo", "b_out", "bv", "b_out2", "bo_ffn", "lng", "lnb"]


class Own:

    def __init__(self, eng, sem):
        self.eng, self.sem, self.base, self.n = eng, sem, 0, 0

    def did(self, ins):
        ins.then_inc(self.sem, 1)
        self.n += 1

    def wait(self):
        self.eng.wait_ge(self.sem, self.base + self.n)

    def enter(self, i, per):
        self.start, self.per = self.base + self.n, per
        self.base, self.n = self.start + i * per, 0

    def leave(self, count):
        assert self.n == self.per, (self.n, self.per)
        self.base, self.n = self.start + count * self.per, 0


class Batch:

    def __init__(self, offset, trip=0, looped=False):
        self.offset, self.trip, self.looped = offset, trip, looped
        self.index = offset + 2 * trip
        self.slot = offset % 2

    def near(self, delta):
        return Batch(self.offset + delta, self.trip, self.looped)


class Order:

    def __init__(self, base, sequence):
        self.places = {item: base + n for n, item in enumerate(sequence)}
        self.end = base + len(sequence)

    def place(self, key, b):
        at = self.places[key, b.offset]
        if b.looped:
            step = self.places[key, b.offset + 2] - at
            assert self.places[key, b.offset + 4] == at + 2 * step
            at = at + b.trip * step
        return at


class Plan:

    def __init__(self, full, free, base, uses):
        self.full, self.free = full, free
        self.bank = {key: bank for key, _, bank in uses}
        self.orders = [Order(base[n], [(key, b) for key, b, bank in uses if bank == n]) for n in range(8)]
        self.end = [order.end for order in self.orders]

    def count(self, key, b):
        return self.orders[self.bank[key]].place(key, b)

    def wait_full(self, eng, key, b):
        eng.wait_ge(self.full[self.bank[key]], self.count(key, b) + 1)

    def wait_free(self, eng, key, b):
        eng.wait_ge(self.free[self.bank[key]], self.count(key, b) + 1)

    def wait_freed(self, eng, key, b):
        eng.wait_ge(self.free[self.bank[key]], self.count(key, b) + 2)

    def fills(self, ins, key):
        ins.then_inc(self.full[self.bank[key]], 1)

    def frees(self, ins, key):
        ins.then_inc(self.free[self.bank[key]], 1)


def over_batches(eng, body, own=None, per=0):
    body(Batch(0), True, False)
    with eng.Fori(0, B // 2 - 1) as j:
        if own:
            own.enter(j, per)
        body(Batch(1, j, True), False, False)
        body(Batch(2, j, True), False, False)
        if own:
            own.leave(B // 2 - 1)
    body(Batch(B - 1), False, True)


def build_program(nc, dr):
    ctx = ExitStack()
    with ctx:
        def sb(name, shape, dt=F32):
            return ctx.enter_context(nc.sbuf_tensor(name, shape, dt))

        def ps(name, shape, dt=F32):
            return ctx.enter_context(nc.psum_tensor(name, shape, dt))

        def sem(name):
            return ctx.enter_context(nc.semaphore(name))

        cols = sb("cols", [P, NCOLS])
        rows = sb("rows", [P, len(ROWS), D])
        ident = sb("ident", [P, P])
        identb = sb("identb", [P, P], BF16)
        causal = sb("causal", [P, P], BF16)
        headm = sb("headm", [P, 8])
        x_tok = sb("x_tok", [P, 16, D])

        def col(name, j=0):
            a = COLS[name][0]
            return cols[:, a + j:a + j + 1]

        def row(name):
            return rows[:, ROWS.index(name), :]

        front = ExitStack()
        fsb = lambda name, shape, dt=F32: front.enter_context(nc.sbuf_tensor(name, shape, dt))
        w_in = fsb("w_in", [P, KD, 2 * DI])
        w_xp = fsb("w_xp", [P, ND, 96])
        w_dt = fsb("w_dt", [DTR, DI])
        w_o0 = fsb("w_o0", [P, ND, D])
        w_ch = fsb("w_ch", [P, 5, KD, D])
        wi_t, wg_t, a_t, bm_t, wo_t = (w_ch[:, j] for j in range(5))
        a_neg = fsb("a_neg", [P, KD, D])
        a_parts = [fsb(f"a_part{j}", [P, KD, D], BF16) for j in range(3)]
        a_coef = fsb("a_coef", [P, NS * ND])
        d_diag = fsb("d_diag", [P, ND, P])
        causal_f = fsb("causal_f", [P, P])
        ctxT = fsb("ctxT", [P, KD, T])
        work4 = fsb("work4", [P, 4, KD * CC])
        kv = work4[:, :, :].rearrange("p (k a) c -> p k (a c)", k=KD)
        ret = work4[:, 0, :].rearrange("p (k c) -> p k c", k=KD)
        inp = work4[:, 1, :].rearrange("p (k c) -> p k c", k=KD)
        gate = work4[:, 2, :].rearrange("p (k c) -> p k c", k=KD)
        gsc = work4[:, 3, :].rearrange("p (t c) -> p t c", t=TC)
        xTc = fsb("xTc", [P, 2, KD, CC])
        xtk = fsb("xtk", [P, 2, 4, D])
        xp = fsb("xp", [P, ND, CC])
        zs = fsb("zs", [P, ND, CC])
        xd = fsb("xd", [96, CC])
        ee = fsb("ee", [P, ND, CC])
        um = fsb("um", [P, ND, CC])
        bc = fsb("bc", [P, 2, 2, CC])
        abar = fsb("abar", [P, 2, B, TC + 1])
        dbx = fsb("dbx", [P, 2, B, TC + 1])
        scan_out = fsb("scan_out", [P, 2 * B * (TC + 1) + 2 * CC])
        hh = scan_out[:, 0:2 * B * (TC + 1)].rearrange("p (a b t) -> p a b t", a=2, b=B)
        hc = scan_out[:, 2 * B * (TC + 1):].rearrange("p (a c) -> p a c", a=2)
        lnu = scan_out[:, 0:ND * CC].rearrange("p (d c) -> p d c", d=ND)
        hstate = fsb("hstate", [P, NS * ND, B])
        pf = fsb("pf", [P, TC, KD * B])
        pparts = fsb("pparts", [P, TC, 3, KD * B], BF16)
        states = fsb("states", [P, KD * B, TC])
        s_cur = fsb("s_cur", [P, 2, KD * B])
        gsf = fsb("gsf", [P, KD * B])
        gs2 = fsb("gs2", [P, 2, KD * B], FP16)
        x1 = fsb("x1", [P, 2, 4, D])
        res = fsb("res", [P, 4, D])
        x2c = fsb("x2c", [P, 2, 4, D])
        st6 = fsb("st6", [P, 4, 6])
        mv = fsb("mv", [P, 4, 2])
        lu = fsb("lu", [P, 4])
        lr = fsb("lr", [P, 4])
        l1 = fsb("l1", [P, 4])
        l2 = fsb("l2", [P, 4])

        front.close()

        cT = sb("cT", [P, KD, S])
        ones = sb("ones", [P, P])
        prio = sb("prio", [P, 2, NE])
        wsum = sb("wsum", [P, 3])
        wmean = sb("wmean", [P, 3])
        wrec = sb("wrec", [P, 3])
        w_qk = sb("w_qk", [P, KD, 2 * D])
        w_v = sb("w_v", [P, KD, D])
        w_ent = sb("w_ent", [P, KD])
        w_o1 = sb("w_o1", [P, KD, D])
        w_xq = sb("w_xq", [P, KD, XI])
        w_xkv = sb("w_xkv", [P, KD, 2 * XI])
        w_o2 = sb("w_o2", [P, NP, D])
        w_1 = sb("w_1", [P, NE * KD, F])
        w_raw = w_1[:, 0:6, :].rearrange("p (a k) n -> p a (k n)", a=3)
        b_1 = sb("b_1", [P, F])
        w_o3 = sb("w_o3", [P, NF, D])
        w_r = sb("w_r", [P, KD, NE])
        bk_m = sb("bk_m", [P, NH])
        bq_s = sb("bq_s", [P, KD])
        tg = sb("tg", [P, 1])
        nb_ent = sb("nb_ent", [P, 1])
        stats6 = sb("stats6", [P, 2, 6])
        mvb = sb("mvb", [P, 2, 2])
        lub = sb("lub", [P, 2])
        lrb = sb("lrb", [P, 2])
        l1b = sb("l1b", [P, 2])
        l2b = sb("l2b", [P, 2])
        resb = sb("resb", [P, 2, D])
        qv = sb("qv", [P, 2, 6, 2])
        hs = sb("hs", [P, 2, 5, 2])

        def work(fn):
            with ExitStack() as region:
                return fn(lambda name, shape, dt=F32: region.enter_context(nc.sbuf_tensor(name, shape, dt)))

        f_b = work(lambda w: dict(wg_q=w("wg_q", [P, KD, F], BF16), wu_q=w("wu_q", [P, KD, F], BF16), wd_q=w("wd_q", [P, NF, D], BF16),
                                  tmp=w("f_tmp", [P, 2, F]), xq=w("f_xq", [P, 2, D], BF16), xqT=w("f_xqT", [P, 2, 2, KD, P], BF16),
                                  sg=w("f_sg", [P, 2, F]), hv=w("f_hv", [P, 2, F]), hq=w("f_hq", [P, 2, F], BF16),
                                  hqT=w("f_hqT", [P, 2, NF, P], BF16)))
        a_b = work(lambda w: dict(xn=w("a_xn", [P, 2, D]), xnT=w("a_xnT", [P, KD, S]), qT=w("a_qT", [P, 2, KD, S]), kT=w("a_kT", [P, KD, S]),
                                  km=w("a_km", [P, 2, NH, S]), vm=w("a_vm", [P, 2, 2, 2, HG * (P + 16)]), nm=w("a_nm", [P, NH, 2]),
                                  sm=w("a_sm", [P, NH, 2]), rr=w("a_rr", [P, NH, 2]), e=w("a_e", [P, 4, 384]),
                                  pt=w("a_pt", [P, 4, 384]), oT=w("a_oT", [P, KD, S]), gt=w("a_gt", [P, 4, 2])))
        x_b = work(lambda w: dict(xn=w("x_xn", [P, 2, D]), xnT=w("x_xnT", [P, KD, S]), 
                                  qT=w("x_qT", [P, 2, NP, S]), kz=w("x_kz", [P, 2, NH, S]), v=w("x_v", [P, 2, 2, XI]),
                                  nm=w("x_nm", [P, NH, 2]), sm=w("x_sm", [P, NH, 2]), rr=w("x_rr", [P, NH, 2]),
                                  e=w("x_e", [P, 4, 2 * S]), pt=w("x_pt", [P, 4, 2 * S]), oT=w("x_oT", [P, NP, S])))
        wg_q, wu_q, wd_q = (f_b[n] for n in ("wg_q", "wu_q", "wd_q"))
        m_b = work(lambda w: dict(xs=w("m_xs", [P, 2, D]), xT=w("m_xT", [P, KD, S]), lg=w("m_lg", [P, 2, NE]),
                                  oh=w("m_oh", [P, 2, NE]), mx=w("m_mx", [P, 4, 2]), xm=w("m_xm", [P, 2, NE, D]),
                                  xmT=w("m_xmT", [P, 2, NE, KD, S]), ohT=w("m_ohT", [P, 2, S]), hT=w("m_hT", [P, NF, S]),
                                  y=w("m_y", [P, 2, D]), o=w("m_o", [P, 2, D])))

        ybank = [ps(f"ybank{d}", [P, 512]) for d in range(4)]
        cbank = [ps(f"cbank{j}", [P, 512]) for j in range(2)]
        gbank = [ps(f"gbank{j}", [P, 512]) for j in range(2)]
        banks = ybank + cbank + gbank

        in_w = sem("in_w")
        in_w2 = sem("in_w2")
        in_ctx = sem("in_ctx")
        in_xT = [sem(f"in_xT{j}") for j in range(2)]
        in_xtk = [sem(f"in_xtk{j}") for j in range(2)]
        setup_dve = sem("setup_dve")
        setup_act = sem("setup_act")
        dve_own = sem("dve_own")
        act_own = sem("act_own")
        g_full = [sem(f"g_full{j}") for j in range(2)]
        g_free = [sem(f"g_free{j}") for j in range(2)]
        xd_ready = sem("xd_ready")
        xp_ready = sem("xp_ready")
        zs_ready = sem("zs_ready")
        bc_stored = sem("bc_stored")
        bc_loaded = [sem(f"bc_loaded{j}") for j in range(2)]
        e_ready = sem("e_ready")
        ec_ready = sem("ec_ready")
        lnu_ready = sem("lnu_ready")
        dt_ready = sem("dt_ready")
        seeded = sem("seeded")
        abar_ready = sem("abar_ready")
        scans = sem("scans")
        h_saved = sem("h_saved")
        hc_ready = sem("hc_ready")
        h_in = sem("h_in")
        hc_used = sem("hc_used")
        gs_ready = sem("gs_ready")
        chain_mm = sem("chain_mm")
        tanh_done = sem("tanh_done")
        y_ready = sem("y_ready")
        ln_u = sem("ln_u")
        ln_r = sem("ln_r")
        x1_ready = sem("x1_ready")
        ret_ready = sem("ret_ready")
        inp_ready = sem("inp_ready")
        gate_ready = sem("gate_ready")
        om_ready = sem("om_ready")
        pf_ready = sem("pf_ready")
        p_ready = sem("p_ready")
        st_copied = sem("st_copied")
        x2_ready = sem("x2_ready")
        x2_moved = [sem(f"x2_moved{j}") for j in range(2)]
        b_full = [sem(f"b_full{j}") for j in range(8)]
        b_free = [sem(f"b_free{j}") for j in range(8)]
        in_b1 = sem("in_b1")
        in_b2 = sem("in_b2")
        in_b3 = sem("in_b3")
        front_done = sem("front_done")
        w_summed = sem("w_summed")
        w_total = sem("w_total")
        w_ready = sem("w_ready")
        act_set = sem("act_set")
        dve_set = sem("dve_set")
        pool_set = sem("pool_set")
        stats_seen = sem("stats_seen")
        b_lnu = sem("b_lnu")
        b_lnr = sem("b_lnr")
        f_xq = sem("f_xq")
        f_hq = sem("f_hq")
        a_xn = sem("a_xn")
        a_xnT = sem("a_xnT")
        a_q = sem("a_q")
        a_km = sem("a_km")
        a_v = sem("a_v")
        x_zeroed = sem("x_zeroed")
        a_max = sem("a_max")
        a_norm = sem("a_norm")
        x_xn = sem("x_xn")
        x_xnT = sem("x_xnT")
        x_ctx = sem("x_ctx")
        x_max = sem("x_max")
        x_norm = sem("x_norm")
        m_xs = sem("m_xs")
        m_oh = sem("m_oh")
        m_out = sem("m_out")
        stored = sem("stored")

        uses = []
        for s in range(NCH + 1):
            if s < NCH:
                uses += [("xz", s, m) for m in range(5)] + [("xd", s, 0)]
                uses += [("xz", s, m) for m in range(5, 8)] + [("dt", s, m) for m in range(4)]
                uses += [("o1", s, j) for j in range(4)] + [("xt", s, k) for k in range(KD)]
                uses += [(what, s, m) for what in ("inp", "gate", "pp") for m in range(KD)]
            if s:
                uses += [("o2", s - 1, j) for j in range(4)]
        use_at = {key: n for n, key in enumerate(uses)}

        def before_loop(key, s):
            what, c, _ = key
            return c < s - (what == "o2") or (c == s and what in ("xz", "xd", "dt"))

        def bank_of(*key):
            return gbank[use_at[key] % 2]

        def wait_full(eng, *key):
            n = use_at[key]
            eng.wait_ge(g_full[n % 2], n // 2 + 1)

        def wait_free(eng, *key):
            n = use_at[key]
            if n >= 2:
                eng.wait_ge(g_free[n % 2], n // 2)

        def fills(ins, *key):
            ins.then_inc(g_full[use_at[key] % 2], 1)

        def frees(ins, *key):
            ins.then_inc(g_free[use_at[key] % 2], 1)

        def btc(ap):
            return ap.rearrange("p (b t) -> p b t", b=B)

        def in_chunk(ap, s):
            return ap.rearrange("p (b c t) -> p c b t", b=B, c=NCH)[:, s]

        def lncount(kind, s):
            order = []
            for q in range(NCH + 1):
                order += [("a", q)] * (q < NCH) + [("b", q - 1)] * (q > 0)
            return order.index((kind, s))

        def staged(before, body, after):
            return ([(key, b, bank) for key, b, bank in before]
                    + [(key, b + d, bank) for b in range(B) for key, d, bank in body if 0 <= b + d < B]
                    + [(key, b, bank) for key, b, bank in after])

        pro = [(("xt", h), 0, 4) for h in range(2)]
        gu = lambda h: [(("g", h, 0), 0, 0), (("g", h, 1), 0, 1), (("u", h, 0), 0, 2), (("u", h, 1), 0, 3)]
        down = lambda h, d: [(("ht", h), d, 5), (("dn", h), d, 6 + h)]
        plan_f = Plan(b_full, b_free, [0] * 7 + [1], staged(
            pro, gu(0) + down(1, -1) + gu(1) + [(("xt", h), 1, 4) for h in range(2)] + down(0, 0),
            [(key, B - 1, bank) for key, _, bank in down(1, 0)]))
        heads = lambda p: (2 * p, 2 * p + 1)

        def attention_uses(mid, late, sums):
            body = []
            for p in range(NP):
                body += [(("s", n % NH), n // NH, n % 4) for n in heads(p + 2)]
                body += mid.get(p, [])
                body += [(("t", n), 0, 4 + n % 2) for n in heads(p)]
                body += [(("o", g), 0, bank) for first, g, bank in sums if p - 1 == first]
                body += late.get(p, [])
            return body

        first_scores = [(("s", n), 0, n) for n in range(4)]
        plan_a = Plan(b_full, b_free, plan_f.end, staged(
            [("xt", 0, 7), ("q", 0, 7), ("k", 0, 7), ("ge", 0, 7), ("v", 0, 6)] + first_scores,
            attention_uses({2: [("xt", 1, 7)], 3: [("k", 1, 7)], 5: [("v", 1, 6)]},
                           {1: [("out", -1, 7)], 2: [("q", 1, 7)], 3: [("ge", 1, 7)]}, ((0, 0, 6), (4, 1, 7))),
            [("out", B - 1, 7)]))
        X_MID = {0: ("k", 0), 1: ("k", 2), 2: ("k", 3), 3: ("q", 0), 4: ("q", 2), 5: ("v", 0), 6: ("v", 2)}
        X_LATE = {0: ("k", 1), 2: "xt", 3: ("q", 1), 4: ("q", 3), 5: ("v", 1), 6: ("v", 3)}
        plan_x = Plan(b_full, b_free, plan_a.end, staged(
            [(key, 0, 7) for key in [("k", m) for m in range(4)] + ["xt"] + [("q", m) for m in range(4)]
             + [("v", m) for m in range(4)]] + first_scores,
            attention_uses({p: [(key, 1, 7)] for p, key in X_MID.items()},
                           {**{p: [(key, 1, 7)] for p, key in X_LATE.items()}, 1: [("out", -1, 7)]},
                           [(2 * g, g, 6) for g in range(NP // 2)]),
            [("out", B - 1, 7)]))
        m_next = [("oh", 1, 6)] + [(("xm", e), 1, 4 + e) for e in range(NE)]
        plan_m = Plan(b_full, b_free, plan_x.end, staged(
            [("xt", 0, 4), ("lg", 0, 5)] + [(key, 0, bank) for key, _, bank in m_next],
            [(("h", 0), 0, 0), ("out", -1, 7), ("xt", 1, 4), (("h", 1), 0, 1), ("lg", 1, 5), (("h", 2), 0, 2)]
            + m_next + [(("h", 3), 0, 3)], [("out", B - 1, 7)]))

        steps_of = lambda *body: [(key, b + d) for b in range(B) for key, d in body if 0 <= b + d < B]
        norms = Order(0, steps_of(("f", -1)) + [("f", B - 1), ("a0", 0)] + steps_of(("a0", 1), ("a1", -1))
                      + [("a1", B - 1), ("x0", 0)] + steps_of(("x0", 1), ("x1", -1)) + [("x1", B - 1)]
                      + steps_of(("m0", -1), ("m1", -1)) + [("m0", B - 1), ("m1", B - 1)])

        block = ctx.enter_context(nc.Block())

        @block.sync
        def _(sp):
            sp.sem_inc(stored, 16)
            for b in range(8):
                sp.sem_inc(b_free[b], 1)
            for dst, src in ((w_in[:, :, :], dr["w_in"]), (w_xp[:, :, :], dr["w_xp"]), (w_dt[:, :], dr["w_dt"]),
                             (cols[:, :], dr["cols"]), (ident[:, :], dr["ident"])):
                sp.dma_start(dst, src).then_inc(in_w, 16)
            sp.dma_start(xTc[:, 0], dr["xT"][:, 0]).then_inc(in_xT[0], 16)
            for dst, src in ((w_o0[:, :, :], dr["w_o0"]), (w_ch[:, :, :, :], dr["w_ch"]),
                             (causal_f[:, :], dr["causal"]), (headm[:, :], dr["headm"]),
                             (rows[:, :, :].rearrange("p a b -> p (a b)"), dr["rows"].broadcast_to([P, len(ROWS) * D]))):
                sp.dma_start(dst, src).then_inc(in_w2, 16)
            sp.dma_start(ctxT[:, :, :], dr["ctxT"]).then_inc(in_ctx, 16)
            sp.dma_start(xtk[:, 0], dr["x_tok"][0]).then_inc(in_xtk[0], 16)
            for s in range(NCH + 1):
                if s < NCH:
                    if s + 1 < NCH:
                        if s:
                            sp.wait_ge(zs_ready, s)
                            sp.wait_ge(x1_ready, s)
                        sp.dma_start(xTc[:, (s + 1) % 2], dr["xT"][:, s + 1]).then_inc(in_xT[(s + 1) % 2], 16)
                        sp.dma_start(xtk[:, (s + 1) % 2], dr["x_tok"][s + 1]).then_inc(in_xtk[(s + 1) % 2], 16)
                    sp.wait_ge(xd_ready, s + 1)
                    sp.dma_start(dr["bcd"][s], xd[DTR:96, :]).then_inc(bc_stored, 16)
                    sp.wait_ge(bc_stored, 16 * (s + 1))
                    src = dr["bcd"][s].rearrange("(a n) t -> n a t", a=2)
                    with sp.Fori(0, NS // 2) as i:
                        for u in range(2):
                            sp.wait_ge(hc_ready, 4 * (NS * s + 2 * i + u) + 1)
                            sp.dma_start(bc[:, u], src[bass.ds(2 * i + u, 1)].broadcast_to([P, 2, CC]))\
                              .then_inc(bc_loaded[u], 16)
                if s:
                    sp.wait_ge(x2_ready, s)
                    c = s - 1
                    for j in range(4):
                        for b2 in range(2):
                            sp.dma_start(x_tok[(c % 2) * TC:(c % 2 + 1) * TC, (2 * j + b2) * 2 + c // 2, :],
                                         x2c[b2 * TC:(b2 + 1) * TC, c % 2, j, :]).then_inc(x2_moved[c % 2], 16)
            for j in range(2):
                sp.wait_ge(x2_moved[j], 16 * 8 * NCH // 2)
            sp.wait_ge(front_done, 1)
            for a, name in enumerate(("w_gate", "w_up", "w_down")):
                sp.dma_start(w_raw[:, a, :], dr[name].rearrange("p k n -> p (k n)")).then_inc(in_b1, 16)
            sp.dma_start(prio[:, :, :], dr["prio"]).then_inc(in_b1, 16)
            for dst, name in ((w_qk, "w_qk"), (w_v, "w_v"), (w_o1, "w_o1"), (w_xq, "w_xq"), (w_xkv, "w_xkv"), (w_o2, "w_o2")):
                sp.dma_start(dst[:, :, :], dr[name]).then_inc(in_b2, 16)
            sp.dma_start(w_ent[:, :], dr["w_ent"]).then_inc(in_b2, 16)
            sp.dma_start(w_o3[:, :, :], dr["w_o3"]).then_inc(in_b3, 16)
            sp.dma_start(w_r[:, :, :], dr["w_r"]).then_inc(in_b3, 16)
            sp.wait_ge(pool_set, 1)
            sp.dma_start(b_1[0:NE, :], dr["b_1"]).then_inc(in_b3, 16)
            sp.wait_ge(w_ready, 1)
            sp.dma_start(w_1[:, :, :], dr["w_1"]).then_inc(in_b3, 16)
            ctx_b = dr["ctxT"].rearrange("p k (b c) -> p b k c", b=B)
            sp.dma_start(cT[:, :, :], ctx_b[:, 0]).then_inc(x_ctx, 16)

            def next_context(b):
                plan_x.wait_full(sp, ("v", 3), b)
                nxt = b.near(1).index
                sp.dma_start(cT[:, :, :], ctx_b[:, bass.ds(nxt, 1)].rearrange("p o k c -> p (o k) c")).then_inc(x_ctx, 16)

            next_context(Batch(0))
            with sp.Fori(0, B // 2 - 1) as j:
                next_context(Batch(1, j, True))
                next_context(Batch(2, j, True))
            o_rows = dr["out"].rearrange("b (h p) d -> b p h d", h=2)
            with sp.Fori(0, B) as i:
                sp.wait_ge(m_out, i + 1)
                sp.dma_start(o_rows[bass.ds(i, 1)].rearrange("o p h d -> (o p) h d"), m_b["o"][:, :, :]).then_inc(stored, 16)
            sp.wait_ge(stored, 16 * (B + 1))

        @block.scalar
        def _(act):
            own = Own(act, act_own)
            act.sem_inc(tanh_done, 1)
            act.wait_ge(in_w, 16 * 5)
            a0, a1 = COLS["A_log"]
            act.activation(a_coef[:, :], cols[:, a0:a1], ACT.Exp).then_inc(setup_act, 1)
            for s in range(NCH + 1):
                if s < NCH:
                    if s:
                        act.wait_ge(y_ready, s)
                    for m in range(8):
                        wait_full(act, "xz", s, m)
                        if m < 4:
                            ins = act.activation(xp[:, m, :], bank_of("xz", s, m)[:, :], ACT.Copy)
                        else:
                            ins = act.activation(zs[:, m - 4, :], bank_of("xz", s, m)[:, :], ACT.Silu)
                        frees(ins, "xz", s, m)
                        if m == 4:
                            act.wait_ge(g_free[use_at["xz", s, 3] % 2], use_at["xz", s, 3] // 2 + 1)
                            act.sem_inc(xp_ready, 1)
                    for m in range(4):
                        wait_full(act, "dt", s, m)
                        own.did(act.activation(ee[:, m, :], bank_of("dt", s, m)[:, :], ACT.Exp, bias=col("b_dt", m)))
                        own.wait()
                        act.sem_inc(g_free[use_at["dt", s, m] % 2], 1)
                        act.sem_inc(e_ready, 1)
                    act.sem_inc(zs_ready, 1)
                    act.wait_ge(ec_ready, s + 1)
                    act.activation(lnu[:, :, :], ee[:, :, :], ACT.Ln, bias=1.0).then_inc(lnu_ready, 1)
                    act.wait_ge(dt_ready, s + 1)
                if s:
                    act.wait_ge(p_ready, s)

                def decay_of(j, u):
                    act.wait_ge(scans, 64 * s + j + 1)
                    act.activation(abar[:, u % 2, :, 1:], btc(ee[:, u % 4, :]), ACT.Identity,
                                   scale=a_coef[:, bass.ds(j, 1)], bias=1.0).then_inc(abar_ready, 1)

                def steps(i, last):
                    for u in range(8):
                        j = 8 * i + u
                        if s < NCH:
                            if not (last and u == 7):
                                decay_of(j + 1, u + 1)
                            act.wait_ge(scans, 64 * s + j + 3)
                            act.activation(hstate[:, bass.ds(j, 1), :], hh[:, u % 2, :, TC:TC + 1].rearrange("p b o -> p o b"),
                                           ACT.Copy).then_inc(h_saved, 1)
                        if s:
                            tt = 64 * (s - 1) + j
                            act.wait_ge(chain_mm, tt + 1)
                            act.wait_ge(st_copied, tt + 1)
                            act.activation(s_cur[:, u % 2, :], cbank[u % 2][:, 0:16], ACT.Tanh,
                                           scale=1.0 / GSC).then_inc(tanh_done, 1)

                act.preload_act_table_set("sigmoid_and_others")
                if s < NCH:
                    decay_of(0, 0)
                with act.Fori(0, NS // 2 - 1) as i:
                    steps(i, False)
                steps(NS // 2 - 1, True)
                if s < NCH:
                    act.wait_ge(ln_u, lncount("a", s) + 1)
                    own.did(act.activation(l1[:, :], lu[:, :], ACT.Ln))
                    own.wait()
                    act.activation(lr[:, :], l1[:, :], ACT.Exp, scale=-0.5).then_inc(ln_r, 1)
                    for m in range(KD):
                        wait_full(act, "inp", s, m)
                        own.did(act.activation(inp[:, m, :], bank_of("inp", s, m)[:, :], ACT.Identity, bias=col("bi", m)))
                        own.wait()
                        act.sem_inc(g_free[use_at["inp", s, m] % 2], 1)
                        act.sem_inc(inp_ready, 1)
                    for m in range(KD):
                        wait_full(act, "gate", s, m)
                        own.did(act.activation(gate[:, m, :], bank_of("gate", s, m)[:, :], ACT.Sigmoid, bias=col("bg", m)))
                        own.wait()
                        act.sem_inc(g_free[use_at["gate", s, m] % 2], 1)
                        act.sem_inc(gate_ready, 1)
                    for m in range(KD):
                        wait_full(act, "pp", s, m)
                        own.did(act.activation(pf[:, :, m * B:(m + 1) * B], btc(bank_of("pp", s, m)[:, :]).rearrange("p b t -> p t b"),
                                               ACT.Copy, scale=GSC))
                        own.wait()
                        act.sem_inc(g_free[use_at["pp", s, m] % 2], 1)
                        act.sem_inc(pf_ready, 1)
                if s:
                    act.wait_ge(ln_u, lncount("b", s - 1) + 1)
                    own.did(act.activation(l1[:, :], lu[:, :], ACT.Ln))
                    own.wait()
                    act.activation(lr[:, :], l1[:, :], ACT.Exp, scale=-0.5).then_inc(ln_r, 1)

            act.wait_ge(front_done, 1)
            act.activation(tg[:, :], col("gate"), ACT.Tanh).then_inc(act_set, 1)

            def inverse_root(key, b):
                act.wait_ge(b_lnu, norms.place(key, b) + 1)
                own.did(act.activation(l2b[:, :], lub[:, :], ACT.Ln))
                own.wait()
                act.activation(lrb[:, :], l2b[:, :], ACT.Exp, scale=-0.5).then_inc(b_lnr, 1)

            def ffn_in(b, h):
                pl.wait_full(act, ("xt", h), b)
                pl.frees(act.activation(w["xqT"][:, b.slot, h].rearrange("p k t -> p (k t)"), banks[4][:, 0:P].bitcast(BF16),
                                        ACT.Copy), ("xt", h))

            def ffn_gate(b, h):
                for q in range(2):
                    pl.wait_full(act, ("g", h, q), b)
                    pl.frees(act.activation(w["sg"][:, h, q * 512:(q + 1) * 512], banks[q][:, :], ACT.Silu,
                                            scale=qv[:, b.slot, 4, h:h + 1]), ("g", h, q))

            def ffn_hidden(b, h):
                pl.wait_full(act, ("ht", h), b)
                pl.frees(act.activation(w["hqT"][:, h].rearrange("p k t -> p (k t)"), banks[5][:, :].bitcast(BF16), ACT.Copy),
                         ("ht", h))

            def ffn(b, first, last):
                ffn_gate(b, 0)
                if not first:
                    ffn_hidden(b.near(-1), 1)
                ffn_gate(b, 1)
                if not last:
                    for h in range(2):
                        ffn_in(b.near(1), h)
                if not first:
                    inverse_root("f", b.near(-1))
                ffn_hidden(b, 0)

            pl, w = plan_f, f_b
            for h in range(2):
                ffn_in(Batch(0), h)
            over_batches(act, ffn, own, per=2)
            ffn_hidden(Batch(B - 1), 1)
            act.preload_act_table_set("natural_log_exp_and_others")
            inverse_root("f", Batch(B - 1))

            def exps(b, p):
                for n in heads(p):
                    act.wait_ge(s_max, NH * b.index + n + 1)
                    if p >= 2:
                        pl.wait_full(act, ("t", n - 4), b)
                    elif b.offset:
                        pl.wait_full(act, ("t", n + NH - 4), b.near(-1))
                    for h in range(2):
                        lo, hi = widths[h]
                        ins = act.activation(w["e"][:, n % 4, lo:hi], banks[n % 4][:, lo:hi], ACT.Exp,
                                             bias=w["nm"][:, n, h:h + 1], accum_out=w["sm"][:, n, h:h + 1])
                    pl.frees(ins, ("s", n))

            def attention(b, last, beside):
                for p in range(NP):
                    beside("early", p)
                    if p + 1 < NP:
                        exps(b, p + 1)
                    elif not last:
                        exps(b.near(1), 0)
                    beside("mid", p)
                    pl.wait_full(act, ("t", 2 * p), b)
                    pl.frees(act.activation(w["pt"][:, 2 * p % 4, 0:widths[1][1]], banks[4][:, 0:widths[1][1]], ACT.Copy),
                             ("t", 2 * p))
                    beside("late", p)

            def normalised(b, name, scale, bias, ready):
                pl.wait_full(act, "xt", b)
                for k in range(KD):
                    own.did(act.activation(w["xnT"][:, k, :], banks[7][:, k * S:(k + 1) * S], ACT.Identity,
                                           scale=col(scale, k), bias=col(bias, k)))
                own.wait()
                act.sem_inc(b_free[7], 1)
                act.sem_inc(ready, 1)

            pl, w, widths, s_max = plan_a, a_b, ((0, P), (P, 3 * P)), a_max

            def a_queries(b):
                pl.wait_full(act, "q", b)
                for m in range(KD):
                    own.did(act.activation(w["qT"][:, b.slot, m, :], banks[7][:, m * S:(m + 1) * S], ACT.Identity, scale=SOFT,
                                           bias=bq_s[:, m:m + 1]))
                own.wait()
                act.sem_inc(b_free[7], 1)
                act.sem_inc(a_q, 1)

            def a_keys(b):
                pl.wait_full(act, "k", b)
                for m in range(KD):
                    own.did(act.activation(w["kT"][:, m, :], banks[7][:, m * S:(m + 1) * S], ACT.Identity, bias=col("bk", m)))
                own.wait()
                act.sem_inc(b_free[7], 1)

            def a_masked(b, ns):
                for n in ns:
                    act.activation(w["km"][:, b.slot, n, :], w["kT"][:, n // HG, :], ACT.Copy,
                                   scale=headm[:, n % HG:n % HG + 1]).then_inc(a_km, 1)

            def a_gate(b):
                pl.wait_full(act, "ge", b)
                pl.frees(act.activation(w["gt"][:, 0, :], banks[7][:, 0:2], ACT.Exp, scale=-1.0, bias=nb_ent[:, :]), "ge")

            def a_sums(b, g):
                pl.wait_full(act, ("o", g), b)
                pl.frees(act.activation(w["oT"][:, g, :], banks[6 + g][:, 0:S], ACT.Copy), ("o", g))

            def a_body(b, first, last):
                def beside(when, p):
                    nxt, prev = b.near(1), b.near(-1)
                    if not last:
                        if (when, p) == ("early", 0):
                            inverse_root("a0", nxt)
                        if (when, p) == ("mid", 2):
                            normalised(nxt, "xt", "ln_g", "ln_b", a_xnT)
                        if (when, p) == ("early", 3):
                            a_queries(nxt)
                        if (when, p) == ("mid", 3):
                            a_keys(nxt)
                        if (when, p) == ("early", 4):
                            a_gate(nxt)
                        if when == "late" and 3 <= p < 7:
                            a_masked(nxt, range(4 * (p - 3), 4 * (p - 2)))
                    if not first:
                        if (when, p) == ("late", 0):
                            a_sums(prev, 1)
                        if (when, p) == ("late", 2):
                            inverse_root("a1", prev)
                    if (when, p) == ("late", 4):
                        a_sums(b, 0)

                attention(b, last, beside)

            b0 = Batch(0)
            inverse_root("a0", b0)
            normalised(b0, "xt", "ln_g", "ln_b", a_xnT)
            a_queries(b0)
            a_keys(b0)
            a_gate(b0)
            a_masked(b0, range(NH))
            exps(b0, 0)
            over_batches(act, a_body, own, per=16)
            a_sums(Batch(B - 1), 1)
            inverse_root("a1", Batch(B - 1))

            pl, w, widths, s_max = plan_x, x_b, ((0, S), (S, 2 * S)), x_max

            def x_keys(b, m):
                pl.wait_full(act, ("k", m), b)
                for half in range(2):
                    f = slice(64 * half, 64 * half + 64)
                    ins = act.activation(w["kz"][f, b.slot, 4 * m + half:4 * m + half + 3:2, :],
                                         banks[7][f, :].rearrange("p (a c) -> p a c", a=2), ACT.Copy)
                pl.frees(ins, ("k", m))

            def x_queries(b, m):
                pl.wait_full(act, ("q", m), b)
                pl.frees(act.activation(w["qT"][:, b.slot, 2 * m:2 * m + 2, :].rearrange("p a c -> p (a c)"), banks[7][:, :],
                                        ACT.Copy, scale=0.125), ("q", m))

            def x_sums(b, g):
                pl.wait_full(act, ("o", g), b)
                pl.frees(act.activation(w["oT"][:, 2 * g:2 * g + 2, :].rearrange("p a c -> p (a c)"), banks[6][:, :], ACT.Copy),
                         ("o", g))

            def x_body(b, first, last):
                def beside(when, p):
                    nxt, prev = b.near(1), b.near(-1)
                    if (when, p) == ("early", 0) and not last:
                        inverse_root("x0", nxt)
                    if (when, p) == ("late", 0) and not first:
                        x_sums(prev, 3)
                    if when == "late" and p in (2, 4, 6):
                        x_sums(b, p // 2 - 1)
                    if (when, p) == ("late", 3) and not first:
                        inverse_root("x1", prev)
                    key = {"mid": X_MID, "late": X_LATE}.get(when, {}).get(p)
                    if key and not last:
                        if key == "xt":
                            normalised(nxt, "xt", "gam", "bet", x_xnT)
                        elif key[0] == "k":
                            x_keys(nxt, key[1])
                        elif key[0] == "q":
                            x_queries(nxt, key[1])

                attention(b, last, beside)

            inverse_root("x0", b0)
            act.wait_ge(x_zeroed, 1)
            for m in range(4):
                x_keys(b0, m)
            normalised(b0, "xt", "gam", "bet", x_xnT)
            for m in range(4):
                x_queries(b0, m)
            exps(b0, 0)
            over_batches(act, x_body, own, per=8)
            x_sums(Batch(B - 1), 3)
            inverse_root("x1", Batch(B - 1))

            pl, w = plan_m, m_b

            def m_in(b):
                pl.wait_full(act, "xt", b)
                pl.frees(act.activation(w["xT"][:, :, :].rearrange("p k c -> p (k c)"), banks[4][:, :], ACT.Copy), "xt")

            def m_masked(b):
                for e in (0, 2):
                    pl.wait_full(act, ("xm", e), b)
                    pl.frees(act.activation(w["xmT"][:, b.slot, e].rearrange("p k c -> p (k c)"), banks[4 + e][:, :], ACT.Copy),
                             ("xm", e))

            def m_gelu(b, m):
                pl.wait_full(act, ("h", m), b)
                pl.frees(act.activation(w["hT"][:, 2 * m:2 * m + 2, :].rearrange("p a c -> p (a c)"), banks[m][:, :], ACT.Gelu),
                         ("h", m))

            def m_body(b, first, last):
                if not first:
                    pl.wait_full(act, "out", b.near(-1))
                m_gelu(b, 0)
                if not last:
                    m_in(b.near(1))
                m_gelu(b, 1)
                if not first:
                    inverse_root("m0", b.near(-1))
                m_gelu(b, 2)
                if not last:
                    m_masked(b.near(1))
                if not first:
                    inverse_root("m1", b.near(-1))
                m_gelu(b, 3)

            m_in(b0)
            m_masked(b0)
            over_batches(act, m_body, own, per=4)
            inverse_root("m0", Batch(B - 1))
            inverse_root("m1", Batch(B - 1))

        @block.vector
        def _(dve):
            own = Own(dve, dve_own)
            dve.sem_inc(scans, 2)
            dve.sem_inc(hc_ready, 5)

            def link(ins):
                own.did(ins)
                own.wait()

            dve.memset(abar[:, :, :, 0:1], 0.0).then_inc(setup_dve, 1)
            dve.memset(hstate[:, :, :], 0.0).then_inc(setup_dve, 1)
            dve.memset(s_cur[:, :, :], 0.0).then_inc(setup_dve, 1)
            dve.wait_ge(in_w, 16 * 5)
            dve.wait_ge(in_w2, 16 * 5)
            dve.wait_ge(setup_act, 1)
            link(dve.tensor_scalar(a_coef[:, :], a_coef[:, :], -1.0, None, ALU.mult))
            for d in range(ND):
                own.did(dve.tensor_scalar(d_diag[:, d, :], ident[:, :], col("Dskip", d), None, ALU.mult))
            own.did(dve.tensor_copy(identb[:, :], ident[:, :]))
            own.did(dve.tensor_copy(causal[:, :], causal_f[:, :]))
            own.did(dve.tensor_scalar(a_neg[:, :, :], a_t, -1.0, None, ALU.mult))
            link(dve.tensor_copy(a_parts[0][:, :, :], a_t))
            link(dve.tensor_tensor(ret[:, 0, :].rearrange("p (k n) -> p k n", k=2), a_t, a_parts[0][:, :, :], ALU.subtract))
            link(dve.tensor_copy(a_parts[1][:, :, :], ret[:, 0, :].rearrange("p (k n) -> p k n", k=2)))
            own.did(dve.tensor_tensor(a_parts[2][:, :, :], ret[:, 0, :].rearrange("p (k n) -> p k n", k=2),
                                      a_parts[1][:, :, :], ALU.subtract))
            own.wait()
            dve.sem_inc(setup_dve, 1)
            dve.wait_ge(in_ctx, 16)
            link(dve.tensor_tensor(kv[:, :, :], ctxT[:, :, :], ctxT[:, :, :], ALU.mult))
            for k in range(KD):
                for b in range(B):
                    own.did(dve.tensor_tensor_scan(ctxT[:, k, b * S:(b + 1) * S], col("decay", k).to_broadcast([P, S]),
                                                   kv[:, k, b * S:(b + 1) * S], 0.0, ALU.mult, ALU.add))
            own.wait()

            def norm_stats(n_ln, eps, tiles):
                for j in tiles:
                    own.did(dve.bn_stats(st6[:, j, :], res[:, j, :]))
                own.wait()
                for j in tiles:
                    own.did(dve.bn_aggr(mv[:, j, :], st6[:, j, :]))
                own.wait()
                dve.tensor_scalar(lu[:, :], mv[:, :, 1], eps, None, ALU.add).then_inc(ln_u, 1)
                dve.wait_ge(ln_u, n_ln + 1)
                dve.wait_ge(ln_r, n_ln + 1)
                link(dve.tensor_tensor(l1[:, :], lr[:, :], lr[:, :], ALU.mult))
                link(dve.scalar_tensor_tensor(l2[:, :], l1[:, :], -0.5, lu[:, :], ALU.mult, ALU.mult))
                link(dve.scalar_tensor_tensor(l1[:, :], l2[:, :], 1.5, lr[:, :], ALU.add, ALU.mult))

            for s in range(NCH + 1):
                if s < NCH:
                    wait_full(dve, "xd", s, 0)
                    if s:
                        dve.wait_ge(bc_stored, 16 * s)
                    own.did(dve.tensor_copy(xd[:, :], bank_of("xd", s, 0)[0:96, :]))
                    own.wait()
                    dve.sem_inc(g_free[use_at["xd", s, 0] % 2], 1)
                    dve.sem_inc(xd_ready, 1)
                    dve.wait_ge(e_ready, 4 * (s + 1))
                    own.did(dve.tensor_scalar(ee[:, :, :], ee[:, :, :], 2.0 ** -11, 1.0, ALU.max, ALU.min))
                    own.wait()
                    dve.sem_inc(ec_ready, 1)
                    link(dve.tensor_scalar(um[:, :, :], ee[:, :, :], 1.0, 1.0, ALU.add, ALU.subtract))
                    link(dve.reciprocal(um[:, :, :], um[:, :, :]))
                    dve.wait_ge(lnu_ready, s + 1)
                    link(dve.tensor_tensor(um[:, :, :], um[:, :, :], ee[:, :, :], ALU.mult))
                    link(dve.tensor_tensor(ee[:, :, :], um[:, :, :], lnu[:, :, :], ALU.mult))
                    link(dve.tensor_scalar(ee[:, :, :], ee[:, :, :], 0.001, 0.1, ALU.max, ALU.min))
                    own.did(dve.tensor_tensor(um[:, :, :], ee[:, :, :], xp[:, :, :], ALU.mult))
                    own.wait()
                    dve.sem_inc(dt_ready, 1)

                def drive(u):
                    own.did(dve.tensor_tensor(dbx[:, u % 2, :, 1:], btc(um[:, u % 4, :]), btc(bc[:, u // 4 % 2, 0, :]), ALU.mult))

                def steps(i, last):
                    for u in range(8):
                        j = 8 * i + u
                        if s:
                            dve.wait_ge(tanh_done, 64 * (s - 1) + j + 1)
                            g = gsc[:, bass.ds(j, 1), :].rearrange("p o c -> p (o c)")
                            own.did(dve.tensor_tensor(gsf[:, :], g, s_cur[:, (u + 1) % 2, :], ALU.mult))
                            own.did(dve.tensor_tensor(gs2[:, 0, :], g, s_cur[:, (u + 1) % 2, :], ALU.mult))
                            own.wait()
                            dve.tensor_tensor(gs2[:, 1, :], gsf[:, :], gs2[:, 0, :], ALU.subtract).then_inc(gs_ready, 1)
                        if s < NCH:
                            jj = 64 * s + j
                            dve.wait_ge(abar_ready, jj + 1)
                            dve.wait_ge(h_in, jj + 1)
                            dve.wait_ge(h_saved, jj + 1)
                            own.wait()
                            dve.tensor_tensor_scan(hh[:, u % 2].rearrange("p b t -> p (b t)"),
                                                   abar[:, u % 2].rearrange("p b t -> p (b t)"),
                                                   dbx[:, u % 2].rearrange("p b t -> p (b t)"), 0.0,
                                                   ALU.mult, ALU.add).then_inc(scans, 1)
                        if s < NCH:
                            if not (last and u == 7):
                                if u % 4 == 3:
                                    dve.wait_ge(bc_loaded[(u // 4 + 1) % 2], 16 * ((NS // 2) * s + i + 1 + (u == 7)))
                                drive(u + 1)
                            dve.wait_ge(scans, jj + 3)
                            dve.wait_ge(hc_used, jj + 1)
                            dve.tensor_tensor(btc(hc[:, u % 2, :]), hh[:, u % 2, :, 1:], btc(bc[:, u // 4, 1, :]),
                                              ALU.mult).then_inc(hc_ready, 1)

                if s < NCH:
                    dve.wait_ge(bc_loaded[0], 16 * ((NS // 2) * s + 1))
                    drive(0)
                with dve.Fori(0, NS // 2 - 1) as i:
                    own.enter(i, 8 * (2 * (s > 0) + (s < NCH)))
                    steps(i, False)
                    own.leave(NS // 2 - 1)
                steps(NS // 2 - 1, True)
                if s < NCH:
                    dve.wait_ge(hc_used, 64 * (s + 1) + 2)
                    for d in range(ND):
                        own.did(dve.tensor_tensor(zs[:, d, :], ybank[d][:, :], zs[:, d, :], ALU.mult))
                    own.wait()
                    dve.sem_inc(y_ready, 1)
                    dve.wait_ge(in_xtk[s % 2], 16 * (s // 2 + 1))
                    for j in range(4):
                        wait_full(dve, "o1", s, j)
                        own.did(dve.tensor_tensor(res[:, j, :], bank_of("o1", s, j)[:, 0:D], xtk[:, s % 2, j, :], ALU.add))
                        own.wait()
                        dve.sem_inc(g_free[use_at["o1", s, j] % 2], 1)
                    norm_stats(lncount("a", s), 1e-5, range(4))
                    for j in range(4):
                        own.did(dve.tensor_scalar(x1[:, s % 2, j, :], res[:, j, :], mv[:, j, 0:1], l1[:, j:j + 1],
                                                  ALU.subtract, ALU.mult))
                    own.wait()
                    dve.sem_inc(x1_ready, 1)
                    for k in range(KD):
                        wait_full(dve, "xt", s, k)
                        own.did(dve.tensor_tensor(btc(ret[:, k, :]), btc(bank_of("xt", s, k)[:, :]), in_chunk(ctxT[:, k, :], s), ALU.mult))
                        own.wait()
                        dve.sem_inc(g_free[use_at["xt", s, k] % 2], 1)
                        dve.sem_inc(ret_ready, 1)
                    for m in range(KD):
                        dve.wait_ge(gate_ready, KD * s + m + 1)
                        own.did(dve.scalar_tensor_tensor(ret[:, m, :], gate[:, m, :], 1.0, inp[:, m, :], ALU.subtract, ALU.mult))
                        own.did(dve.tensor_scalar(gsc[:, :, m * B:(m + 1) * B], btc(gate[:, m, :]).rearrange("p b t -> p t b"),
                                                  GSC, None, ALU.mult))
                        own.wait()
                        dve.sem_inc(om_ready, 1)
                    dve.wait_ge(pf_ready, KD * (s + 1))
                    link(dve.tensor_copy(pparts[:, :, 0, :], pf[:, :, :]))
                    link(dve.tensor_tensor(pf[:, :, :], pf[:, :, :], pparts[:, :, 0, :], ALU.subtract))
                    link(dve.tensor_copy(pparts[:, :, 1, :], pf[:, :, :]))
                    own.did(dve.tensor_tensor(pparts[:, :, 2, :], pf[:, :, :], pparts[:, :, 1, :], ALU.subtract))
                    own.wait()
                    dve.sem_inc(p_ready, 1)
                if s:
                    c = s - 1
                    for j in range(4):
                        wait_full(dve, "o2", c, j)
                        own.did(dve.tensor_tensor(res[:, j, :], bank_of("o2", c, j)[:, 0:D], x1[:, c % 2, j, :], ALU.add))
                        own.wait()
                        dve.sem_inc(g_free[use_at["o2", c, j] % 2], 1)
                    for j in range(4):
                        own.did(dve.tensor_tensor(res[:, j, :], res[:, j, :], row("bo"), ALU.add))
                    own.wait()
                    norm_stats(lncount("b", c), 1e-5, range(4))
                    if c >= 2:
                        dve.wait_ge(x2_moved[c % 2], 16 * 8 * (c // 2))
                    for j in range(4):
                        own.did(dve.tensor_scalar(x2c[:, c % 2, j, :], res[:, j, :], mv[:, j, 0:1], l1[:, j:j + 1],
                                                  ALU.subtract, ALU.mult))
                    own.wait()
                    dve.sem_inc(x2_ready, 1)

            for j in range(2):
                dve.wait_ge(x2_moved[j], 16 * 8 * NCH // 2)
            dve.wait_ge(st_copied, TC * NCH + 2)
            dve.sem_inc(front_done, 1)
            own.did(dve.memset(ones[:, :], 1.0))
            for n in range(NH):
                own.did(dve.tensor_scalar(bk_m[:, n:n + 1], headm[:, n % HG:n % HG + 1], col("bk", n // HG), None, ALU.mult))
            a0 = COLS["bq"][0]
            own.did(dve.tensor_scalar(bq_s[:, :], cols[:, a0:a0 + KD], SOFT, None, ALU.mult))
            own.did(dve.tensor_scalar(nb_ent[:, :], col("b_ent"), -1.0, None, ALU.mult))
            own.wait()
            dve.sem_inc(dve_set, 1)
            dve.wait_ge(in_b1, 16 * 4)
            for a in range(3):
                own.did(dve.tensor_reduce(wsum[:, a:a + 1], w_raw[:, a, :], AX.X, ALU.add, apply_absolute_value=True))
            own.wait()
            dve.sem_inc(w_summed, 1)
            dve.wait_ge(b_full[7], 1)
            own.did(dve.tensor_scalar(wmean[:, :], banks[7][:, 0:3], 1.0 / (D * F), TINY, ALU.mult, ALU.max))
            own.wait()
            dve.sem_inc(b_free[7], 1)
            link(dve.reciprocal(wrec[:, :], wmean[:, :]))
            for a, q in enumerate((wg_q, wu_q, wd_q)):
                qf = q[:, :, :].rearrange("p k n -> p (k n)")
                link(dve.tensor_scalar(w_raw[:, a, :], w_raw[:, a, :], wrec[:, a:a + 1], MAGIC, ALU.mult, ALU.add))
                link(dve.tensor_scalar(w_raw[:, a, :], w_raw[:, a, :], MAGIC, 1.0, ALU.subtract, ALU.min))
                link(dve.tensor_scalar(qf, w_raw[:, a, :], -1.0, None, ALU.max))
            dve.sem_inc(w_ready, 1)

            def tiles(b):
                return x_tok[:, bass.ds(2 * b.index, 2), :]

            def tile(b, h):
                return x_tok[:, bass.ds(2 * b.index + h, 1), :].rearrange("p o d -> p (o d)")

            def norm_start(key, b, src, eps):
                for h in range(2):
                    own.did(dve.bn_stats(stats6[:, h, :], src[h]))
                own.wait()
                dve.sem_inc(stats_seen, 1)
                for h in range(2):
                    own.did(dve.bn_aggr(mvb[:, h, :], stats6[:, h, :]))
                own.wait()
                dve.tensor_scalar(lub[:, :], mvb[:, :, 1], eps, None, ALU.add).then_inc(b_lnu, 1)

            def norm_end(key, b, dst, src):
                dve.wait_ge(b_lnu, norms.place(key, b) + 1)
                dve.wait_ge(b_lnr, norms.place(key, b) + 1)
                link(dve.tensor_tensor(l1b[:, :], lrb[:, :], lrb[:, :], ALU.mult))
                link(dve.scalar_tensor_tensor(l2b[:, :], l1b[:, :], -0.5, lub[:, :], ALU.mult, ALU.mult))
                link(dve.scalar_tensor_tensor(l1b[:, :], l2b[:, :], 1.5, lrb[:, :], ALU.add, ALU.mult))
                for h in range(2):
                    own.did(dve.tensor_scalar(dst[h], src[h], mvb[:, h, 0:1], l1b[:, h:h + 1], ALU.subtract, ALU.mult))
                own.wait()

            halves = lambda ap: [ap[:, h, :] for h in range(2)]
            both = lambda b: [tile(b, h) for h in range(2)]

            def quantise(src, scale, tmp, dst):
                link(dve.tensor_scalar(tmp, src, scale, MAGIC, ALU.mult, ALU.add))
                return dve.tensor_scalar(dst, tmp, MAGIC, None, ALU.subtract)

            pl, w = plan_f, f_b

            def ffn_in(b):
                q = qv[:, b.slot]
                link(dve.tensor_reduce(q[:, 0, :], tiles(b), AX.X, ALU.max, apply_absolute_value=True))
                link(dve.tensor_scalar(q[:, 1, :], q[:, 0, :], TINY, None, ALU.max))
                link(dve.reciprocal(q[:, 2, :], q[:, 1, :]))
                own.did(dve.tensor_scalar(q[:, 3, :], q[:, 2, :], 127.0, None, ALU.mult))
                own.did(dve.tensor_scalar(q[:, 4, :], q[:, 1, :], 1.0 / 127.0, wmean[:, 0:1], ALU.mult, ALU.mult))
                link(dve.tensor_scalar(q[:, 5, :], q[:, 1, :], 1.0 / 127.0, wmean[:, 1:2], ALU.mult, ALU.mult))
                for h in range(2):
                    quantise(tile(b, h), q[:, 3, h:h + 1], w["tmp"][:, h, 0:D], w["xq"][:, h, :]).then_inc(f_xq, 1)

            def ffn_hidden(b, h):
                for q in range(2):
                    c = slice(q * 512, (q + 1) * 512)
                    pl.wait_full(dve, ("u", h, q), b)
                    pl.wait_freed(dve, ("g", h, q), b)
                    pl.frees(dve.scalar_tensor_tensor(w["hv"][:, h, c], banks[2 + q][:, :], qv[:, b.slot, 5, h:h + 1],
                                                      w["sg"][:, h, c], ALU.mult, ALU.mult), ("u", h, q))
                pl.wait_freed(dve, ("u", h, 1), b)
                r = [hs[:, b.slot, a, h:h + 1] for a in range(5)]
                link(dve.tensor_reduce(r[0], w["hv"][:, h, :], AX.X, ALU.max, apply_absolute_value=True))
                link(dve.tensor_scalar(r[1], r[0], TINY, None, ALU.max))
                link(dve.reciprocal(r[2], r[1]))
                own.did(dve.tensor_scalar(r[3], r[2], 127.0, None, ALU.mult))
                link(dve.tensor_scalar(r[4], r[1], 1.0 / 127.0, wmean[:, 2:3], ALU.mult, ALU.mult))
                quantise(w["hv"][:, h, :], r[3], w["tmp"][:, h, :], w["hq"][:, h, :]).then_inc(f_hq, 1)

            def ffn_sum(b):
                for h in range(2):
                    pl.wait_full(dve, ("dn", h), b)
                    own.did(dve.scalar_tensor_tensor(resb[:, h, :], banks[6 + h][:, 0:D], hs[:, b.slot, 4, h:h + 1], tile(b, h),
                                                     ALU.mult, ALU.add))
                    own.wait()
                    dve.sem_inc(b_free[6 + h], 1)
                norm_start("f", b, halves(resb), 1e-5)

            def ffn(b, first, last):
                ffn_hidden(b, 0)
                if not last:
                    ffn_in(b.near(1))
                if not first:
                    ffn_sum(b.near(-1))
                ffn_hidden(b, 1)
                if not first:
                    norm_end("f", b.near(-1), both(b.near(-1)), halves(resb))

            ffn_in(Batch(0))
            over_batches(dve, ffn, own, per=62)
            b0, b7 = Batch(0), Batch(B - 1)
            ffn_sum(b7)
            norm_end("f", b7, both(b7), halves(resb))

            def top(b, p):
                for n in heads(p):
                    pl.wait_full(dve, ("s", n), b)
                    for h, (scores, out) in enumerate(maxima(n)):
                        ins = dve.tensor_reduce(out, scores, AX.X, ALU.max, negate=True)
                    ins.then_inc(s_max, 1)

            def attention(b, last, beside):
                for p in range(NP):
                    beside("early", p)
                    for n in heads(p):
                        pl.wait_freed(dve, ("s", n), b)
                    n2 = slice(2 * p, 2 * p + 2)
                    link(dve.reciprocal(w["rr"][:, n2, :], w["sm"][:, n2, :]))
                    for n in heads(p):
                        for h in range(2):
                            lo, hi = widths[h]
                            ins = dve.tensor_scalar(w["e"][:, n % 4, lo:hi], w["e"][:, n % 4, lo:hi], w["rr"][:, n, h:h + 1],
                                                    None, ALU.mult)
                        ins.then_inc(s_norm, 1)
                    if p + 2 < NP:
                        top(b, p + 2)
                    elif not last:
                        top(b.near(1), p + 2 - NP)
                    beside("mid", p)
                    n = 2 * p + 1
                    pl.wait_full(dve, ("t", n), b)
                    pl.frees(dve.tensor_copy(w["pt"][:, n % 4, 0:widths[1][1]], banks[5][:, 0:widths[1][1]]), ("t", n))
                    beside("late", p)

            def att_sum(b, key, bias, factor):
                pl.wait_full(dve, "out", b)
                for h in range(2):
                    own.did(dve.tensor_tensor(resb[:, h, :], banks[7][:, h * D:(h + 1) * D], row(bias), ALU.add))
                own.wait()
                dve.sem_inc(b_free[7], 1)
                for h in range(2):
                    own.did(dve.scalar_tensor_tensor(resb[:, h, :], resb[:, h, :], factor, tile(b, h), ALU.mult, ALU.add))
                own.wait()
                norm_start(key, b, halves(resb), 1e-5)

            pl, w, widths, s_max, s_norm = plan_a, a_b, ((0, P), (P, 3 * P)), a_max, a_norm

            def maxima(n):
                return [(banks[n % 4][:, lo:hi], w["nm"][:, n, h:h + 1]) for h, (lo, hi) in enumerate(widths)]

            def a_values(b):
                pl.wait_freed(dve, "ge", b)
                gt = w["gt"]
                link(dve.tensor_scalar(gt[:, 1, :], gt[:, 0, :], 1.0, None, ALU.add))
                link(dve.reciprocal(gt[:, 2, :], gt[:, 1, :]))
                own.did(dve.tensor_scalar(gt[:, 3, :], gt[:, 2, :], 0.1, 2.0, ALU.max, ALU.min))
                pl.wait_full(dve, "v", b)
                vh = [w["vm"][:, b.slot, h].rearrange("p g (j c) -> p g j c", c=P + 16)[:, :, :, 0:16] for h in range(2)]
                for h in range(2):
                    own.did(dve.tensor_tensor(vh[h], banks[6][:, h * D:(h + 1) * D].rearrange("p (g j c) -> p g j c", g=2, c=16),
                                              row("bv").rearrange("p (g j c) -> p g j c", g=2, c=16), ALU.add))
                own.wait()
                dve.sem_inc(b_free[6], 1)
                for h in range(2):
                    own.did(dve.tensor_scalar(vh[h], vh[h], gt[:, 3, h:h + 1], None, ALU.mult))
                own.wait()
                dve.sem_inc(a_v, 1)

            def a_body(b, first, last):
                def beside(when, p):
                    nxt, prev = b.near(1), b.near(-1)
                    if not last:
                        if (when, p) == ("early", 0):
                            norm_start("a0", nxt, both(nxt), 1e-6)
                        if (when, p) == ("late", 0):
                            norm_end("a0", nxt, halves(w["xn"]), both(nxt))
                            dve.sem_inc(a_xn, 1)
                        if (when, p) == ("late", 6):
                            a_values(nxt)
                    if not first:
                        if (when, p) == ("late", 1):
                            att_sum(prev, "a1", "b_out", 0.1)
                        if (when, p) == ("late", 3):
                            norm_end("a1", prev, both(prev), halves(resb))

                attention(b, last, beside)

            norm_start("a0", b0, both(b0), 1e-6)
            norm_end("a0", b0, halves(w["xn"]), both(b0))
            dve.sem_inc(a_xn, 1)
            link(dve.memset(w["vm"][:, :, :, :, :], 0.0))
            a_values(b0)
            top(b0, 0)
            top(b0, 1)
            over_batches(dve, a_body, own, per=74)
            att_sum(b7, "a1", "b_out", 0.1)
            norm_end("a1", b7, both(b7), halves(resb))

            pl, w, widths, s_max, s_norm = plan_x, x_b, ((0, S), (S, 2 * S)), x_max, x_norm

            def maxima(n):
                return [(banks[n % 4][:, :].rearrange("p (h c) -> p h c", h=2), w["nm"][:, n, :])]

            def x_values(b, m):
                pl.wait_full(dve, ("v", m), b)
                pl.frees(dve.tensor_copy(w["v"][:, b.slot, m // 2, (m % 2) * 512:(m % 2 + 1) * 512], banks[7][:, :]), ("v", m))

            def x_body(b, first, last):
                def beside(when, p):
                    nxt, prev = b.near(1), b.near(-1)
                    if not last:
                        if (when, p) == ("early", 0):
                            norm_start("x0", nxt, both(nxt), 1e-5)
                        if (when, p) == ("late", 0):
                            norm_end("x0", nxt, halves(w["xn"]), both(nxt))
                            dve.sem_inc(x_xn, 1)
                        key = {"mid": X_MID, "late": X_LATE}.get(when, {}).get(p)
                        if key and key[0] == "v":
                            x_values(nxt, key[1])
                    if not first:
                        if (when, p) == ("late", 1):
                            att_sum(prev, "x1", "b_out2", tg[:, :])
                        if (when, p) == ("late", 3):
                            norm_end("x1", prev, both(prev), halves(resb))

                attention(b, last, beside)

            norm_start("x0", b0, both(b0), 1e-5)
            norm_end("x0", b0, halves(w["xn"]), both(b0))
            dve.sem_inc(x_xn, 1)
            for slot in range(2):
                own.did(dve.memset(w["kz"][:, slot], 0.0))
            own.wait()
            dve.sem_inc(x_zeroed, 1)
            for m in range(4):
                x_values(b0, m)
            top(b0, 0)
            top(b0, 1)
            over_batches(dve, x_body, own, per=60)
            att_sum(b7, "x1", "b_out2", tg[:, :])
            norm_end("x1", b7, both(b7), halves(resb))

            pl, w = plan_m, m_b

            def m_copy(b):
                for h in range(2):
                    ins = dve.tensor_copy(w["xs"][:, h, :], tile(b, h))
                ins.then_inc(m_xs, 1)

            def m_route(b):
                mx, lg, oh = w["mx"], w["lg"], w["oh"]
                pl.wait_full(dve, "lg", b)
                own.did(dve.tensor_copy(lg[:, :, :].rearrange("p h e -> p (h e)"), banks[5][:, 0:2 * NE]))
                own.wait()
                dve.sem_inc(b_free[5], 1)
                link(dve.tensor_reduce(mx[:, 0, :], lg[:, :, :], AX.X, ALU.max))
                for h in range(2):
                    own.did(dve.tensor_scalar(oh[:, h, :], lg[:, h, :], mx[:, 0, h:h + 1], None, ALU.is_ge))
                own.wait()
                link(dve.tensor_tensor(lg[:, :, :], oh[:, :, :], prio[:, :, :], ALU.mult))
                link(dve.tensor_reduce(mx[:, 1, :], lg[:, :, :], AX.X, ALU.max))
                for h in range(2):
                    own.did(dve.tensor_scalar(oh[:, h, :], lg[:, h, :], mx[:, 1, h:h + 1], None, ALU.is_ge))
                own.wait()
                dve.wait_ge(m_xs, b.index + 1)
                for h in range(2):
                    for e in range(NE):
                        ins = dve.tensor_scalar(w["xm"][:, h, e, :], w["xs"][:, h, :], oh[:, h, e:e + 1], None, ALU.mult)
                ins.then_inc(m_oh, 1)

            def m_masked(b):
                pl.wait_full(dve, "oh", b)
                pl.frees(dve.tensor_copy(w["ohT"][0:NE, b.slot, :], banks[6][0:NE, 0:S]), "oh")
                for e in (1, 3):
                    pl.wait_full(dve, ("xm", e), b)
                    pl.frees(dve.tensor_copy(w["xmT"][:, b.slot, e].rearrange("p k c -> p (k c)"), banks[4 + e][:, :]), ("xm", e))

            def m_sum(b):
                pl.wait_full(dve, "out", b)
                for h in range(2):
                    own.did(dve.tensor_tensor(resb[:, h, :], banks[7][:, h * D:(h + 1) * D], row("bo_ffn"), ALU.add))
                own.wait()
                dve.sem_inc(b_free[7], 1)
                for h in range(2):
                    own.did(dve.tensor_tensor(resb[:, h, :], resb[:, h, :], tile(b, h), ALU.add))
                own.wait()
                norm_start("m0", b, halves(resb), 1e-12)

            def m_inner(b):
                y = halves(w["y"])
                norm_end("m0", b, y, halves(resb))
                for h in range(2):
                    own.did(dve.tensor_tensor(y[h], y[h], row("lng"), ALU.mult))
                own.wait()
                for h in range(2):
                    own.did(dve.tensor_tensor(y[h], y[h], row("lnb"), ALU.add))
                own.wait()
                for h in range(2):
                    own.did(dve.tensor_tensor(resb[:, h, :], y[h], tile(b, h), ALU.add))
                own.wait()
                norm_start("m1", b, halves(resb), 1e-5)

            def m_last(b):
                dve.wait_ge(stored, 16 * (b.index + 1))
                norm_end("m1", b, halves(w["o"]), halves(resb))
                dve.sem_inc(m_out, 1)

            def m_body(b, first, last):
                if not last:
                    m_copy(b.near(1))
                if not first:
                    m_sum(b.near(-1))
                if not last:
                    m_route(b.near(1))
                if not first:
                    m_inner(b.near(-1))
                if not last:
                    m_masked(b.near(1))
                if not first:
                    m_last(b.near(-1))

            link(dve.memset(w["ohT"][:, :, :], 0.0))
            m_copy(b0)
            m_route(b0)
            m_masked(b0)
            over_batches(dve, m_body, own, per=72)
            m_sum(b7)
            m_inner(b7)
            m_last(b7)

        @block.gpsimd
        def _(pool):
            pool.sem_inc(st_copied, 2)
            for s in range(NCH + 1):
                def carry_in(j, u):
                    pool.wait_ge(scans, 64 * s + j + 1)
                    pool.tensor_copy(dbx[:, u % 2, :, 0:1], hstate[:, bass.ds(j, 1), :].rearrange("p o b -> p b o")).then_inc(h_in, 1)

                def steps(i, last):
                    for u in range(8):
                        j = 8 * i + u
                        if s < NCH and not (last and u == 7):
                            carry_in(j + 1, u + 1)
                        if s:
                            pool.wait_ge(tanh_done, TC * (s - 1) + j + 2)
                            pool.tensor_copy(states[:, :, bass.ds(j, 1)].rearrange("p c o -> p (c o)"), s_cur[:, u % 2, :])\
                                .then_inc(st_copied, 1)

                if s > 1:
                    pool.wait_ge(x2_ready, s - 1)
                if s < NCH:
                    pool.wait_ge(setup_dve, 4)
                    pool.wait_ge(h_saved, 64 * s + 2)
                    carry_in(0, 0)
                with pool.Fori(0, NS // 2 - 1) as i:
                    steps(i, False)
                steps(NS // 2 - 1, True)
            pool.wait_ge(front_done, 1)
            pool.memset(b_1[:, :], 0.0).then_inc(pool_set, 1)

        @block.tensor
        def _(pe):
            def product(out, pairs, start=True, stop=True, skip=False):
                n = len(pairs)
                for q, (lhs, rhs) in enumerate(pairs):
                    ins = pe.matmul(out, lhs, rhs, start=start and q == 0, stop=stop and q == n - 1, skip_group_check=skip)
                return ins

            pe.sem_inc(hc_used, 2)
            pe.sem_inc(h_saved, 2)
            pe.wait_ge(in_w, 16 * 5)
            pe.wait_ge(in_w2, 16 * 5)
            for s in range(NCH + 1):
                if s < NCH:
                    pe.wait_ge(in_xT[s % 2], 16 * (s // 2 + 1))

                    def xz(m):
                        wait_free(pe, "xz", s, m)
                        fills(product(bank_of("xz", s, m)[:, :],
                                      [(w_in[:, k, m * P:(m + 1) * P], xTc[:, s % 2, k, :]) for k in range(KD)]), "xz", s, m)

                    for m in range(5):
                        xz(m)
                    wait_free(pe, "xd", s, 0)
                    pe.wait_ge(xp_ready, s + 1)
                    fills(product(bank_of("xd", s, 0)[0:96, :], [(w_xp[:, k, :], xp[:, k, :]) for k in range(ND)]), "xd", s, 0)
                    for m in range(5, 8):
                        xz(m)
                    pe.wait_ge(xd_ready, s + 1)
                    for m in range(4):
                        wait_free(pe, "dt", s, m)
                        fills(product(bank_of("dt", s, m)[:, :], [(w_dt[:, m * P:(m + 1) * P], xd[0:DTR, :])]), "dt", s, m)
                    pe.wait_ge(setup_dve, 4)
                    if s:
                        pe.wait_ge(y_ready, s)
                    for d in range(ND):
                        pe.matmul(ybank[d][:, :], d_diag[:, d, :], xp[:, d, :], start=True, stop=True)
                if s:
                    pe.wait_ge(p_ready, s)
                for j in range(2):
                    pe.wait_ge(g_free[j], sum(1 for key, n in use_at.items() if n % 2 == j and before_loop(key, s)))
                with pe.Fori(0, NS // 2) as i:
                    for u in range(8):
                        d = u % 4
                        j = 8 * i + u
                        if s:
                            cb = cbank[u % 2]
                            for q in range(3):
                                pe.matmul(cb[:, 0:16], identb[:, :], pparts[:, bass.ds(j, 1), q, :].rearrange("p o c -> p (o c)"),
                                          start=q == 0, stop=False, skip_group_check=True)
                            pe.matmul(gbank[0][:, :], identb[:, :], a_parts[0][:, :, :].rearrange("p k n -> p (k n)"),
                                      start=True, stop=True)
                            pe.wait_ge(gs_ready, 64 * (s - 1) + j + 1)
                            for m in range(KD):
                                for k in range(KD):
                                    for a, g in ((0, 0), (0, 1), (1, 0), (1, 1), (2, 0)):
                                        ins = pe.matmul(cb[:, m * B:(m + 1) * B], a_parts[a][:, k, m * P:(m + 1) * P],
                                                        gs2[:, g, k * B:(k + 1) * B], start=False,
                                                        stop=(k == KD - 1 and a == 2), skip_group_check=True)
                            ins.then_inc(chain_mm, 1)
                        if s < NCH:
                            jj = 64 * s + j
                            pe.wait_ge(hc_ready, jj + 6)
                            pe.matmul(ybank[d][:, :], ident[:, :], hc[:, u % 2, :], start=False, stop=True,
                                      skip_group_check=True).then_inc(hc_used, 1)
                if s < NCH:
                    pe.wait_ge(y_ready, s + 1)
                    for j in range(4):
                        wait_free(pe, "o1", s, j)
                        fills(product(bank_of("o1", s, j)[:, 0:D],
                                      [(zs[:, d, j * P:(j + 1) * P], w_o0[:, d, :]) for d in range(ND)]), "o1", s, j)
                    pe.wait_ge(x1_ready, s + 1)
                    for k in range(KD):
                        wait_free(pe, "xt", s, k)
                        for j in range(4):
                            ins = pe.transpose(bank_of("xt", s, k)[:, j * P:(j + 1) * P], x1[:, s % 2, j, k * P:(k + 1) * P], ident[:, :])
                        fills(ins, "xt", s, k)
                    pe.wait_ge(ret_ready, KD * (s + 1))
                    for m in range(KD):
                        wait_free(pe, "inp", s, m)
                        fills(product(bank_of("inp", s, m)[:, :],
                                      [(wi_t[:, k, m * P:(m + 1) * P], ret[:, k, :]) for k in range(KD)]), "inp", s, m)
                    pe.wait_ge(inp_ready, KD * (s + 1))
                    for m in range(KD):
                        wait_free(pe, "gate", s, m)
                        fills(product(bank_of("gate", s, m)[:, :],
                                      [(wg_t[:, k, m * P:(m + 1) * P], inp[:, k, :]) for k in range(KD)]), "gate", s, m)
                    pe.wait_ge(om_ready, KD * (s + 1))
                    for m in range(KD):
                        wait_free(pe, "pp", s, m)
                        fills(product(bank_of("pp", s, m)[:, :],
                                      [(a_neg[:, k, m * P:(m + 1) * P], ret[:, k, :]) for k in range(KD)]
                                      + [(bm_t[:, k, m * P:(m + 1) * P], inp[:, k, :]) for k in range(KD)]), "pp", s, m)
                if s:
                    c = s - 1
                    pe.wait_ge(st_copied, TC * s + 2)
                    for j in range(4):
                        wait_free(pe, "o2", c, j)
                        lhs = [states[:, k * B + 2 * j:k * B + 2 * j + 2, :].rearrange("p b t -> p (b t)") for k in range(KD)]
                        fills(product(bank_of("o2", c, j)[:, 0:D], [(lhs[k], wo_t[:, k, :]) for k in range(KD)]), "o2", c, j)

            pe.wait_ge(dve_set, 1)
            pe.wait_ge(w_summed, 1)
            product(banks[7][:, 0:3], [(ones[:, :], wsum[:, :])]).then_inc(b_full[7], 1)
            pe.wait_ge(w_ready, 1)
            b0, b7 = Batch(0), Batch(B - 1)
            pl, w = plan_f, f_b

            def ffn_in(b, h):
                pe.wait_ge(f_xq, 2 * b.index + h + 1)
                pl.wait_free(pe, ("xt", h), b)
                xt = banks[4][:, 0:P].bitcast(BF16)
                for k in range(KD):
                    ins = pe.transpose(xt[:, k * P:(k + 1) * P], w["xq"][:, h, k * P:(k + 1) * P], identb[:, :])
                pl.fills(ins, ("xt", h))

            def ffn_up(b, h):
                pl.wait_freed(pe, ("xt", h), b)
                for name, wq, bank in (("g", wg_q, 0), ("u", wu_q, 2)):
                    for q in range(2):
                        pl.wait_free(pe, (name, h, q), b)
                        pl.fills(product(banks[bank + q][:, :], [(w["xqT"][:, b.slot, h, k, :], wq[:, k, q * 512:(q + 1) * 512])
                                                                 for k in range(KD)]), (name, h, q))

            def ffn_down(b, h):
                pe.wait_ge(f_hq, 2 * b.index + h + 1)
                pl.wait_free(pe, ("ht", h), b)
                ht = banks[5][:, :].bitcast(BF16)
                for m in range(NF):
                    ins = pe.transpose(ht[:, m * P:(m + 1) * P], w["hq"][:, h, m * P:(m + 1) * P], identb[:, :])
                pl.fills(ins, ("ht", h))
                pl.wait_freed(pe, ("ht", h), b)
                pl.wait_free(pe, ("dn", h), b)
                pl.fills(product(banks[6 + h][:, 0:D], [(w["hqT"][:, h, m, :], wd_q[:, m, :]) for m in range(NF)]), ("dn", h))

            def ffn(b, first, last):
                ffn_up(b, 0)
                if not first:
                    ffn_down(b.near(-1), 1)
                ffn_up(b, 1)
                if not last:
                    for h in range(2):
                        ffn_in(b.near(1), h)
                ffn_down(b, 0)

            for h in range(2):
                ffn_in(b0, h)
            over_batches(pe, ffn)
            ffn_down(b7, 1)

            def transposed(key, bank, b, src):
                pl.wait_free(pe, key, b)
                for k in range(KD):
                    for h in range(2):
                        ins = pe.transpose(bank[:, k * S + h * P:k * S + (h + 1) * P], src[:, h, k * P:(k + 1) * P], ident[:, :])
                pl.fills(ins, key)

            def attention(b, first, last, beside):
                for p in range(NP):
                    if p + 2 < NP:
                        scores(b, p + 2)
                    elif not last:
                        scores(b.near(1), p + 2 - NP)
                    beside("mid", p)
                    transposed_weights(b, p)
                    if p:
                        weighted_values(b, p - 1)
                    elif not first:
                        weighted_values(b.near(-1), NP - 1)
                    beside("late", p)

            pe.wait_ge(in_b2, 16 * 7)
            pl, w = plan_a, a_b

            def a_project(b, key):
                if key == "xt":
                    pe.wait_ge(a_xn, b.index + 1)
                    transposed("xt", banks[7], b, w["xn"])
                    return
                xnT = w["xnT"]
                if key == "q":
                    pe.wait_ge(a_xnT, b.index + 1)
                pl.wait_free(pe, key, b)
                if key in ("q", "k"):
                    for m in range(KD):
                        c = (key == "k") * D + m * P
                        ins = product(banks[7][:, m * S:(m + 1) * S], [(w_qk[:, k, c:c + P], xnT[:, k, :]) for k in range(KD)])
                for h in range(2):
                    t = slice(h * P, (h + 1) * P)
                    if key == "v":
                        ins = product(banks[6][:, h * D:(h + 1) * D], [(xnT[:, k, t], w_v[:, k, :]) for k in range(KD)])
                    if key == "ge":
                        ins = product(banks[7][:, h:h + 1], [(xnT[:, k, t], w_ent[:, k:k + 1]) for k in range(KD)])
                pl.fills(ins, key)

            def scores(b, p):
                if p == 0:
                    pe.wait_ge(a_q, b.index + 1)
                for n in heads(p):
                    pe.wait_ge(a_km, NH * b.index + n + 1)
                    pl.wait_free(pe, ("s", n), b)
                    m, bank = n // HG, banks[n % 4]
                    for h, (lo, hi) in enumerate(((0, P), (P, 3 * P))):
                        pe.matmul(bank[:, lo:hi], w["qT"][:, b.slot, m, h * P:(h + 1) * P], w["km"][:, b.slot, n, 0:hi - lo],
                                  start=True, stop=False)
                        ins = pe.matmul(bank[:, hi - P:hi], identb[:, :], causal[:, :], start=False, stop=True)
                    pl.fills(ins, ("s", n))

            def transposed_weights(b, p):
                for n in heads(p):
                    pe.wait_ge(a_norm, NH * b.index + n + 1)
                    pl.wait_free(pe, ("t", n), b)
                    for a in range(3):
                        c = slice(a * P, (a + 1) * P)
                        ins = pe.transpose(banks[4 + n % 2][:, c], w["e"][:, n % 4, c], ident[:, :])
                    pl.fills(ins, ("t", n))

            def weighted_values(b, p):
                g = p // 4
                if p == 0:
                    pe.wait_ge(a_v, b.index + 1)
                if p % 4 == 0:
                    pl.wait_free(pe, ("o", g), b)
                for n in heads(p):
                    pl.wait_freed(pe, ("t", n), b)
                    j, bank = n % HG, banks[6 + g]
                    lhs = [w["vm"][:, b.slot, h, g, j * P:(j + 1) * P] for h in range(2)]
                    pe.matmul(bank[:, 0:S], lhs[0], w["pt"][:, n % 4, 0:S], start=j == 0, stop=False)
                    ins = pe.matmul(bank[:, P:S], lhs[1], w["pt"][:, n % 4, S:S + P], start=False, stop=j == HG - 1)
                if p % 4 == 3:
                    pl.fills(ins, ("o", g))

            def a_out(b):
                for g in range(2):
                    pl.wait_freed(pe, ("o", g), b)
                pl.wait_free(pe, "out", b)
                for h in range(2):
                    ins = product(banks[7][:, h * D:(h + 1) * D], [(w["oT"][:, k, h * P:(h + 1) * P], w_o1[:, k, :]) for k in range(KD)])
                pl.fills(ins, "out")

            def a_body(b, first, last):
                def beside(when, p):
                    key = {("mid", 2): "xt", ("late", 2): "q", ("mid", 3): "k", ("late", 3): "ge", ("mid", 5): "v"}.get((when, p))
                    if key and not last:
                        a_project(b.near(1), key)
                    if (when, p) == ("late", 1) and not first:
                        a_out(b.near(-1))

                attention(b, first, last, beside)

            for key in ("xt", "q", "k", "ge", "v"):
                a_project(b0, key)
            scores(b0, 0)
            scores(b0, 1)
            over_batches(pe, a_body)
            weighted_values(b7, NP - 1)
            a_out(b7)

            pl, w = plan_x, x_b

            def x_project(b, key):
                if key == "xt":
                    pe.wait_ge(x_xn, b.index + 1)
                    transposed("xt", banks[7], b, w["xn"])
                    return
                name, m = key
                if key == ("q", 0):
                    pe.wait_ge(x_xnT, b.index + 1)
                if key == ("k", 0):
                    pe.wait_ge(x_ctx, 16 * (b.index + 1))
                pl.wait_free(pe, key, b)
                if name == "v":
                    c, h = XI + (m % 2) * 512, m // 2
                    ins = product(banks[7][:, :], [(cT[:, k, h * P:(h + 1) * P], w_xkv[:, k, c:c + 512]) for k in range(KD)])
                else:
                    wt, src = (w_xkv, cT) if name == "k" else (w_xq, w["xnT"])
                    for a in range(2):
                        c = (2 * m + a) * P
                        ins = product(banks[7][:, a * S:(a + 1) * S], [(wt[:, k, c:c + P], src[:, k, :]) for k in range(KD)])
                pl.fills(ins, key)

            def scores(b, p):
                if p == 0:
                    pl.wait_freed(pe, ("k", 3), b)
                    pl.wait_freed(pe, ("q", 3), b)
                for n in heads(p):
                    pl.wait_free(pe, ("s", n), b)
                    for h in range(2):
                        ins = pe.matmul(banks[n % 4][:, h * S:(h + 1) * S], w["qT"][:, b.slot, p, h * P:(h + 1) * P],
                                        w["kz"][:, b.slot, n, :], start=True, stop=True)
                    pl.fills(ins, ("s", n))

            def transposed_weights(b, p):
                for n in heads(p):
                    pe.wait_ge(x_norm, NH * b.index + n + 1)
                    pl.wait_free(pe, ("t", n), b)
                    for kt in range(2):
                        for h in range(2):
                            ins = pe.transpose(banks[4 + n % 2][:, kt * S + h * P:kt * S + (h + 1) * P],
                                               w["e"][:, n % 4, h * S + kt * P:h * S + (kt + 1) * P], ident[:, :])
                    pl.fills(ins, ("t", n))

            def weighted_values(b, p):
                if p == 0:
                    pl.wait_freed(pe, ("v", 3), b)
                if p % 2 == 0:
                    pl.wait_free(pe, ("o", p // 2), b)
                for n in heads(p):
                    pl.wait_freed(pe, ("t", n), b)
                    f = slice(64 * (n % 2), 64 * (n % 2) + 64)
                    ins = product(banks[6][f, (p % 2) * S:(p % 2 + 1) * S],
                                  [(w["v"][:, b.slot, kt, n * 64:(n + 1) * 64], w["pt"][:, n % 4, kt * S:(kt + 1) * S])
                                   for kt in range(2)])
                if p % 2:
                    pl.fills(ins, ("o", p // 2))

            def x_out(b):
                pl.wait_freed(pe, ("o", NP // 2 - 1), b)
                pl.wait_free(pe, "out", b)
                for h in range(2):
                    ins = product(banks[7][:, h * D:(h + 1) * D], [(w["oT"][:, p, h * P:(h + 1) * P], w_o2[:, p, :]) for p in range(NP)])
                pl.fills(ins, "out")

            def x_body(b, first, last):
                def beside(when, p):
                    key = {"mid": X_MID, "late": X_LATE}[when].get(p)
                    if key and not last:
                        x_project(b.near(1), key)
                    if (when, p) == ("late", 1) and not first:
                        x_out(b.near(-1))

                attention(b, first, last, beside)

            for key in [("k", m) for m in range(4)] + ["xt"] + [(name, m) for name in "qv" for m in range(4)]:
                x_project(b0, key)
            scores(b0, 0)
            scores(b0, 1)
            over_batches(pe, x_body)
            weighted_values(b7, NP - 1)
            x_out(b7)

            pe.wait_ge(in_b3, 16 * 4)
            pl, w = plan_m, m_b

            def m_in(b):
                pe.wait_ge(m_xs, b.index + 1)
                transposed("xt", banks[4], b, w["xs"])

            def m_logits(b):
                pl.wait_freed(pe, "xt", b)
                pl.wait_free(pe, "lg", b)
                for h in range(2):
                    ins = product(banks[5][:, h * NE:(h + 1) * NE], [(w["xT"][:, k, h * P:(h + 1) * P], w_r[:, k, :]) for k in range(KD)])
                pl.fills(ins, "lg")

            def m_masked(b):
                pe.wait_ge(m_oh, b.index + 1)
                pl.wait_free(pe, "oh", b)
                for h in range(2):
                    ins = pe.transpose(banks[6][0:NE, h * P:(h + 1) * P], w["oh"][:, h, :], ident[:, :])
                pl.fills(ins, "oh")
                for e in range(NE):
                    transposed(("xm", e), banks[4 + e], b, w["xm"][:, :, e])

            def m_hidden(b, m):
                if m == 0:
                    for e in range(NE):
                        pl.wait_freed(pe, ("xm", e), b)
                pl.wait_free(pe, ("h", m), b)
                for a in range(2):
                    c = slice((2 * m + a) * P, (2 * m + a + 1) * P)
                    ins = product(banks[m][:, a * S:(a + 1) * S],
                                  [(w_1[:, e * KD + k, c], w["xmT"][:, b.slot, e, k, :]) for e in range(NE) for k in range(KD)]
                                  + [(b_1[:, c], w["ohT"][:, b.slot, :])])
                pl.fills(ins, ("h", m))

            def m_project(b):
                pl.wait_freed(pe, ("h", 3), b)
                pl.wait_free(pe, "out", b)
                for h in range(2):
                    ins = product(banks[7][:, h * D:(h + 1) * D], [(w["hT"][:, m, h * P:(h + 1) * P], w_o3[:, m, :]) for m in range(NF)])
                pl.fills(ins, "out")

            def m_body(b, first, last):
                m_hidden(b, 0)
                if not first:
                    m_project(b.near(-1))
                if not last:
                    m_in(b.near(1))
                m_hidden(b, 1)
                if not last:
                    m_logits(b.near(1))
                m_hidden(b, 2)
                if not last:
                    m_masked(b.near(1))
                m_hidden(b, 3)

            m_in(b0)
            m_logits(b0)
            m_masked(b0)
            over_batches(pe, m_body)
            m_project(b7)


def _layout(inp):
    import numpy as np

    f = lambda a: np.ascontiguousarray(np.asarray(a), dtype=None)

    def ktiles(w):
        k, n = w.shape
        return w.reshape(k // P, P, n).transpose(1, 0, 2)

    def fcols(v):
        return v.reshape(-1, P).T

    a = {k: np.asarray(v) for k, v in inp.items()}
    x, c = a["x"], a["ctx_1024"]
    out = {}
    out["w_in"] = ktiles(a["L0_attn_W_in"])
    out["w_xp"] = ktiles(a["L0_attn_W_xproj"])
    out["w_dt"] = a["L0_attn_W_dt"]
    out["w_o0"] = ktiles(a["L0_attn_W_out"])
    out["w_ch"] = np.stack([ktiles(a[f"L0_xattn_{n}"].T) for n in ("Wi", "Wg", "A", "Bm", "Wo")], axis=1)
    alog = a["L0_attn_A_log"].reshape(ND, P, NS).transpose(1, 2, 0).reshape(P, NS * ND)
    bqkv = a["L1_attn_b_qkv"]
    one = lambda v: np.broadcast_to(v.reshape(1, 1), (P, 1))
    out["cols"] = np.concatenate([
        fcols(a["L0_attn_b_dt"]), alog, fcols(a["L0_attn_D"]), fcols(a["L0_xattn_bi"]), fcols(a["L0_xattn_bg"]),
        fcols(np.repeat(a["L0_xattn_decay"].reshape(-1), D // 16)),
        fcols(a["L1_attn_ln_g"]), fcols(a["L1_attn_ln_b"]), fcols(bqkv[:D]), fcols(bqkv[D:2 * D]),
        fcols(a["L1_xattn_ln_gamma"]), fcols(a["L1_xattn_ln_beta"]),
        one(a["L1_attn_b_ent"]), one(a["L1_xattn_gate"])], axis=1)
    out["rows"] = np.concatenate([a["L0_xattn_bo"], a["L1_attn_b_out"], bqkv[2 * D:], a["L1_xattn_b_out"],
                                  a["L1_ffn_bo"], a["L1_ffn_ln_gamma"], a["L1_ffn_ln_beta"]]).reshape(1, -1)
    out["xT"] = x.reshape(B, NCH, TC, KD, P).transpose(4, 1, 3, 0, 2).reshape(P, NCH, KD, CC)
    out["x_tok"] = x.reshape(4, 2, NCH, TC, D).transpose(2, 1, 3, 0, 4).reshape(NCH, P, 4, D)
    out["ctxT"] = ktiles(c.reshape(T, D).T)
    out["ident"] = np.eye(P, dtype=np.float32)
    q, k = np.arange(P)[:, None], np.arange(P)[None, :]
    out["causal"] = np.where(k > q, np.float32(-1e30), np.float32(0)).astype(np.float32)
    out["w_gate"] = ktiles(a["L0_ffn_w_gate"].T)
    out["w_up"] = ktiles(a["L0_ffn_w_up"].T)
    out["w_down"] = ktiles(a["L0_ffn_w_down"].T)
    wqkv = a["L1_attn_w_qkv"].T
    out["w_qk"] = ktiles(wqkv[:, :2 * D])
    out["w_v"] = ktiles(wqkv[:, 2 * D:])
    out["w_ent"] = fcols(a["L1_attn_w_ent"])
    out["w_o1"] = ktiles(a["L1_attn_w_out"].T)
    out["w_xq"] = ktiles(a["L1_xattn_w_q"])
    out["w_xkv"] = ktiles(a["L1_xattn_w_kv"])
    out["w_o2"] = ktiles(a["L1_xattn_w_out"])
    out["w_r"] = ktiles(a["L1_ffn_W_router"])
    out["w_1"] = ktiles(a["L1_ffn_W1"].reshape(NE * D, F))
    out["b_1"] = a["L1_ffn_b1"]
    out["w_o3"] = ktiles(a["L1_ffn_Wo"])
    out["prio"] = np.broadcast_to(np.arange(NE, 0, -1, dtype=np.float32), (P, 2, NE))
    out["headm"] = (np.arange(P)[:, None] // 16 == np.arange(8)[None, :]).astype(np.float32)
    return {k: f(v) for k, v in out.items()}


def build(nc, arrays):
    dr = {n: nc.dram_tensor("in_" + n, list(a.shape), F32, kind="ExternalInput").ap() for n, a in arrays.items()}
    dr["bcd"] = nc.dram_tensor("bcd", [NCH, 32, CC], F32, kind="Internal").ap()
    dr["out"] = nc.dram_tensor("out", [B, S, D], F32, kind="ExternalOutput").ap()
    build_program(nc, dr)


def kernel(**inputs):
    import concourse.bacc as _bacc
    from concourse.bass_utils import run_bass_kernel_spmd as _run

    nc = _bacc.Bacc("TRN2", target_bir_lowering=False, num_devices=1)
    arrays = _layout(inputs)
    build(nc, arrays)
    r = _run(nc, [{"in_" + n: v for n, v in arrays.items()}], core_ids=[0])
    return r.results[0]["out"]
```

```python
from contextlib import ExitStack

import concourse.bass as bass
from concourse import mybir

P = 128
F32 = mybir.dt.float32
BF16 = mybir.dt.bfloat16
FP16 = mybir.dt.float16
ALU = mybir.AluOpType
ACT = mybir.ActivationFunctionType
AX = mybir.AxisListType

B, S, D = 8, 256, 256
T = B * S
KD = D // P
NCH = 4
TC = S // NCH
CC = B * TC
DI = 512
ND = DI // P
NS = 16
DTR = 64
NH = 16
HG = NH // 2
XI = 1024
NP = NH // 2
F = 1024
NF = F // P
NE = 4
MAGIC = 1.5 * 2.0 ** 23
TINY = 1e-5
SOFT = 2.5
GSC = 1024.0

COLS = {}
_at = 0
for _name, _n in (("b_dt", 4), ("A_log", 64), ("Dskip", 4), ("bi", 2), ("bg", 2), ("decay", 2),
                  ("ln_g", 2), ("ln_b", 2), ("bq", 2), ("bk", 2), ("gam", 2), ("bet", 2),
                  ("b_ent", 1), ("gate", 1)):
    COLS[_name] = (_at, _at + _n)
    _at += _n
NCOLS = _at
ROWS = ["bo", "b_out", "bv", "b_out2", "bo_ffn", "lng", "lnb"]


class Own:

    def __init__(self, eng, sem):
        self.eng, self.sem, self.base, self.n = eng, sem, 0, 0

    def did(self, ins):
        ins.then_inc(self.sem, 1)
        self.n += 1

    def wait(self):
        self.eng.wait_ge(self.sem, self.base + self.n)

    def enter(self, i, per):
        self.start, self.per = self.base + self.n, per
        self.base, self.n = self.start + i * per, 0

    def leave(self, count):
        assert self.n == self.per, (self.n, self.per)
        self.base, self.n = self.start + count * self.per, 0


class Batch:

    def __init__(self, offset, trip=0, looped=False):
        self.offset, self.trip, self.looped = offset, trip, looped
        self.index = offset + 2 * trip
        self.slot = offset % 2

    def near(self, delta):
        return Batch(self.offset + delta, self.trip, self.looped)


class Order:

    def __init__(self, base, sequence):
        self.places = {item: base + n for n, item in enumerate(sequence)}
        self.end = base + len(sequence)

    def place(self, key, b):
        at = self.places[key, b.offset]
        if b.looped:
            step = self.places[key, b.offset + 2] - at
            assert self.places[key, b.offset + 4] == at + 2 * step
            at = at + b.trip * step
        return at


class Plan:

    def __init__(self, full, free, base, uses):
        self.full, self.free = full, free
        self.bank = {key: bank for key, _, bank in uses}
        self.orders = [Order(base[n], [(key, b) for key, b, bank in uses if bank == n]) for n in range(8)]
        self.end = [order.end for order in self.orders]

    def count(self, key, b):
        return self.orders[self.bank[key]].place(key, b)

    def wait_full(self, eng, key, b):
        eng.wait_ge(self.full[self.bank[key]], self.count(key, b) + 1)

    def wait_free(self, eng, key, b):
        eng.wait_ge(self.free[self.bank[key]], self.count(key, b) + 1)

    def wait_freed(self, eng, key, b):
        eng.wait_ge(self.free[self.bank[key]], self.count(key, b) + 2)

    def fills(self, ins, key):
        ins.then_inc(self.full[self.bank[key]], 1)

    def frees(self, ins, key):
        ins.then_inc(self.free[self.bank[key]], 1)


def over_batches(eng, body, own=None, per=0):
    body(Batch(0), True, False)
    with eng.Fori(0, B // 2 - 1) as j:
        if own:
            own.enter(j, per)
        body(Batch(1, j, True), False, False)
        body(Batch(2, j, True), False, False)
        if own:
            own.leave(B // 2 - 1)
    body(Batch(B - 1), False, True)


def build_program(nc, dr):
    ctx = ExitStack()
    with ctx:
        def sb(name, shape, dt=F32):
            return ctx.enter_context(nc.sbuf_tensor(name, shape, dt))

        def ps(name, shape, dt=F32):
            return ctx.enter_context(nc.psum_tensor(name, shape, dt))

        def sem(name):
            return ctx.enter_context(nc.semaphore(name))

        cols = sb("cols", [P, NCOLS])
        rows = sb("rows", [P, len(ROWS), D])
        ident = sb("ident", [P, P])
        identb = sb("identb", [P, P], BF16)
        causal = sb("causal", [P, P], BF16)
        headm = sb("headm", [P, 8])
        x_tok = sb("x_tok", [P, 16, D])

        ones = sb("ones", [P, P])
        prio = sb("prio", [P, 2, NE])
        wsum = sb("wsum", [P, 3])
        wmean = sb("wmean", [P, 3])
        wrec = sb("wrec", [P, 3])
        bq_s = sb("bq_s", [P, KD])
        tg = sb("tg", [P, 1])
        nb_ent = sb("nb_ent", [P, 1])
        n_magic = sb("n_magic", [P, 1])
        wpart = sb("wpart", [P, 3, NS // 2])

        def col(name, j=0):
            a = COLS[name][0]
            return cols[:, a + j:a + j + 1]

        def row(name):
            return rows[:, ROWS.index(name), :]

        front = ExitStack()
        fsb = lambda name, shape, dt=F32: front.enter_context(nc.sbuf_tensor(name, shape, dt))
        w_ch = fsb("w_ch", [P, 5, KD, D])
        work4 = fsb("work4", [P, 4, KD * CC])
        pparts = fsb("pparts", [P, TC, 3, KD * B], BF16)
        states = fsb("states", [P, KD * B, TC])
        s_cur = fsb("s_cur", [P, 2, KD * B])
        gsf = fsb("gsf", [P, KD * B])
        gs2 = fsb("gs2", [P, 2, KD * B], FP16)
        x1 = fsb("x1", [P, 2, 4, D])
        res = fsb("res", [P, 4, D])
        x2c = fsb("x2c", [P, 2, 4, D])
        st6 = fsb("st6", [P, 4, 6])
        mv = fsb("mv", [P, 4, 2])
        lu = fsb("lu", [P, 4])
        lr = fsb("lr", [P, 4])
        l1 = fsb("l1", [P, 4])
        l2 = fsb("l2", [P, 4])
        a_parts = [fsb(f"a_part{j}", [P, KD, D], BF16) for j in range(3)]
        kv = work4[:, :, :].rearrange("p (k a) c -> p k (a c)", k=KD)
        ret = work4[:, 0, :].rearrange("p (k c) -> p k c", k=KD)
        inp = work4[:, 1, :].rearrange("p (k c) -> p k c", k=KD)
        gate = work4[:, 2, :].rearrange("p (k c) -> p k c", k=KD)
        gsc = work4[:, 3, :].rearrange("p (t c) -> p t c", t=TC)
        wi_t, wg_t, a_t, bm_t, wo_t = (w_ch[:, j] for j in range(5))
        w_in = fsb("w_in", [P, KD, 2 * DI])
        w_xp = fsb("w_xp", [P, ND, 96])
        w_dt = fsb("w_dt", [DTR, DI])
        w_o0 = fsb("w_o0", [P, ND, D])
        a_neg = fsb("a_neg", [P, KD, D])
        a_coef = fsb("a_coef", [P, NS * ND])
        d_diag = fsb("d_diag", [P, ND, P])
        causal_f = fsb("causal_f", [P, P])
        ctxT = fsb("ctxT", [P, KD, T])
        xTc = fsb("xTc", [P, 2, KD, CC])
        xtk = fsb("xtk", [P, 2, 4, D])
        xp = fsb("xp", [P, ND, CC])
        zs = fsb("zs", [P, ND, CC])
        xd = fsb("xd", [96, CC])
        ee = fsb("ee", [P, ND, CC])
        um = fsb("um", [P, ND, CC])
        bc = fsb("bc", [P, 2, 2, CC])
        abar = fsb("abar", [P, 2, B, TC + 1])
        dbx = fsb("dbx", [P, 2, B, TC + 1])
        scan_out = fsb("scan_out", [P, 2 * B * (TC + 1) + 2 * CC])
        hh = scan_out[:, 0:2 * B * (TC + 1)].rearrange("p (a b t) -> p a b t", a=2, b=B)
        hc = scan_out[:, 2 * B * (TC + 1):].rearrange("p (a c) -> p a c", a=2)
        lnu = scan_out[:, 0:ND * CC].rearrange("p (d c) -> p d c", d=ND)
        hstate = fsb("hstate", [P, NS * ND, B])
        pf = fsb("pf", [P, TC, KD * B])

        front.close()

        cT = sb("cT", [P, KD, S])
        w_qk = sb("w_qk", [P, KD, 2 * D])
        w_v = sb("w_v", [P, KD, D])
        w_ent = sb("w_ent", [P, KD])
        w_o1 = sb("w_o1", [P, KD, D])
        w_xq = sb("w_xq", [P, KD, XI])
        w_xkv = sb("w_xkv", [P, KD, 2 * XI])
        w_o2 = sb("w_o2", [P, NP, D])
        b_1 = sb("b_1", [P, F])
        w_o3 = sb("w_o3", [P, NF, D])
        w_r = sb("w_r", [P, KD, NE])
        stats6 = sb("stats6", [P, 2, 6])
        mvb = sb("mvb", [P, 2, 2])
        lub = sb("lub", [P, 2])
        lrb = sb("lrb", [P, 2])
        l1b = sb("l1b", [P, 2])
        l2b = sb("l2b", [P, 2])
        resb = sb("resb", [P, 2, D])
        qv = sb("qv", [P, 2, 6, 2])
        hs = sb("hs", [P, 2, 5, 2])

        w_1 = sb("w_1", [P, NE * KD, F])
        w_raw = w_1[:, 2:8, :].rearrange("p (a k) n -> p a (k n)", a=3)

        def work(fn):
            with ExitStack() as region:
                return fn(lambda name, shape, dt=F32: region.enter_context(nc.sbuf_tensor(name, shape, dt)))

        f_b = work(lambda w: dict(xtmp=w("f_xtmp", [P, 2, D]), wg_q=w("wg_q", [P, KD, F], BF16), wu_q=w("wu_q", [P, KD, F], BF16), wd_q=w("wd_q", [P, NF, D], BF16),
                                  tmp=w("f_tmp", [P, 2, F]), xq=w("f_xq", [P, 2, D], BF16), xqT=w("f_xqT", [P, 2, 2, KD, P], BF16),
                                  sg=w("f_sg", [P, 2, F]), hv=w("f_hv", [P, 2, F]), hq=w("f_hq", [P, 2, F], BF16),
                                  hqT=w("f_hqT", [P, 2, NF, P], BF16)))
        a_b = work(lambda w: dict(xn=w("a_xn", [P, 2, D]), xnT=w("a_xnT", [P, KD, S]), qT=w("a_qT", [P, 2, KD, S]), kT=w("a_kT", [P, KD, S]),
                                  km=w("a_km", [P, 2, NH, S]), vm=w("a_vm", [P, 2, 2, 2, HG * (P + 16)]), nm=w("a_nm", [P, NH, 2]),
                                  sm=w("a_sm", [P, NH, 2]), rr=w("a_rr", [P, NH, 2]), e=w("a_e", [P, 4, 384]),
                                  pt=w("a_pt", [P, 4, 384]), oT=w("a_oT", [P, KD, S]), gt=w("a_gt", [P, 4, 2])))
        x_b = work(lambda w: dict(xn=w("x_xn", [P, 2, D]), xnT=w("x_xnT", [P, KD, S]), 
                                  qT=w("x_qT", [P, 2, NP, S]), kz=w("x_kz", [P, 2, NH, S]), v=w("x_v", [P, 2, 2, XI]),
                                  nm=w("x_nm", [P, NH, 2]), sm=w("x_sm", [P, NH, 2]), rr=w("x_rr", [P, NH, 2]),
                                  e=w("x_e", [P, 4, 2 * S]), pt=w("x_pt", [P, 4, 2 * S]), oT=w("x_oT", [P, NP, S])))
        wg_q, wu_q, wd_q = (f_b[n] for n in ("wg_q", "wu_q", "wd_q"))
        m_b = work(lambda w: dict(xs=w("m_xs", [P, 2, D]), xT=w("m_xT", [P, KD, S]), lg=w("m_lg", [P, 2, NE]),
                                  oh=w("m_oh", [P, 2, NE]), mx=w("m_mx", [P, 4, 2]), xm=w("m_xm", [P, 2, NE, D]),
                                  xmT=w("m_xmT", [P, 2, NE, KD, S]), ohT=w("m_ohT", [P, 2, S], BF16), oh3=w("m_oh3", [P, 2, P]),
                                  b1p=w("m_b1p", [P, F], BF16), b1r=w("m_b1r", [P, F]), hT=w("m_hT", [P, NF, S]),
                                  y=w("m_y", [P, 2, D]), o=w("m_o", [P, 2, D])))

        ybank = [ps(f"ybank{d}", [P, 512]) for d in range(4)]
        cbank = [ps(f"cbank{j}", [P, 512]) for j in range(2)]
        gbank = [ps(f"gbank{j}", [P, 512]) for j in range(2)]
        banks = ybank + cbank + gbank

        in_w = sem("in_w")
        in_w2 = sem("in_w2")
        in_ctx = sem("in_ctx")
        in_xT = [sem(f"in_xT{j}") for j in range(2)]
        in_xtk = [sem(f"in_xtk{j}") for j in range(2)]
        setup_dve = sem("setup_dve")
        setup_act = sem("setup_act")
        dve_own = sem("dve_own")
        act_own = sem("act_own")
        g_full = [sem(f"g_full{j}") for j in range(2)]
        g_free = [sem(f"g_free{j}") for j in range(2)]
        xd_ready = sem("xd_ready")
        xp_ready = sem("xp_ready")
        zs_ready = sem("zs_ready")
        bc_stored = sem("bc_stored")
        bc_loaded = [sem(f"bc_loaded{j}") for j in range(2)]
        e_ready = sem("e_ready")
        ec_ready = sem("ec_ready")
        lnu_ready = sem("lnu_ready")
        dt_ready = sem("dt_ready")
        abar_ready = sem("abar_ready")
        scans = sem("scans")
        scan_seen = sem("scan_seen")
        h_saved = sem("h_saved")
        hc_ready = sem("hc_ready")
        h_in = sem("h_in")
        hc_used = sem("hc_used")
        gs_first = sem("gs_first")
        gs_ready = sem("gs_ready")
        chain_mm = sem("chain_mm")
        tanh_done = sem("tanh_done")
        y_ready = sem("y_ready")
        ln_u = sem("ln_u")
        ln_r = sem("ln_r")
        x1_ready = sem("x1_ready")
        ret_ready = sem("ret_ready")
        inp_ready = sem("inp_ready")
        gate_ready = sem("gate_ready")
        om_ready = sem("om_ready")
        pp_full = sem("pp_full")
        pf_ready = sem("pf_ready")
        p_ready = sem("p_ready")
        st_copied = sem("st_copied")
        x2_ready = sem("x2_ready")
        x2_moved = [sem(f"x2_moved{j}") for j in range(2)]
        b_full = [sem(f"b_full{j}") for j in range(8)]
        b_free = [sem(f"b_free{j}") for j in range(8)]
        in_b1 = sem("in_b1")
        in_b2 = sem("in_b2")
        in_b3 = sem("in_b3")
        front_done = sem("front_done")
        w_summed = sem("w_summed")
        w_ready = sem("w_ready")
        act_set = sem("act_set")
        dve_set = sem("dve_set")
        pool_set = sem("pool_set")
        stats_seen = sem("stats_seen")
        b_lnu = sem("b_lnu")
        b_lnr = sem("b_lnr")
        f_xrounded = sem("f_xrounded")
        f_rounded = sem("f_rounded")
        f_xq = sem("f_xq")
        f_hq = sem("f_hq")
        a_xn = sem("a_xn")
        a_xnT = sem("a_xnT")
        a_q = sem("a_q")
        a_km = sem("a_km")
        a_v = sem("a_v")
        x_zeroed = sem("x_zeroed")
        a_max = sem("a_max")
        a_norm = sem("a_norm")
        x_xn = sem("x_xn")
        x_xnT = sem("x_xnT")
        x_ctx = sem("x_ctx")
        x_max = sem("x_max")
        x_norm = sem("x_norm")
        m_xs = sem("m_xs")
        m_oh = sem("m_oh")
        m_bias = sem("m_bias")
        m_out = sem("m_out")
        stored = sem("stored")

        uses = [("xz", 0, m) for m in range(4)] + [("xd", 0, 0)] + [("dt", 0, m) for m in range(4)]
        uses += [("xz", 0, m) for m in range(4, 8)]
        for s in range(NCH):
            nxt = s + 1 < NCH
            uses += [("xz", s + 1, m) for m in range(4)] * nxt + [("o1", s, j) for j in range(4)]
            uses += ([("xd", s + 1, 0)] + [("dt", s + 1, m) for m in range(4)]) * nxt
            uses += [("xt", s, k) for k in range(KD)]
            uses += [("o2", s - 1, j) for j in range(2)] * (s > 0) + [("inp", s, m) for m in range(KD)]
            uses += [("o2", s - 1, j) for j in range(2, 4)] * (s > 0) + [("gate", s, m) for m in range(KD)]
            uses += [("xz", s + 1, m) for m in range(4, 6)] * nxt
            uses += [("xz", s + 1, m) for m in range(6, 8)] * nxt
        uses += [("o2", NCH - 1, j) for j in range(4)]
        use_at = {key: n for n, key in enumerate(uses)}

        def before_loop(key, s):
            what, c, _ = key
            return c < s - (what == "o2") or (c == s and what in ("xz", "xd", "dt"))

        def bank_of(*key):
            return gbank[use_at[key] % 2]

        def wait_full(eng, *key):
            n = use_at[key]
            eng.wait_ge(g_full[n % 2], n // 2 + 1)

        def wait_free(eng, *key):
            n = use_at[key]
            if n >= 2:
                eng.wait_ge(g_free[n % 2], n // 2)

        def fills(ins, *key):
            ins.then_inc(g_full[use_at[key] % 2], 1)

        def frees(ins, *key):
            ins.then_inc(g_free[use_at[key] % 2], 1)

        def btc(ap):
            return ap.rearrange("p (b t) -> p b t", b=B)

        def in_chunk(ap, s):
            return ap.rearrange("p (b c t) -> p c b t", b=B, c=NCH)[:, s]

        def lncount(kind, s):
            order = []
            for q in range(NCH + 1):
                order += [("a", q)] * (q < NCH) + [("b", q - 1)] * (q > 0)
            return order.index((kind, s))

        def staged(before, body, after):
            return ([(key, b, bank) for key, b, bank in before]
                    + [(key, b + d, bank) for b in range(B) for key, d, bank in body if 0 <= b + d < B]
                    + [(key, b, bank) for key, b, bank in after])

        pro = [(("xt", h), 0, 4) for h in range(2)]
        gu = lambda h: [(("g", h, 0), 0, 0), (("g", h, 1), 0, 1), (("u", h, 0), 0, 2), (("u", h, 1), 0, 3)]
        down = lambda h, d: [(("ht", h), d, 5), (("dn", h), d, 6 + h)]
        plan_f = Plan(b_full, b_free, [0] * 4 + [1] + [0] * 3, staged(
            pro, gu(0) + down(1, -1) + gu(1) + [(("xt", h), 1, 4) for h in range(2)] + down(0, 0),
            [(key, B - 1, bank) for key, _, bank in down(1, 0)]))
        heads = lambda p: (2 * p, 2 * p + 1)

        def attention_uses(mid, late, sums):
            body = []
            for p in range(NP):
                body += [(("s", n % NH), n // NH, n % 4) for n in heads(p + 2)]
                body += mid.get(p, [])
                body += [(("t", n), 0, 4 + n % 2) for n in heads(p)]
                body += [(("o", g), 0, bank) for first, g, bank in sums if p - 1 == first]
                body += late.get(p, [])
            return body

        first_scores = [(("s", n), 0, n) for n in range(4)]
        plan_a = Plan(b_full, b_free, plan_f.end, staged(
            [("xt", 0, 7), ("q", 0, 7), ("k", 0, 7), ("ge", 0, 7), ("v", 0, 6)] + first_scores,
            attention_uses({2: [("xt", 1, 7)], 3: [("k", 1, 7)], 5: [("v", 1, 6)]},
                           {1: [("out", -1, 7)], 2: [("q", 1, 7)], 3: [("ge", 1, 7)]}, ((0, 0, 6), (4, 1, 7))),
            [("out", B - 1, 7)]))
        X_MID = {0: ("k", 0), 1: ("k", 2), 2: ("k", 3), 3: ("q", 0), 4: ("q", 2), 5: ("v", 0), 6: ("v", 2)}
        X_LATE = {0: ("k", 1), 2: "xt", 3: ("q", 1), 4: ("q", 3), 5: ("v", 1), 6: ("v", 3)}
        plan_x = Plan(b_full, b_free, plan_a.end, staged(
            [(key, 0, 7) for key in [("k", m) for m in range(4)] + ["xt"] + [("q", m) for m in range(4)]
             + [("v", m) for m in range(4)]] + first_scores,
            attention_uses({p: [(key, 1, 7)] for p, key in X_MID.items()},
                           {**{p: [(key, 1, 7)] for p, key in X_LATE.items()}, 1: [("out", -1, 7)]},
                           [(2 * g, g, 6) for g in range(NP // 2)]),
            [("out", B - 1, 7)]))
        m_next = [("oh", 1, 7)] + [(("xm", e), 1, 4 + e) for e in range(NE)]
        plan_m = Plan(b_full, b_free, plan_x.end, staged(
            [("xt", 0, 4), ("lg", 0, 5)] + [(key, 0, bank) for key, _, bank in m_next],
            [(("h", 0), 0, 0), ("out", -1, 7), ("xt", 1, 4), (("h", 1), 0, 1), ("lg", 1, 5), (("h", 2), 0, 2)]
            + m_next + [(("h", 3), 0, 3)], [("out", B - 1, 7)]))

        steps_of = lambda *body: [(key, b + d) for b in range(B) for key, d in body if 0 <= b + d < B]
        norms = Order(0, steps_of(("f", -1)) + [("f", B - 1), ("a0", 0)] + steps_of(("a0", 1), ("a1", -1))
                      + [("a1", B - 1), ("x0", 0)] + steps_of(("x0", 1), ("x1", -1)) + [("x1", B - 1)]
                      + steps_of(("m0", -1), ("m1", -1)) + [("m0", B - 1), ("m1", B - 1)])

        W8 = D * F // P // (NS // 2)
        block = ctx.enter_context(nc.Block())

        @block.sync
        def _(sp):
            sp.sem_inc(stored, 16)
            for b in range(8):
                sp.sem_inc(b_free[b], 1)
            for dst, src in ((w_in[:, :, :], dr["w_in"]), (w_xp[:, :, :], dr["w_xp"]), (w_dt[:, :], dr["w_dt"]),
                             (cols[:, :], dr["cols"]), (ident[:, :], dr["ident"])):
                sp.dma_start(dst, src).then_inc(in_w, 16)
            sp.dma_start(xTc[:, 0], dr["xT"][:, 0]).then_inc(in_xT[0], 16)
            for dst, src in ((w_o0[:, :, :], dr["w_o0"]), (w_ch[:, :, :, :], dr["w_ch"]),
                             (causal_f[:, :], dr["causal"]), (headm[:, :], dr["headm"]), (prio[:, :, :], dr["prio"]),
                             (rows[:, :, :].rearrange("p a b -> p (a b)"), dr["rows"].broadcast_to([P, len(ROWS) * D]))):
                sp.dma_start(dst, src).then_inc(in_w2, 16)
            sp.dma_start(ctxT[:, :, :], dr["ctxT"]).then_inc(in_ctx, 16)
            sp.dma_start(xtk[:, 0], dr["x_tok"][0]).then_inc(in_xtk[0], 16)

            def move_x2(c):
                sp.wait_ge(x2_ready, c + 1)
                for j in range(4):
                    for b2 in range(2):
                        sp.dma_start(x_tok[(c % 2) * TC:(c % 2 + 1) * TC, (2 * j + b2) * 2 + c // 2, :],
                                     x2c[b2 * TC:(b2 + 1) * TC, c % 2, j, :]).then_inc(x2_moved[c % 2], 16)

            for s in range(NCH + 1):
                if s < NCH:
                    if s + 1 < NCH:
                        if s:
                            sp.wait_ge(zs_ready, s)
                            sp.wait_ge(x1_ready, s)
                        sp.dma_start(xTc[:, (s + 1) % 2], dr["xT"][:, s + 1]).then_inc(in_xT[(s + 1) % 2], 16)
                        sp.dma_start(xtk[:, (s + 1) % 2], dr["x_tok"][s + 1]).then_inc(in_xtk[(s + 1) % 2], 16)
                    sp.wait_ge(xd_ready, s + 1)
                    sp.dma_start(dr["bcd"][s], xd[DTR:96, :]).then_inc(bc_stored, 16)
                    sp.wait_ge(bc_stored, 16 * (s + 1))
                    src = dr["bcd"][s].rearrange("(a n) t -> n a t", a=2)

                    def load_rows(i):
                        for u in range(2):
                            sp.wait_ge(hc_ready, 4 * (NS * s + 2 * i + u) + 1)
                            sp.dma_start(bc[:, u], src[bass.ds(2 * i + u, 1)].broadcast_to([P, 2, CC]))\
                              .then_inc(bc_loaded[u], 16)

                    load_rows(0)
                if s >= 2:
                    move_x2(s - 2)
                if s < NCH:
                    with sp.Fori(1, NS // 2) as i:
                        load_rows(i)
            sp.wait_ge(p_ready, NCH)
            for a, name in enumerate(("w_gate", "w_up", "w_down")):
                sp.dma_start(w_raw[:, a, :], dr[name].rearrange("p k n -> p (k n)")).then_inc(in_b1, 16)
            move_x2(NCH - 1)
            for j in range(2):
                sp.wait_ge(x2_moved[j], 16 * 8 * NCH // 2)
            sp.wait_ge(front_done, 1)
            for dst, name in ((w_qk, "w_qk"), (w_v, "w_v"), (w_o1, "w_o1"), (w_xq, "w_xq"), (w_xkv, "w_xkv"), (w_o2, "w_o2")):
                sp.dma_start(dst[:, :, :], dr[name]).then_inc(in_b2, 16)
            sp.dma_start(w_ent[:, :], dr["w_ent"]).then_inc(in_b2, 16)
            sp.dma_start(w_o3[:, :, :], dr["w_o3"]).then_inc(in_b3, 16)
            sp.dma_start(w_r[:, :, :], dr["w_r"]).then_inc(in_b3, 16)
            sp.wait_ge(pool_set, 1)
            for part in range(3):
                sp.dma_start(b_1[32 * part:32 * part + NE, :], dr["b_1"]).then_inc(in_b3, 16)
            sp.wait_ge(w_ready, 1)
            sp.dma_start(w_1[:, :, :], dr["w_1"]).then_inc(in_b3, 16)
            ctx_b = dr["ctxT"].rearrange("p k (b c) -> p b k c", b=B)
            sp.dma_start(cT[:, :, :], ctx_b[:, 0]).then_inc(x_ctx, 16)

            def next_context(b):
                plan_x.wait_full(sp, ("v", 3), b)
                nxt = b.near(1).index
                sp.dma_start(cT[:, :, :], ctx_b[:, bass.ds(nxt, 1)].rearrange("p o k c -> p (o k) c")).then_inc(x_ctx, 16)

            next_context(Batch(0))
            with sp.Fori(0, B // 2 - 1) as j:
                next_context(Batch(1, j, True))
                next_context(Batch(2, j, True))
            o_rows = dr["out"].rearrange("b (h p) d -> b p h d", h=2)
            with sp.Fori(0, B) as i:
                sp.wait_ge(m_out, i + 1)
                sp.dma_start(o_rows[bass.ds(i, 1)].rearrange("o p h d -> (o p) h d"), m_b["o"][:, :, :]).then_inc(stored, 16)
            sp.wait_ge(stored, 16 * (B + 1))

        @block.scalar
        def _(act):
            own = Own(act, act_own)
            act.sem_inc(tanh_done, 1)
            act.wait_ge(in_w, 16 * 5)
            a0, a1 = COLS["A_log"]
            act.activation(a_coef[:, :], cols[:, a0:a1], ACT.Exp).then_inc(setup_act, 1)

            def inputs(c):
                if c:
                    act.wait_ge(y_ready, c)
                for m in range(4):
                    wait_full(act, "xz", c, m)
                    frees(act.activation(xp[:, m, :], bank_of("xz", c, m)[:, :], ACT.Copy), "xz", c, m)
                act.wait_ge(g_free[use_at["xz", c, 3] % 2], use_at["xz", c, 3] // 2 + 1)
                act.wait_ge(g_free[use_at["xz", c, 2] % 2], use_at["xz", c, 2] // 2 + 1)
                act.sem_inc(xp_ready, 1)

            def silus(c, ms):
                for m in ms:
                    wait_full(act, "xz", c, m)
                    frees(act.activation(zs[:, m - 4, :], bank_of("xz", c, m)[:, :], ACT.Silu), "xz", c, m)
                if m == 7:
                    act.sem_inc(zs_ready, 1)

            def step_exps(c):
                for m in range(4):
                    wait_full(act, "dt", c, m)
                    own.did(act.activation(ee[:, m, :], bank_of("dt", c, m)[:, :], ACT.Exp, bias=col("b_dt", m)))
                    own.wait()
                    act.sem_inc(g_free[use_at["dt", c, m] % 2], 1)
                    act.sem_inc(e_ready, 1)

            def step_logs(c):
                for m in range(4):
                    act.wait_ge(ec_ready, 4 * c + m + 1)
                    act.activation(lnu[:, m, :], ee[:, m, :], ACT.Ln, bias=1.0).then_inc(lnu_ready, 1)

            def root(kind, c):
                act.wait_ge(ln_u, lncount(kind, c) + 1)
                own.did(act.activation(l1[:, :], lu[:, :], ACT.Ln))
                own.wait()
                act.activation(lr[:, :], l1[:, :], ACT.Exp, scale=-0.5).then_inc(ln_r, 1)

            act.preload_act_table_set("natural_log_exp_and_others")
            inputs(0)
            step_exps(0)
            step_logs(0)
            act.preload_act_table_set("silu_and_others")
            silus(0, range(4, 8))
            for s in range(NCH + 1):
                if s < NCH:
                    act.wait_ge(dt_ready, s + 1)
                if s:
                    act.wait_ge(p_ready, s)

                def decay_of(j, u):
                    act.wait_ge(scans, 64 * s + j + 1)
                    act.activation(abar[:, u % 2, :, 1:], btc(ee[:, u % 4, :]), ACT.Identity,
                                   scale=a_coef[:, bass.ds(j, 1)], bias=1.0).then_inc(abar_ready, 1)

                    act.activation(dbx[:, u % 2, :, 0:1], hstate[:, bass.ds(j, 1), :].rearrange("p o b -> p b o"),
                                   ACT.Copy).then_inc(h_in, 1)

                def steps(i, last):
                    for u in range(8):
                        j = 8 * i + u
                        if s < NCH and not (last and u == 7):
                            decay_of(j + 1, u + 1)
                        if s:
                            act.wait_ge(chain_mm, TC * (s - 1) + j + 1)
                            act.activation(s_cur[:, u % 2, :], cbank[u % 2][:, 0:16], ACT.Tanh,
                                           scale=1.0 / GSC).then_inc(tanh_done, 1)
                            act.activation(states[:, :, bass.ds(j, 1)].rearrange("p c o -> p (c o)"), cbank[u % 2][:, 0:16],
                                           ACT.Tanh, scale=1.0 / GSC).then_inc(st_copied, 1)
                        if s < NCH:
                            act.wait_ge(scans, 64 * s + j + 3)
                            act.sem_inc(scan_seen, 1)
                            act.activation(hstate[:, bass.ds(j, 1), :], hh[:, u % 2, :, TC:TC + 1].rearrange("p b o -> p o b"),
                                           ACT.Copy).then_inc(h_saved, 1)

                if s > 1:
                    act.wait_ge(x2_ready, s - 1)
                if s < NCH:
                    act.wait_ge(setup_dve, 4)
                    act.wait_ge(h_saved, 64 * s + 2)
                    decay_of(0, 0)
                with act.Fori(0, NS // 2 - 1) as i:
                    steps(i, False)
                steps(NS // 2 - 1, True)
                if s < NCH:
                    nxt = s + 1 < NCH
                    act.preload_act_table_set("natural_log_exp_and_others")
                    if nxt:
                        inputs(s + 1)
                    root("a", s)
                    if nxt:
                        step_exps(s + 1)
                    for m in range(KD):
                        wait_full(act, "inp", s, m)
                        own.did(act.activation(inp[:, m, :], bank_of("inp", s, m)[:, :], ACT.Identity, bias=col("bi", m)))
                        own.wait()
                        act.sem_inc(g_free[use_at["inp", s, m] % 2], 1)
                        act.sem_inc(inp_ready, 1)
                    if nxt:
                        step_logs(s + 1)
                    if s:
                        root("b", s - 1)
                    act.preload_act_table_set("sigmoid_and_others")
                    for m in range(KD):
                        wait_full(act, "gate", s, m)
                        own.did(act.activation(gate[:, m, :], bank_of("gate", s, m)[:, :], ACT.Sigmoid, bias=col("bg", m)))
                        own.wait()
                        act.sem_inc(g_free[use_at["gate", s, m] % 2], 1)
                        act.sem_inc(gate_ready, 1)
                    act.preload_act_table_set("silu_and_others")
                    if nxt:
                        wait_full(act, "o1", s, 3)
                        wait_full(act, "o1", s, 2)
                        silus(s + 1, (4, 5))
                    for m in range(KD):
                        act.wait_ge(pp_full, KD * s + m + 1)
                        act.activation(pf[:, :, m * B:(m + 1) * B], btc(cbank[m][:, :]).rearrange("p b t -> p t b"),
                                       ACT.Copy, scale=GSC).then_inc(pf_ready, 1)
                    if nxt:
                        silus(s + 1, (6, 7))
                else:
                    act.preload_act_table_set("natural_log_exp_and_others")
                    root("b", s - 1)

            act.wait_ge(front_done, 1)
            act.activation(tg[:, :], col("gate"), ACT.Tanh).then_inc(act_set, 1)

            def inverse_root(key, b):
                act.wait_ge(b_lnu, norms.place(key, b) + 1)
                own.did(act.activation(l2b[:, :], lub[:, :], ACT.Ln))
                own.wait()
                act.activation(lrb[:, :], l2b[:, :], ACT.Exp, scale=-0.5).then_inc(b_lnr, 1)

            def ffn_integers(b, h):
                act.wait_ge(f_rounded, 2 * b.index + h + 1)
                act.activation(w["hq"][:, h, :], w["tmp"][:, h, :], ACT.Identity, bias=n_magic[:, :]).then_inc(f_hq, 1)

            def ffn_quantised(b):
                for h in range(2):
                    act.wait_ge(f_xrounded, 2 * b.index + h + 1)
                    act.activation(w["xq"][:, h, :], w["xtmp"][:, h, :], ACT.Identity, bias=n_magic[:, :]).then_inc(f_xq, 1)

            def ffn_in(b, h):
                pl.wait_full(act, ("xt", h), b)
                pl.frees(act.activation(w["xqT"][:, b.slot, h].rearrange("p k t -> p (k t)"), banks[4][:, 0:P].bitcast(BF16),
                                        ACT.Copy), ("xt", h))

            def ffn_gate(b, h):
                for q in range(2):
                    pl.wait_full(act, ("g", h, q), b)
                    pl.frees(act.activation(w["sg"][:, h, q * 512:(q + 1) * 512], banks[q][:, :], ACT.Silu,
                                            scale=qv[:, b.slot, 4, h:h + 1]), ("g", h, q))

            def ffn_hidden(b, h):
                pl.wait_full(act, ("ht", h), b)
                pl.frees(act.activation(w["hqT"][:, h].rearrange("p k t -> p (k t)"), banks[5][:, :].bitcast(BF16), ACT.Copy),
                         ("ht", h))

            def ffn(b, first, last):
                ffn_gate(b, 0)
                if not first:
                    ffn_integers(b.near(-1), 1)
                    ffn_hidden(b.near(-1), 1)
                ffn_gate(b, 1)
                ffn_integers(b, 0)
                if not last:
                    ffn_quantised(b.near(1))
                    for h in range(2):
                        ffn_in(b.near(1), h)
                ffn_hidden(b, 0)
                if not first:
                    act.preload_act_table_set("natural_log_exp_and_others")
                    inverse_root("f", b.near(-1))
                act.preload_act_table_set("silu_and_others")

            pl, w = plan_f, f_b
            ffn_quantised(Batch(0))
            for h in range(2):
                ffn_in(Batch(0), h)
            over_batches(act, ffn, own, per=2)
            ffn_integers(Batch(B - 1), 1)
            ffn_hidden(Batch(B - 1), 1)
            act.preload_act_table_set("natural_log_exp_and_others")
            inverse_root("f", Batch(B - 1))

            def exps(b, p):
                for n in heads(p):
                    act.wait_ge(s_max, NH * b.index + n + 1)
                    if p >= 2:
                        pl.wait_full(act, ("t", n - 4), b)
                    elif b.offset:
                        pl.wait_full(act, ("t", n + NH - 4), b.near(-1))
                    for h in range(2):
                        lo, hi = widths[h]
                        ins = act.activation(w["e"][:, n % 4, lo:hi], banks[n % 4][:, lo:hi], ACT.Exp,
                                             bias=w["nm"][:, n, h:h + 1], accum_out=w["sm"][:, n, h:h + 1])
                    pl.frees(ins, ("s", n))

            def attention(b, last, beside):
                for p in range(NP):
                    beside("early", p)
                    if p + 1 < NP:
                        exps(b, p + 1)
                    elif not last:
                        exps(b.near(1), 0)
                    beside("mid", p)
                    pl.wait_full(act, ("t", 2 * p), b)
                    pl.frees(act.activation(w["pt"][:, 2 * p % 4, 0:widths[1][1]], banks[4][:, 0:widths[1][1]], ACT.Copy),
                             ("t", 2 * p))
                    beside("late", p)

            def normalised(b, name, scale, bias, ready):
                pl.wait_full(act, "xt", b)
                for k in range(KD):
                    own.did(act.activation(w["xnT"][:, k, :], banks[7][:, k * S:(k + 1) * S], ACT.Identity,
                                           scale=col(scale, k), bias=col(bias, k)))
                own.wait()
                act.sem_inc(b_free[7], 1)
                act.sem_inc(ready, 1)

            pl, w, widths, s_max = plan_a, a_b, ((0, P), (P, 3 * P)), a_max

            def a_queries(b):
                pl.wait_full(act, "q", b)
                for m in range(KD):
                    own.did(act.activation(w["qT"][:, b.slot, m, :], banks[7][:, m * S:(m + 1) * S], ACT.Identity, scale=SOFT,
                                           bias=bq_s[:, m:m + 1]))
                own.wait()
                act.sem_inc(b_free[7], 1)
                act.sem_inc(a_q, 1)

            def a_keys(b):
                pl.wait_full(act, "k", b)
                for m in range(KD):
                    own.did(act.activation(w["kT"][:, m, :], banks[7][:, m * S:(m + 1) * S], ACT.Identity, bias=col("bk", m)))
                own.wait()
                act.sem_inc(b_free[7], 1)

            def a_masked(b, ns):
                for n in ns:
                    act.activation(w["km"][:, b.slot, n, :], w["kT"][:, n // HG, :], ACT.Copy,
                                   scale=headm[:, n % HG:n % HG + 1]).then_inc(a_km, 1)

            def a_gate(b):
                pl.wait_full(act, "ge", b)
                pl.frees(act.activation(w["gt"][:, 0, :], banks[7][:, 0:2], ACT.Exp, scale=-1.0, bias=nb_ent[:, :]), "ge")

            def a_sums(b, g):
                pl.wait_full(act, ("o", g), b)
                pl.frees(act.activation(w["oT"][:, g, :], banks[6 + g][:, 0:S], ACT.Copy), ("o", g))

            def a_body(b, first, last):
                def beside(when, p):
                    nxt, prev = b.near(1), b.near(-1)
                    if not last:
                        if (when, p) == ("early", 0):
                            inverse_root("a0", nxt)
                        if (when, p) == ("mid", 2):
                            normalised(nxt, "xt", "ln_g", "ln_b", a_xnT)
                        if (when, p) == ("early", 3):
                            a_queries(nxt)
                        if (when, p) == ("mid", 3):
                            a_keys(nxt)
                        if (when, p) == ("early", 4):
                            a_gate(nxt)
                        if when == "late" and 3 <= p < 7:
                            a_masked(nxt, range(4 * (p - 3), 4 * (p - 2)))
                    if not first:
                        if (when, p) == ("late", 0):
                            a_sums(prev, 1)
                        if (when, p) == ("late", 3):
                            inverse_root("a1", prev)
                    if (when, p) == ("late", 4):
                        a_sums(b, 0)

                attention(b, last, beside)

            b0 = Batch(0)
            inverse_root("a0", b0)
            normalised(b0, "xt", "ln_g", "ln_b", a_xnT)
            a_queries(b0)
            a_keys(b0)
            a_gate(b0)
            a_masked(b0, range(NH))
            exps(b0, 0)
            over_batches(act, a_body, own, per=16)
            a_sums(Batch(B - 1), 1)
            inverse_root("a1", Batch(B - 1))

            pl, w, widths, s_max = plan_x, x_b, ((0, S), (S, 2 * S)), x_max

            def x_keys(b, m):
                pl.wait_full(act, ("k", m), b)
                for half in range(2):
                    f = slice(64 * half, 64 * half + 64)
                    ins = act.activation(w["kz"][f, b.slot, 4 * m + half:4 * m + half + 3:2, :],
                                         banks[7][f, :].rearrange("p (a c) -> p a c", a=2), ACT.Copy)
                pl.frees(ins, ("k", m))

            def x_queries(b, m):
                pl.wait_full(act, ("q", m), b)
                pl.frees(act.activation(w["qT"][:, b.slot, 2 * m:2 * m + 2, :].rearrange("p a c -> p (a c)"), banks[7][:, :],
                                        ACT.Copy, scale=0.125), ("q", m))

            def x_sums(b, g):
                pl.wait_full(act, ("o", g), b)
                pl.frees(act.activation(w["oT"][:, 2 * g:2 * g + 2, :].rearrange("p a c -> p (a c)"), banks[6][:, :], ACT.Copy),
                         ("o", g))

            def x_body(b, first, last):
                def beside(when, p):
                    nxt, prev = b.near(1), b.near(-1)
                    if (when, p) == ("early", 0) and not last:
                        inverse_root("x0", nxt)
                    if (when, p) == ("late", 0) and not first:
                        x_sums(prev, 3)
                    if when == "late" and p in (2, 4, 6):
                        x_sums(b, p // 2 - 1)
                    if (when, p) == ("late", 3) and not first:
                        inverse_root("x1", prev)
                    key = {"mid": X_MID, "late": X_LATE}.get(when, {}).get(p)
                    if key and not last:
                        if key == "xt":
                            normalised(nxt, "xt", "gam", "bet", x_xnT)
                        elif key[0] == "k":
                            x_keys(nxt, key[1])
                        elif key[0] == "q":
                            x_queries(nxt, key[1])

                attention(b, last, beside)

            inverse_root("x0", b0)
            act.wait_ge(x_zeroed, 1)
            for m in range(4):
                x_keys(b0, m)
            normalised(b0, "xt", "gam", "bet", x_xnT)
            for m in range(4):
                x_queries(b0, m)
            exps(b0, 0)
            over_batches(act, x_body, own, per=8)
            x_sums(Batch(B - 1), 3)
            inverse_root("x1", Batch(B - 1))

            pl, w = plan_m, m_b

            def m_in(b):
                pl.wait_full(act, "xt", b)
                pl.frees(act.activation(w["xT"][:, :, :].rearrange("p k c -> p (k c)"), banks[4][:, :], ACT.Copy), "xt")

            def m_masked(b):
                for e in (0, 2):
                    pl.wait_full(act, ("xm", e), b)
                    pl.frees(act.activation(w["xmT"][:, b.slot, e].rearrange("p k c -> p (k c)"), banks[4 + e][:, :], ACT.Copy),
                             ("xm", e))

            def m_gelu(b, m):
                pl.wait_full(act, ("h", m), b)
                pl.frees(act.activation(w["hT"][:, 2 * m:2 * m + 2, :].rearrange("p a c -> p (a c)"), banks[m][:, :], ACT.Gelu),
                         ("h", m))

            def m_body(b, first, last):
                if not first:
                    pl.wait_full(act, "out", b.near(-1))
                m_gelu(b, 0)
                if not last:
                    m_in(b.near(1))
                m_gelu(b, 1)
                if not first:
                    act.preload_act_table_set("natural_log_exp_and_others")
                    inverse_root("m0", b.near(-1))
                    act.preload_act_table_set("gelu_and_others")
                m_gelu(b, 2)
                if not last:
                    m_masked(b.near(1))
                if not first:
                    act.preload_act_table_set("natural_log_exp_and_others")
                    inverse_root("m1", b.near(-1))
                    act.preload_act_table_set("gelu_and_others")
                m_gelu(b, 3)

            m_in(b0)
            m_masked(b0)
            over_batches(act, m_body, own, per=4)
            inverse_root("m0", Batch(B - 1))
            inverse_root("m1", Batch(B - 1))

        @block.vector
        def _(dve):
            own = Own(dve, dve_own)
            dve.sem_inc(scans, 2)
            dve.sem_inc(hc_ready, 5)

            def link(ins):
                own.did(ins)
                own.wait()

            dve.memset(abar[:, :, :, 0:1], 0.0).then_inc(setup_dve, 1)
            dve.memset(hstate[:, :, :], 0.0).then_inc(setup_dve, 1)
            dve.memset(s_cur[:, :, :], 0.0).then_inc(setup_dve, 1)
            dve.wait_ge(in_w, 16 * 5)
            dve.wait_ge(in_w2, 16 * 6)
            dve.wait_ge(setup_act, 1)
            link(dve.tensor_scalar(a_coef[:, :], a_coef[:, :], -1.0, None, ALU.mult))
            for d in range(ND):
                own.did(dve.tensor_scalar(d_diag[:, d, :], ident[:, :], col("Dskip", d), None, ALU.mult))
            own.did(dve.tensor_copy(identb[:, :], ident[:, :]))
            own.did(dve.tensor_copy(causal[:, :], causal_f[:, :]))
            own.did(dve.tensor_scalar(a_neg[:, :, :], a_t, -1.0, None, ALU.mult))
            link(dve.tensor_copy(a_parts[0][:, :, :], a_t))
            link(dve.tensor_tensor(ret[:, 0, :].rearrange("p (k n) -> p k n", k=2), a_t, a_parts[0][:, :, :], ALU.subtract))
            link(dve.tensor_copy(a_parts[1][:, :, :], ret[:, 0, :].rearrange("p (k n) -> p k n", k=2)))
            own.did(dve.tensor_tensor(a_parts[2][:, :, :], ret[:, 0, :].rearrange("p (k n) -> p k n", k=2),
                                      a_parts[1][:, :, :], ALU.subtract))
            own.wait()
            dve.sem_inc(setup_dve, 1)
            def norm_start(eps):
                for j in range(4):
                    own.did(dve.bn_stats(st6[:, j, :], res[:, j, :]))
                own.wait()
                for j in range(4):
                    own.did(dve.bn_aggr(mv[:, j, :], st6[:, j, :]))
                own.wait()
                dve.tensor_scalar(lu[:, :], mv[:, :, 1], eps, None, ALU.add).then_inc(ln_u, 1)

            def norm_end(n_ln):
                dve.wait_ge(ln_u, n_ln + 1)
                dve.wait_ge(ln_r, n_ln + 1)
                link(dve.tensor_tensor(l1[:, :], lr[:, :], lr[:, :], ALU.mult))
                link(dve.scalar_tensor_tensor(l2[:, :], l1[:, :], -0.5, lu[:, :], ALU.mult, ALU.mult))
                link(dve.scalar_tensor_tensor(l1[:, :], l2[:, :], 1.5, lr[:, :], ALU.add, ALU.mult))

            def rows_bc(c):
                wait_full(dve, "xd", c, 0)
                if c:
                    dve.wait_ge(bc_stored, 16 * c)
                own.did(dve.tensor_copy(xd[:, :], bank_of("xd", c, 0)[0:96, :]))
                own.wait()
                dve.sem_inc(g_free[use_at["xd", c, 0] % 2], 1)
                dve.sem_inc(xd_ready, 1)

            def step_sizes(c, stage):
                for m in range(4):
                    if stage == 0:
                        dve.wait_ge(e_ready, 4 * c + m + 1)
                        own.did(dve.tensor_scalar(ee[:, m, :], ee[:, m, :], 2.0 ** -11, 1.0, ALU.max, ALU.min))
                        own.wait()
                        dve.sem_inc(ec_ready, 1)
                        link(dve.tensor_scalar(um[:, m, :], ee[:, m, :], 1.0, 1.0, ALU.add, ALU.subtract))
                        own.did(dve.tensor_tensor(um[:, m, :], ee[:, m, :], um[:, m, :], ALU.subtract))
                    else:
                        dve.wait_ge(lnu_ready, 4 * c + m + 1)
                        link(dve.tensor_tensor(ee[:, m, :], um[:, m, :], lnu[:, m, :], ALU.add))
                        link(dve.tensor_scalar(ee[:, m, :], ee[:, m, :], 0.001, 0.1, ALU.max, ALU.min))
                        own.did(dve.tensor_tensor(um[:, m, :], ee[:, m, :], xp[:, m, :], ALU.mult))
                own.wait()
                if stage:
                    dve.sem_inc(dt_ready, 1)

            def x2_sums(c, js):
                for j in js:
                    wait_full(dve, "o2", c, j)
                    own.did(dve.tensor_tensor(res[:, j, :], bank_of("o2", c, j)[:, 0:D], x1[:, c % 2, j, :], ALU.add))
                    own.wait()
                    dve.sem_inc(g_free[use_at["o2", c, j] % 2], 1)

            def x2_stats(c):
                for j in range(4):
                    own.did(dve.tensor_tensor(res[:, j, :], res[:, j, :], row("bo"), ALU.add))
                own.wait()
                norm_start(1e-5)

            def x2_norm(c):
                norm_end(lncount("b", c))
                if c >= 2:
                    dve.wait_ge(x2_moved[c % 2], 16 * 8 * (c // 2))
                for j in range(4):
                    own.did(dve.tensor_scalar(x2c[:, c % 2, j, :], res[:, j, :], mv[:, j, 0:1], l1[:, j:j + 1],
                                              ALU.subtract, ALU.mult))
                own.wait()
                dve.sem_inc(x2_ready, 1)

            def context_sum():
                dve.wait_ge(in_ctx, 16)
                link(dve.tensor_tensor(kv[:, :, :], ctxT[:, :, :], ctxT[:, :, :], ALU.mult))
                for k in range(KD):
                    for b in range(B):
                        own.did(dve.tensor_tensor_scan(ctxT[:, k, b * S:(b + 1) * S], col("decay", k).to_broadcast([P, S]),
                                                       kv[:, k, b * S:(b + 1) * S], 0.0, ALU.mult, ALU.add))
                own.wait()

            def constants():
                own.did(dve.memset(ones[:, :], 1.0))
                own.did(dve.memset(n_magic[:, :], -MAGIC))
                a0 = COLS["bq"][0]
                own.did(dve.tensor_scalar(bq_s[:, :], cols[:, a0:a0 + KD], SOFT, None, ALU.mult))
                own.did(dve.tensor_scalar(nb_ent[:, :], col("b_ent"), -1.0, None, ALU.mult))
                own.wait()
                dve.sem_inc(dve_set, 1)

            rows_bc(0)
            step_sizes(0, 0)
            step_sizes(0, 1)
            for s in range(NCH + 1):
                def second_half(tt):
                    dve.wait_ge(gs_first, tt + 1)
                    dve.tensor_tensor(gs2[:, 1, :], gsf[:, :], gs2[:, 0, :], ALU.subtract).then_inc(gs_ready, 1)

                def drive(u):
                    own.did(dve.tensor_tensor(dbx[:, u % 2, :, 1:], btc(um[:, u % 4, :]), btc(bc[:, u // 4 % 2, 0, :]), ALU.mult))

                def steps(i, last):
                    for u in range(8):
                        j = 8 * i + u
                        tt = 64 * (s - 1) + j
                        if s:
                            dve.wait_ge(tanh_done, tt + 1)
                            g = gsc[:, bass.ds(j, 1), :].rearrange("p o c -> p (o c)")
                            dve.tensor_tensor(gsf[:, :], g, s_cur[:, (u + 1) % 2, :], ALU.mult)
                            dve.tensor_tensor(gs2[:, 0, :], g, s_cur[:, (u + 1) % 2, :], ALU.mult).then_inc(gs_first, 1)
                        if s == NCH:
                            second_half(tt)
                        if s == NCH and u < 3:
                            own.did(dve.tensor_reduce(wpart[:, u, bass.ds(i, 1)], w_raw[:, u, bass.ds(W8 * i, W8)], AX.X, ALU.add,
                                                      apply_absolute_value=True))
                        if s < NCH:
                            jj = 64 * s + j
                            dve.wait_ge(abar_ready, jj + 1)
                            dve.wait_ge(h_in, jj + 1)
                            dve.wait_ge(h_saved, jj + 1)
                            own.wait()
                            dve.tensor_tensor_scan(hh[:, u % 2].rearrange("p b t -> p (b t)"),
                                                   abar[:, u % 2].rearrange("p b t -> p (b t)"),
                                                   dbx[:, u % 2].rearrange("p b t -> p (b t)"), 0.0,
                                                   ALU.mult, ALU.add).then_inc(scans, 1)
                        if 0 < s < NCH:
                            second_half(tt)
                        if s < NCH:
                            if not (last and u == 7):
                                if u % 4 == 3:
                                    dve.wait_ge(bc_loaded[(u // 4 + 1) % 2], 16 * ((NS // 2) * s + i + 1 + (u == 7)))
                                drive(u + 1)
                            dve.wait_ge(scans, jj + 3)
                            dve.wait_ge(hc_used, jj + 1)
                            dve.tensor_tensor(btc(hc[:, u % 2, :]), hh[:, u % 2, :, 1:], btc(bc[:, u // 4, 1, :]),
                                              ALU.mult).then_inc(hc_ready, 1)

                if s < NCH:
                    dve.wait_ge(bc_loaded[0], 16 * ((NS // 2) * s + 1))
                    drive(0)
                else:
                    dve.wait_ge(in_b1, 16 * 3)
                with dve.Fori(0, NS // 2 - 1) as i:
                    own.enter(i, 8 * (s < NCH) + 3 * (s == NCH))
                    steps(i, False)
                    own.leave(NS // 2 - 1)
                steps(NS // 2 - 1, True)
                if s < NCH:
                    nxt = s + 1 < NCH
                    dve.wait_ge(hc_used, 64 * (s + 1) + 2)
                    dve.wait_ge(zs_ready, s + 1)
                    for d in range(ND):
                        own.did(dve.tensor_tensor(zs[:, d, :], ybank[d][:, :], zs[:, d, :], ALU.mult))
                    own.wait()
                    dve.sem_inc(y_ready, 1)
                    if s == 0:
                        context_sum()
                    dve.wait_ge(in_xtk[s % 2], 16 * (s // 2 + 1))
                    for j in range(4):
                        wait_full(dve, "o1", s, j)
                        own.did(dve.tensor_tensor(res[:, j, :], bank_of("o1", s, j)[:, 0:D], xtk[:, s % 2, j, :], ALU.add))
                        own.wait()
                        dve.sem_inc(g_free[use_at["o1", s, j] % 2], 1)
                    norm_start(1e-5)
                    if nxt:
                        rows_bc(s + 1)
                    norm_end(lncount("a", s))
                    for j in range(4):
                        own.did(dve.tensor_scalar(x1[:, s % 2, j, :], res[:, j, :], mv[:, j, 0:1], l1[:, j:j + 1],
                                                  ALU.subtract, ALU.mult))
                    own.wait()
                    dve.sem_inc(x1_ready, 1)
                    for k in range(KD):
                        wait_full(dve, "xt", s, k)
                        own.did(dve.tensor_tensor(btc(ret[:, k, :]), btc(bank_of("xt", s, k)[:, :]), in_chunk(ctxT[:, k, :], s), ALU.mult))
                        own.wait()
                        dve.sem_inc(g_free[use_at["xt", s, k] % 2], 1)
                        dve.sem_inc(ret_ready, 1)
                    if s:
                        x2_sums(s - 1, range(2))
                    if nxt:
                        step_sizes(s + 1, 0)
                    if s:
                        x2_sums(s - 1, range(2, 4))
                        x2_stats(s - 1)
                    else:
                        constants()
                    for m in range(KD):
                        dve.wait_ge(gate_ready, KD * s + m + 1)
                        own.did(dve.scalar_tensor_tensor(ret[:, m, :], gate[:, m, :], 1.0, inp[:, m, :], ALU.subtract, ALU.mult))
                        own.wait()
                        dve.sem_inc(om_ready, 1)
                    if nxt:
                        step_sizes(s + 1, 1)
                    for m in range(KD):
                        own.did(dve.tensor_scalar(gsc[:, :, m * B:(m + 1) * B], btc(gate[:, m, :]).rearrange("p b t -> p t b"),
                                                  GSC, None, ALU.mult))
                    if s:
                        x2_norm(s - 1)
                    for m in range(KD):
                        dve.wait_ge(pf_ready, KD * s + m + 1)
                        c = slice(m * B, (m + 1) * B)
                        link(dve.tensor_copy(pparts[:, :, 0, c], pf[:, :, c]))
                        link(dve.tensor_tensor(pf[:, :, c], pf[:, :, c], pparts[:, :, 0, c], ALU.subtract))
                        link(dve.tensor_copy(pparts[:, :, 1, c], pf[:, :, c]))
                        own.did(dve.tensor_tensor(pparts[:, :, 2, c], pf[:, :, c], pparts[:, :, 1, c], ALU.subtract))
                    own.wait()
                    dve.sem_inc(p_ready, 1)
                else:
                    own.wait()
                    own.did(dve.tensor_reduce(wsum[:, :], wpart[:, :, :], AX.X, ALU.add))
                    own.wait()
                    dve.sem_inc(w_summed, 1)
                    x2_sums(s - 1, range(4))
                    x2_stats(s - 1)
                    x2_norm(s - 1)

            dve.wait_ge(b_full[4], 1)
            own.did(dve.tensor_scalar(wmean[:, :], banks[4][:, 0:3], 1.0 / (D * F), TINY, ALU.mult, ALU.max))
            own.wait()
            dve.sem_inc(b_free[4], 1)
            link(dve.reciprocal(wrec[:, :], wmean[:, :]))
            for a, q in enumerate((wg_q, wu_q, wd_q)):
                qf = q[:, :, :].rearrange("p k n -> p (k n)")
                link(dve.tensor_scalar(w_raw[:, a, :], w_raw[:, a, :], wrec[:, a:a + 1], MAGIC, ALU.mult, ALU.add))
                link(dve.tensor_scalar(w_raw[:, a, :], w_raw[:, a, :], MAGIC, 1.0, ALU.subtract, ALU.min))
                link(dve.tensor_scalar(qf, w_raw[:, a, :], -1.0, None, ALU.max))
            dve.sem_inc(w_ready, 1)
            for j in range(2):
                dve.wait_ge(x2_moved[j], 16 * 8 * NCH // 2)
            dve.wait_ge(st_copied, TC * NCH + 2)
            dve.sem_inc(front_done, 1)
            def tiles(b):
                return x_tok[:, bass.ds(2 * b.index, 2), :]

            def tile(b, h):
                return x_tok[:, bass.ds(2 * b.index + h, 1), :].rearrange("p o d -> p (o d)")

            def norm_start(key, b, src, eps):
                for h in range(2):
                    own.did(dve.bn_stats(stats6[:, h, :], src[h]))
                own.wait()
                dve.sem_inc(stats_seen, 1)
                for h in range(2):
                    own.did(dve.bn_aggr(mvb[:, h, :], stats6[:, h, :]))
                own.wait()
                dve.tensor_scalar(lub[:, :], mvb[:, :, 1], eps, None, ALU.add).then_inc(b_lnu, 1)

            def norm_end(key, b, dst, src):
                dve.wait_ge(b_lnu, norms.place(key, b) + 1)
                dve.wait_ge(b_lnr, norms.place(key, b) + 1)
                link(dve.tensor_tensor(l1b[:, :], lrb[:, :], lrb[:, :], ALU.mult))
                link(dve.scalar_tensor_tensor(l2b[:, :], l1b[:, :], -0.5, lub[:, :], ALU.mult, ALU.mult))
                link(dve.scalar_tensor_tensor(l1b[:, :], l2b[:, :], 1.5, lrb[:, :], ALU.add, ALU.mult))
                for h in range(2):
                    own.did(dve.tensor_scalar(dst[h], src[h], mvb[:, h, 0:1], l1b[:, h:h + 1], ALU.subtract, ALU.mult))
                own.wait()

            halves = lambda ap: [ap[:, h, :] for h in range(2)]
            both = lambda b: [tile(b, h) for h in range(2)]

            pl, w = plan_f, f_b

            def ffn_in(b):
                q = qv[:, b.slot]
                link(dve.tensor_reduce(q[:, 0, :], tiles(b), AX.X, ALU.max, apply_absolute_value=True))
                link(dve.tensor_scalar(q[:, 1, :], q[:, 0, :], TINY, None, ALU.max))
                link(dve.reciprocal(q[:, 2, :], q[:, 1, :]))
                own.did(dve.tensor_scalar(q[:, 3, :], q[:, 2, :], 127.0, None, ALU.mult))
                own.did(dve.tensor_scalar(q[:, 4, :], q[:, 1, :], 1.0 / 127.0, wmean[:, 0:1], ALU.mult, ALU.mult))
                link(dve.tensor_scalar(q[:, 5, :], q[:, 1, :], 1.0 / 127.0, wmean[:, 1:2], ALU.mult, ALU.mult))
                for h in range(2):
                    dve.tensor_scalar(w["xtmp"][:, h, :], tile(b, h), q[:, 3, h:h + 1], MAGIC, ALU.mult, ALU.add)\
                        .then_inc(f_xrounded, 1)

            def ffn_hidden(b, h):
                for q in range(2):
                    c = slice(q * 512, (q + 1) * 512)
                    pl.wait_full(dve, ("u", h, q), b)
                    pl.wait_freed(dve, ("g", h, q), b)
                    pl.frees(dve.scalar_tensor_tensor(w["hv"][:, h, c], banks[2 + q][:, :], qv[:, b.slot, 5, h:h + 1],
                                                      w["sg"][:, h, c], ALU.mult, ALU.mult), ("u", h, q))
                pl.wait_freed(dve, ("u", h, 1), b)
                r = [hs[:, b.slot, a, h:h + 1] for a in range(5)]
                link(dve.tensor_reduce(r[0], w["hv"][:, h, :], AX.X, ALU.max, apply_absolute_value=True))
                link(dve.tensor_scalar(r[1], r[0], TINY, None, ALU.max))
                link(dve.reciprocal(r[2], r[1]))
                own.did(dve.tensor_scalar(r[4], r[1], 1.0 / 127.0, wmean[:, 2:3], ALU.mult, ALU.mult))
                link(dve.tensor_scalar(r[3], r[2], 127.0, None, ALU.mult))
                dve.tensor_scalar(w["tmp"][:, h, :], w["hv"][:, h, :], r[3], MAGIC, ALU.mult, ALU.add).then_inc(f_rounded, 1)

            def ffn_sum(b):
                for h in range(2):
                    pl.wait_full(dve, ("dn", h), b)
                    own.did(dve.scalar_tensor_tensor(resb[:, h, :], banks[6 + h][:, 0:D], hs[:, b.slot, 4, h:h + 1], tile(b, h),
                                                     ALU.mult, ALU.add))
                    own.wait()
                    dve.sem_inc(b_free[6 + h], 1)
                norm_start("f", b, halves(resb), 1e-5)

            def ffn(b, first, last):
                ffn_hidden(b, 0)
                if not last:
                    ffn_in(b.near(1))
                if not first:
                    ffn_sum(b.near(-1))
                ffn_hidden(b, 1)
                if not first:
                    norm_end("f", b.near(-1), both(b.near(-1)), halves(resb))

            ffn_in(Batch(0))
            over_batches(dve, ffn, own, per=54)
            b0, b7 = Batch(0), Batch(B - 1)
            ffn_sum(b7)
            norm_end("f", b7, both(b7), halves(resb))

            def top(b, p):
                for n in heads(p):
                    pl.wait_full(dve, ("s", n), b)
                    for h, (scores, out) in enumerate(maxima(n)):
                        ins = dve.tensor_reduce(out, scores, AX.X, ALU.max, negate=True)
                    ins.then_inc(s_max, 1)

            def attention(b, last, beside):
                for p in range(NP):
                    beside("early", p)
                    for n in heads(p):
                        pl.wait_freed(dve, ("s", n), b)
                    n2 = slice(2 * p, 2 * p + 2)
                    link(dve.reciprocal(w["rr"][:, n2, :], w["sm"][:, n2, :]))
                    for n in heads(p):
                        for h in range(2):
                            lo, hi = widths[h]
                            ins = dve.tensor_scalar(w["e"][:, n % 4, lo:hi], w["e"][:, n % 4, lo:hi], w["rr"][:, n, h:h + 1],
                                                    None, ALU.mult)
                        ins.then_inc(s_norm, 1)
                    if p + 2 < NP:
                        top(b, p + 2)
                    elif not last:
                        top(b.near(1), p + 2 - NP)
                    beside("mid", p)
                    n = 2 * p + 1
                    pl.wait_full(dve, ("t", n), b)
                    pl.frees(dve.tensor_copy(w["pt"][:, n % 4, 0:widths[1][1]], banks[5][:, 0:widths[1][1]]), ("t", n))
                    beside("late", p)

            def att_bias(b, bias):
                pl.wait_full(dve, "out", b)
                for h in range(2):
                    own.did(dve.tensor_tensor(resb[:, h, :], banks[7][:, h * D:(h + 1) * D], row(bias), ALU.add))
                own.wait()
                dve.sem_inc(b_free[7], 1)

            def att_sum(b, key, factor):
                for h in range(2):
                    own.did(dve.scalar_tensor_tensor(resb[:, h, :], resb[:, h, :], factor, tile(b, h), ALU.mult, ALU.add))
                own.wait()
                norm_start(key, b, halves(resb), 1e-5)

            pl, w, widths, s_max, s_norm = plan_a, a_b, ((0, P), (P, 3 * P)), a_max, a_norm

            def maxima(n):
                return [(banks[n % 4][:, lo:hi], w["nm"][:, n, h:h + 1]) for h, (lo, hi) in enumerate(widths)]

            def a_values(b):
                pl.wait_freed(dve, "ge", b)
                gt = w["gt"]
                link(dve.tensor_scalar(gt[:, 1, :], gt[:, 0, :], 1.0, None, ALU.add))
                link(dve.reciprocal(gt[:, 2, :], gt[:, 1, :]))
                own.did(dve.tensor_scalar(gt[:, 3, :], gt[:, 2, :], 0.1, 2.0, ALU.max, ALU.min))
                pl.wait_full(dve, "v", b)
                vh = [w["vm"][:, b.slot, h].rearrange("p g (j c) -> p g j c", c=P + 16)[:, :, :, 0:16] for h in range(2)]
                for h in range(2):
                    own.did(dve.tensor_tensor(vh[h], banks[6][:, h * D:(h + 1) * D].rearrange("p (g j c) -> p g j c", g=2, c=16),
                                              row("bv").rearrange("p (g j c) -> p g j c", g=2, c=16), ALU.add))
                own.wait()
                dve.sem_inc(b_free[6], 1)
                for h in range(2):
                    own.did(dve.tensor_scalar(vh[h], vh[h], gt[:, 3, h:h + 1], None, ALU.mult))
                own.wait()
                dve.sem_inc(a_v, 1)

            def a_body(b, first, last):
                def beside(when, p):
                    nxt, prev = b.near(1), b.near(-1)
                    if not last:
                        if (when, p) == ("early", 0):
                            norm_start("a0", nxt, both(nxt), 1e-6)
                        if (when, p) == ("late", 0):
                            norm_end("a0", nxt, halves(w["xn"]), both(nxt))
                            dve.sem_inc(a_xn, 1)
                        if (when, p) == ("late", 6):
                            a_values(nxt)
                    if not first:
                        if (when, p) == ("late", 1):
                            att_bias(prev, "b_out")
                        if (when, p) == ("late", 2):
                            att_sum(prev, "a1", 0.1)
                        if (when, p) == ("late", 4):
                            norm_end("a1", prev, both(prev), halves(resb))

                attention(b, last, beside)

            norm_start("a0", b0, both(b0), 1e-6)
            norm_end("a0", b0, halves(w["xn"]), both(b0))
            dve.sem_inc(a_xn, 1)
            link(dve.memset(w["vm"][:, 0], 0.0))
            a_values(b0)
            top(b0, 0)
            top(b0, 1)
            own.did(dve.memset(w["vm"][:, 1], 0.0))
            over_batches(dve, a_body, own, per=74)
            att_bias(b7, "b_out")
            att_sum(b7, "a1", 0.1)

            def x_zeros(slot):
                for half in range(2):
                    own.did(dve.memset(x_b["kz"][64 * half:64 * half + 64, slot, 1 - half::2, :], 0.0))
                own.wait()
                dve.sem_inc(x_zeroed, 1)

            x_zeros(0)
            norm_end("a1", b7, both(b7), halves(resb))

            pl, w, widths, s_max, s_norm = plan_x, x_b, ((0, S), (S, 2 * S)), x_max, x_norm

            def maxima(n):
                return [(banks[n % 4][:, :].rearrange("p (h c) -> p h c", h=2), w["nm"][:, n, :])]

            def x_values(b, m):
                pl.wait_full(dve, ("v", m), b)
                pl.frees(dve.tensor_copy(w["v"][:, b.slot, m // 2, (m % 2) * 512:(m % 2 + 1) * 512], banks[7][:, :]), ("v", m))

            def x_body(b, first, last):
                def beside(when, p):
                    nxt, prev = b.near(1), b.near(-1)
                    if not last:
                        if (when, p) == ("early", 0):
                            norm_start("x0", nxt, both(nxt), 1e-5)
                        if (when, p) == ("late", 0):
                            norm_end("x0", nxt, halves(w["xn"]), both(nxt))
                            dve.sem_inc(x_xn, 1)
                        key = {"mid": X_MID, "late": X_LATE}.get(when, {}).get(p)
                        if key and key[0] == "v":
                            x_values(nxt, key[1])
                    if not first:
                        if (when, p) == ("late", 1):
                            att_bias(prev, "b_out2")
                        if (when, p) == ("late", 2):
                            att_sum(prev, "x1", tg[:, :])
                        if (when, p) == ("late", 4):
                            norm_end("x1", prev, both(prev), halves(resb))

                attention(b, last, beside)

            norm_start("x0", b0, both(b0), 1e-5)
            norm_end("x0", b0, halves(w["xn"]), both(b0))
            dve.sem_inc(x_xn, 1)
            for m in range(4):
                x_values(b0, m)
            x_zeros(1)
            top(b0, 0)
            top(b0, 1)
            over_batches(dve, x_body, own, per=60)
            att_bias(b7, "b_out2")
            att_sum(b7, "x1", tg[:, :])
            norm_end("x1", b7, both(b7), halves(resb))

            pl, w = plan_m, m_b

            def m_copy(b):
                for h in range(2):
                    ins = dve.tensor_copy(w["xs"][:, h, :], tile(b, h))
                ins.then_inc(m_xs, 1)

            def m_route(b):
                mx, lg, oh = w["mx"], w["lg"], w["oh"]
                pl.wait_full(dve, "lg", b)
                own.did(dve.tensor_copy(lg[:, :, :].rearrange("p h e -> p (h e)"), banks[5][:, 0:2 * NE]))
                own.wait()
                dve.sem_inc(b_free[5], 1)
                link(dve.tensor_reduce(mx[:, 0, :], lg[:, :, :], AX.X, ALU.max))
                for h in range(2):
                    own.did(dve.tensor_scalar(oh[:, h, :], lg[:, h, :], mx[:, 0, h:h + 1], None, ALU.is_ge))
                own.wait()
                link(dve.tensor_tensor(lg[:, :, :], oh[:, :, :], prio[:, :, :], ALU.mult))
                link(dve.tensor_reduce(mx[:, 1, :], lg[:, :, :], AX.X, ALU.max))
                for h in range(2):
                    own.did(dve.tensor_scalar(oh[:, h, :], lg[:, h, :], mx[:, 1, h:h + 1], None, ALU.is_ge))
                own.wait()
                for h in range(2):
                    own.did(dve.tensor_copy(w["oh3"][:, h, :].rearrange("p (r c) -> p r c", c=32)[:, 0:3, 0:NE],
                                            oh[:, h:h + 1, :].broadcast_to([P, 3, NE])))
                dve.wait_ge(m_xs, b.index + 1)
                for h in range(2):
                    for e in range(NE):
                        ins = dve.tensor_scalar(w["xm"][:, h, e, :], w["xs"][:, h, :], oh[:, h, e:e + 1], None, ALU.mult)
                ins.then_inc(m_oh, 1)

            def m_masked(b):
                pl.wait_full(dve, "oh", b)
                pl.frees(dve.tensor_copy(w["ohT"][:, b.slot, :], banks[7][:, 0:S]), "oh")
                for e in (1, 3):
                    pl.wait_full(dve, ("xm", e), b)
                    pl.frees(dve.tensor_copy(w["xmT"][:, b.slot, e].rearrange("p k c -> p (k c)"), banks[4 + e][:, :]), ("xm", e))

            def m_sum(b):
                pl.wait_full(dve, "out", b)
                for h in range(2):
                    own.did(dve.tensor_tensor(resb[:, h, :], banks[7][:, h * D:(h + 1) * D], row("bo_ffn"), ALU.add))
                own.wait()
                dve.sem_inc(b_free[7], 1)
                for h in range(2):
                    own.did(dve.tensor_tensor(resb[:, h, :], resb[:, h, :], tile(b, h), ALU.add))
                own.wait()
                norm_start("m0", b, halves(resb), 1e-12)

            def m_inner(b):
                y = halves(w["y"])
                norm_end("m0", b, y, halves(resb))
                for h in range(2):
                    own.did(dve.tensor_tensor(y[h], y[h], row("lng"), ALU.mult))
                own.wait()
                for h in range(2):
                    own.did(dve.tensor_tensor(y[h], y[h], row("lnb"), ALU.add))
                own.wait()
                for h in range(2):
                    own.did(dve.tensor_tensor(resb[:, h, :], y[h], tile(b, h), ALU.add))
                own.wait()
                norm_start("m1", b, halves(resb), 1e-5)

            def m_last(b):
                dve.wait_ge(stored, 16 * (b.index + 1))
                norm_end("m1", b, halves(w["o"]), halves(resb))
                dve.sem_inc(m_out, 1)

            def m_body(b, first, last):
                if not last:
                    m_copy(b.near(1))
                if not first:
                    m_sum(b.near(-1))
                if not last:
                    m_route(b.near(1))
                if not first:
                    m_inner(b.near(-1))
                if not last:
                    m_masked(b.near(1))
                if not first:
                    m_last(b.near(-1))

            m_copy(b0)
            link(dve.memset(w["oh3"][:, :, :], 0.0))
            m_route(b0)
            dve.wait_ge(in_b3, 16 * 6)
            link(dve.tensor_copy(w["b1p"][:, :], b_1[:, :]))
            link(dve.tensor_tensor(w["b1r"][:, :], b_1[:, :], w["b1p"][:, :], ALU.subtract))
            for first, end in ((32, 64), (64, P)):
                link(dve.tensor_copy(w["b1p"][first:end, :], w["b1r"][first:end, :]))
            link(dve.tensor_tensor(w["b1r"][64:P, :], w["b1r"][64:P, :], w["b1p"][64:P, :], ALU.subtract))
            link(dve.tensor_copy(w["b1p"][64:P, :], w["b1r"][64:P, :]))
            dve.sem_inc(m_bias, 1)
            m_masked(b0)
            over_batches(dve, m_body, own, per=76)
            m_sum(b7)
            m_inner(b7)
            m_last(b7)

        @block.gpsimd
        def _(pool):
            pool.wait_ge(front_done, 1)
            pool.memset(b_1[:, :], 0.0).then_inc(pool_set, 1)

        @block.tensor
        def _(pe):
            def product(out, pairs, start=True, stop=True, skip=False):
                n = len(pairs)
                for q, (lhs, rhs) in enumerate(pairs):
                    ins = pe.matmul(out, lhs, rhs, start=start and q == 0, stop=stop and q == n - 1, skip_group_check=skip)
                return ins

            pe.sem_inc(hc_used, 2)
            pe.sem_inc(st_copied, 2)
            pe.sem_inc(h_saved, 2)
            pe.wait_ge(in_w, 16 * 5)

            def xz(c, ms):
                pe.wait_ge(in_xT[c % 2], 16 * (c // 2 + 1))
                for m in ms:
                    wait_free(pe, "xz", c, m)
                    fills(product(bank_of("xz", c, m)[:, :],
                                  [(w_in[:, k, m * P:(m + 1) * P], xTc[:, c % 2, k, :]) for k in range(KD)]), "xz", c, m)

            def xd_dt(c):
                wait_free(pe, "xd", c, 0)
                pe.wait_ge(xp_ready, c + 1)
                fills(product(bank_of("xd", c, 0)[0:96, :], [(w_xp[:, k, :], xp[:, k, :]) for k in range(ND)]), "xd", c, 0)
                pe.wait_ge(xd_ready, c + 1)
                for m in range(4):
                    wait_free(pe, "dt", c, m)
                    fills(product(bank_of("dt", c, m)[:, :], [(w_dt[:, m * P:(m + 1) * P], xd[0:DTR, :])]), "dt", c, m)

            def seeds(c):
                if c:
                    pe.wait_ge(y_ready, c)
                for d in range(ND):
                    pe.matmul(ybank[d][:, :], d_diag[:, d, :], xp[:, d, :], start=True, stop=True)

            def block_b(c, js):
                for j in js:
                    wait_free(pe, "o2", c, j)
                    lhs = [states[:, k * B + 2 * j:k * B + 2 * j + 2, :].rearrange("p b t -> p (b t)") for k in range(KD)]
                    fills(product(bank_of("o2", c, j)[:, 0:D], [(lhs[k], wo_t[:, k, :]) for k in range(KD)]), "o2", c, j)

            xz(0, range(4))
            xd_dt(0)
            xz(0, range(4, 8))
            pe.wait_ge(in_w2, 16 * 6)
            pe.wait_ge(setup_dve, 4)
            seeds(0)
            for s in range(NCH + 1):
                if s:
                    pe.wait_ge(p_ready, s)
                for j in range(2):
                    pe.wait_ge(g_free[j], sum(1 for key, n in use_at.items() if n % 2 == j and before_loop(key, s)))
                def stateless(j, u):
                    pe.wait_ge(st_copied, TC * (s - 1) + j + 1)
                    for q in range(3):
                        pe.matmul(cbank[u % 2][:, 0:16], identb[:, :], pparts[:, bass.ds(j, 1), q, :].rearrange("p o c -> p (o c)"),
                                  start=q == 0, stop=False, skip_group_check=True)

                def steps(i, last):
                    for u in range(8):
                        d = u % 4
                        j = 8 * i + u
                        if s:
                            def transition(g, parts):
                                for m in range(KD):
                                    for k in range(KD):
                                        for a in parts:
                                            ins = pe.matmul(cbank[u % 2][:, m * B:(m + 1) * B], a_parts[a][:, k, m * P:(m + 1) * P],
                                                            gs2[:, g, k * B:(k + 1) * B], start=False,
                                                            stop=(g == 1 and k == KD - 1 and a == parts[-1]), skip_group_check=True)
                                return ins

                            pe.wait_ge(gs_first, TC * (s - 1) + j + 1)
                            transition(0, (0, 1, 2))
                            filler = lambda: pe.matmul(gbank[0][:, :], identb[:, :], a_parts[0][:, :, :].rearrange("p k n -> p (k n)"),
                                                       start=True, stop=True)
                            if s < NCH:
                                filler()
                            pe.wait_ge(gs_ready, TC * (s - 1) + j + 1)
                            transition(1, (0, 1)).then_inc(chain_mm, 1)
                            if s == NCH:
                                filler()
                            if not (last and u == 7):
                                stateless(j + 1, u + 1)
                        if s < NCH:
                            jj = 64 * s + j
                            pe.wait_ge(hc_ready, jj + 6)
                            pe.matmul(ybank[d][:, :], ident[:, :], hc[:, u % 2, :], start=False, stop=True,
                                      skip_group_check=True).then_inc(hc_used, 1)

                if s:
                    stateless(0, 0)
                with pe.Fori(0, NS // 2 - 1) as i:
                    steps(i, False)
                steps(NS // 2 - 1, True)
                if s < NCH:
                    nxt = s + 1 < NCH
                    if nxt:
                        xz(s + 1, range(4))
                    pe.wait_ge(y_ready, s + 1)
                    for j in range(4):
                        wait_free(pe, "o1", s, j)
                        fills(product(bank_of("o1", s, j)[:, 0:D],
                                      [(zs[:, d, j * P:(j + 1) * P], w_o0[:, d, :]) for d in range(ND)]), "o1", s, j)
                    if nxt:
                        xd_dt(s + 1)
                    pe.wait_ge(x1_ready, s + 1)
                    for k in range(KD):
                        wait_free(pe, "xt", s, k)
                        for j in range(4):
                            ins = pe.transpose(bank_of("xt", s, k)[:, j * P:(j + 1) * P], x1[:, s % 2, j, k * P:(k + 1) * P], ident[:, :])
                        fills(ins, "xt", s, k)
                    if s:
                        pe.wait_ge(st_copied, TC * s + 2)
                        block_b(s - 1, range(2))
                    pe.wait_ge(ret_ready, KD * (s + 1))
                    for m in range(KD):
                        wait_free(pe, "inp", s, m)
                        fills(product(bank_of("inp", s, m)[:, :],
                                      [(wi_t[:, k, m * P:(m + 1) * P], ret[:, k, :]) for k in range(KD)]), "inp", s, m)
                    if s:
                        block_b(s - 1, range(2, 4))
                    pe.wait_ge(inp_ready, KD * (s + 1))
                    for m in range(KD):
                        wait_free(pe, "gate", s, m)
                        fills(product(bank_of("gate", s, m)[:, :],
                                      [(wg_t[:, k, m * P:(m + 1) * P], inp[:, k, :]) for k in range(KD)]), "gate", s, m)
                    for m in range(KD):
                        product(cbank[m][:, :], [(bm_t[:, k, m * P:(m + 1) * P], inp[:, k, :]) for k in range(KD)],
                                stop=False, skip=True)
                    if nxt:
                        xz(s + 1, (4, 5))
                    pe.wait_ge(om_ready, KD * (s + 1))
                    for m in range(KD):
                        product(cbank[m][:, :], [(a_neg[:, k, m * P:(m + 1) * P], ret[:, k, :]) for k in range(KD)],
                                start=False, skip=True).then_inc(pp_full, 1)
                    if nxt:
                        seeds(s + 1)
                        xz(s + 1, (6, 7))
                else:
                    pe.wait_ge(dve_set, 1)
                    pe.wait_ge(w_summed, 1)
                    pe.wait_ge(st_copied, TC * s + 2)
                    product(banks[4][:, 0:3], [(ones[:, :], wsum[:, :])]).then_inc(b_full[4], 1)
                    block_b(s - 1, range(4))

            pe.wait_ge(w_ready, 1)
            b0, b7 = Batch(0), Batch(B - 1)
            pl, w = plan_f, f_b

            def ffn_in(b, h):
                pe.wait_ge(f_xq, 2 * b.index + h + 1)
                pl.wait_free(pe, ("xt", h), b)
                xt = banks[4][:, 0:P].bitcast(BF16)
                for k in range(KD):
                    ins = pe.transpose(xt[:, k * P:(k + 1) * P], w["xq"][:, h, k * P:(k + 1) * P], identb[:, :])
                pl.fills(ins, ("xt", h))

            def ffn_up(b, h):
                pl.wait_freed(pe, ("xt", h), b)
                for name, wq, bank in (("g", wg_q, 0), ("u", wu_q, 2)):
                    for q in range(2):
                        pl.wait_free(pe, (name, h, q), b)
                        pl.fills(product(banks[bank + q][:, :], [(w["xqT"][:, b.slot, h, k, :], wq[:, k, q * 512:(q + 1) * 512])
                                                                 for k in range(KD)]), (name, h, q))

            def ffn_down(b, h):
                pe.wait_ge(f_hq, 2 * b.index + h + 1)
                pl.wait_free(pe, ("ht", h), b)
                ht = banks[5][:, :].bitcast(BF16)
                for m in range(NF):
                    ins = pe.transpose(ht[:, m * P:(m + 1) * P], w["hq"][:, h, m * P:(m + 1) * P], identb[:, :])
                pl.fills(ins, ("ht", h))
                pl.wait_freed(pe, ("ht", h), b)
                pl.wait_free(pe, ("dn", h), b)
                pl.fills(product(banks[6 + h][:, 0:D], [(w["hqT"][:, h, m, :], wd_q[:, m, :]) for m in range(NF)]), ("dn", h))

            def ffn(b, first, last):
                ffn_up(b, 0)
                if not first:
                    ffn_down(b.near(-1), 1)
                ffn_up(b, 1)
                if not last:
                    for h in range(2):
                        ffn_in(b.near(1), h)
                ffn_down(b, 0)

            for h in range(2):
                ffn_in(b0, h)
            over_batches(pe, ffn)
            ffn_down(b7, 1)

            def transposed(key, bank, b, src):
                pl.wait_free(pe, key, b)
                for k in range(KD):
                    for h in range(2):
                        ins = pe.transpose(bank[:, k * S + h * P:k * S + (h + 1) * P], src[:, h, k * P:(k + 1) * P], ident[:, :])
                pl.fills(ins, key)

            def attention(b, first, last, beside):
                for p in range(NP):
                    if p + 2 < NP:
                        scores(b, p + 2)
                    elif not last:
                        scores(b.near(1), p + 2 - NP)
                    beside("mid", p)
                    transposed_weights(b, p)
                    if p:
                        weighted_values(b, p - 1)
                    elif not first:
                        weighted_values(b.near(-1), NP - 1)
                    beside("late", p)

            pe.wait_ge(in_b2, 16 * 7)
            pl, w = plan_a, a_b

            def a_project(b, key):
                if key == "xt":
                    pe.wait_ge(a_xn, b.index + 1)
                    transposed("xt", banks[7], b, w["xn"])
                    return
                xnT = w["xnT"]
                if key == "q":
                    pe.wait_ge(a_xnT, b.index + 1)
                pl.wait_free(pe, key, b)
                if key in ("q", "k"):
                    for m in range(KD):
                        c = (key == "k") * D + m * P
                        ins = product(banks[7][:, m * S:(m + 1) * S], [(w_qk[:, k, c:c + P], xnT[:, k, :]) for k in range(KD)])
                for h in range(2):
                    t = slice(h * P, (h + 1) * P)
                    if key == "v":
                        ins = product(banks[6][:, h * D:(h + 1) * D], [(xnT[:, k, t], w_v[:, k, :]) for k in range(KD)])
                    if key == "ge":
                        ins = product(banks[7][:, h:h + 1], [(xnT[:, k, t], w_ent[:, k:k + 1]) for k in range(KD)])
                pl.fills(ins, key)

            def scores(b, p):
                if p == 0:
                    pe.wait_ge(a_q, b.index + 1)
                for n in heads(p):
                    pe.wait_ge(a_km, NH * b.index + n + 1)
                    pl.wait_free(pe, ("s", n), b)
                    m, bank = n // HG, banks[n % 4]
                    for h, (lo, hi) in enumerate(((0, P), (P, 3 * P))):
                        pe.matmul(bank[:, lo:hi], w["qT"][:, b.slot, m, h * P:(h + 1) * P], w["km"][:, b.slot, n, 0:hi - lo],
                                  start=True, stop=False)
                        ins = pe.matmul(bank[:, hi - P:hi], identb[:, :], causal[:, :], start=False, stop=True)
                    pl.fills(ins, ("s", n))

            def transposed_weights(b, p):
                for n in heads(p):
                    pe.wait_ge(a_norm, NH * b.index + n + 1)
                    pl.wait_free(pe, ("t", n), b)
                    for a in range(3):
                        c = slice(a * P, (a + 1) * P)
                        ins = pe.transpose(banks[4 + n % 2][:, c], w["e"][:, n % 4, c], ident[:, :])
                    pl.fills(ins, ("t", n))

            def weighted_values(b, p):
                g = p // 4
                if p == 0:
                    pe.wait_ge(a_v, b.index + 1)
                if p % 4 == 0:
                    pl.wait_free(pe, ("o", g), b)
                for n in heads(p):
                    pl.wait_freed(pe, ("t", n), b)
                    j, bank = n % HG, banks[6 + g]
                    lhs = [w["vm"][:, b.slot, h, g, j * P:(j + 1) * P] for h in range(2)]
                    pe.matmul(bank[:, 0:S], lhs[0], w["pt"][:, n % 4, 0:S], start=j == 0, stop=False)
                    ins = pe.matmul(bank[:, P:S], lhs[1], w["pt"][:, n % 4, S:S + P], start=False, stop=j == HG - 1)
                if p % 4 == 3:
                    pl.fills(ins, ("o", g))

            def a_out(b):
                for g in range(2):
                    pl.wait_freed(pe, ("o", g), b)
                pl.wait_free(pe, "out", b)
                for h in range(2):
                    ins = product(banks[7][:, h * D:(h + 1) * D], [(w["oT"][:, k, h * P:(h + 1) * P], w_o1[:, k, :]) for k in range(KD)])
                pl.fills(ins, "out")

            def a_body(b, first, last):
                def beside(when, p):
                    key = {("mid", 2): "xt", ("late", 2): "q", ("mid", 3): "k", ("late", 3): "ge", ("mid", 5): "v"}.get((when, p))
                    if key and not last:
                        a_project(b.near(1), key)
                    if (when, p) == ("late", 1) and not first:
                        a_out(b.near(-1))

                attention(b, first, last, beside)

            for key in ("xt", "q", "k", "ge", "v"):
                a_project(b0, key)
            scores(b0, 0)
            scores(b0, 1)
            over_batches(pe, a_body)
            weighted_values(b7, NP - 1)
            a_out(b7)

            pl, w = plan_x, x_b

            def x_project(b, key):
                if key == "xt":
                    pe.wait_ge(x_xn, b.index + 1)
                    transposed("xt", banks[7], b, w["xn"])
                    return
                name, m = key
                if key == ("q", 0):
                    pe.wait_ge(x_xnT, b.index + 1)
                if key == ("k", 0):
                    pe.wait_ge(x_ctx, 16 * (b.index + 1))
                pl.wait_free(pe, key, b)
                if name == "v":
                    c, h = XI + (m % 2) * 512, m // 2
                    ins = product(banks[7][:, :], [(cT[:, k, h * P:(h + 1) * P], w_xkv[:, k, c:c + 512]) for k in range(KD)])
                else:
                    wt, src = (w_xkv, cT) if name == "k" else (w_xq, w["xnT"])
                    for a in range(2):
                        c = (2 * m + a) * P
                        ins = product(banks[7][:, a * S:(a + 1) * S], [(wt[:, k, c:c + P], src[:, k, :]) for k in range(KD)])
                pl.fills(ins, key)

            def scores(b, p):
                if p == 0:
                    pl.wait_freed(pe, ("k", 3), b)
                    pl.wait_freed(pe, ("q", 3), b)
                for n in heads(p):
                    pl.wait_free(pe, ("s", n), b)
                    for h in range(2):
                        ins = pe.matmul(banks[n % 4][:, h * S:(h + 1) * S], w["qT"][:, b.slot, p, h * P:(h + 1) * P],
                                        w["kz"][:, b.slot, n, :], start=True, stop=True)
                    pl.fills(ins, ("s", n))

            def transposed_weights(b, p):
                for n in heads(p):
                    pe.wait_ge(x_norm, NH * b.index + n + 1)
                    pl.wait_free(pe, ("t", n), b)
                    for kt in range(2):
                        for h in range(2):
                            ins = pe.transpose(banks[4 + n % 2][:, kt * S + h * P:kt * S + (h + 1) * P],
                                               w["e"][:, n % 4, h * S + kt * P:h * S + (kt + 1) * P], ident[:, :])
                    pl.fills(ins, ("t", n))

            def weighted_values(b, p):
                if p == 0:
                    pl.wait_freed(pe, ("v", 3), b)
                if p % 2 == 0:
                    pl.wait_free(pe, ("o", p // 2), b)
                for n in heads(p):
                    pl.wait_freed(pe, ("t", n), b)
                    f = slice(64 * (n % 2), 64 * (n % 2) + 64)
                    ins = product(banks[6][f, (p % 2) * S:(p % 2 + 1) * S],
                                  [(w["v"][:, b.slot, kt, n * 64:(n + 1) * 64], w["pt"][:, n % 4, kt * S:(kt + 1) * S])
                                   for kt in range(2)])
                if p % 2:
                    pl.fills(ins, ("o", p // 2))

            def x_out(b):
                pl.wait_freed(pe, ("o", NP // 2 - 1), b)
                pl.wait_free(pe, "out", b)
                for h in range(2):
                    ins = product(banks[7][:, h * D:(h + 1) * D], [(w["oT"][:, p, h * P:(h + 1) * P], w_o2[:, p, :]) for p in range(NP)])
                pl.fills(ins, "out")

            def x_body(b, first, last):
                def beside(when, p):
                    key = {"mid": X_MID, "late": X_LATE}[when].get(p)
                    if key and not last:
                        x_project(b.near(1), key)
                    if (when, p) == ("late", 1) and not first:
                        x_out(b.near(-1))

                attention(b, first, last, beside)

            for key in [("k", m) for m in range(4)] + ["xt"] + [(name, m) for name in "qv" for m in range(4)]:
                x_project(b0, key)
            scores(b0, 0)
            scores(b0, 1)
            over_batches(pe, x_body)
            weighted_values(b7, NP - 1)
            x_out(b7)

            pe.wait_ge(in_b3, 16 * 6)
            pl, w = plan_m, m_b

            def m_in(b):
                pe.wait_ge(m_xs, b.index + 1)
                transposed("xt", banks[4], b, w["xs"])

            def m_logits(b):
                pl.wait_freed(pe, "xt", b)
                pl.wait_free(pe, "lg", b)
                for h in range(2):
                    ins = product(banks[5][:, h * NE:(h + 1) * NE], [(w["xT"][:, k, h * P:(h + 1) * P], w_r[:, k, :]) for k in range(KD)])
                pl.fills(ins, "lg")

            def m_masked(b):
                pe.wait_ge(m_oh, b.index + 1)
                pl.wait_free(pe, "oh", b)
                for h in range(2):
                    ins = pe.transpose(banks[7][:, h * P:(h + 1) * P], w["oh3"][:, h, :], ident[:, :])
                pl.fills(ins, "oh")
                for e in range(NE):
                    transposed(("xm", e), banks[4 + e], b, w["xm"][:, :, e])

            def m_hidden(b, m):
                if m == 0:
                    for e in range(NE):
                        pl.wait_freed(pe, ("xm", e), b)
                if m == 0:
                    pl.wait_freed(pe, "oh", b)
                    pe.wait_ge(m_bias, 1)
                pl.wait_free(pe, ("h", m), b)
                for a in range(2):
                    c = slice((2 * m + a) * P, (2 * m + a + 1) * P)
                    ins = product(banks[m][:, a * S:(a + 1) * S],
                                  [(w_1[:, e * KD + k, c], w["xmT"][:, b.slot, e, k, :]) for e in range(NE) for k in range(KD)]
                                  + [(w["b1p"][:, c], w["ohT"][:, b.slot, :])])
                pl.fills(ins, ("h", m))

            def m_project(b):
                pl.wait_freed(pe, ("h", 3), b)
                pl.wait_free(pe, "out", b)
                for h in range(2):
                    ins = product(banks[7][:, h * D:(h + 1) * D], [(w["hT"][:, m, h * P:(h + 1) * P], w_o3[:, m, :]) for m in range(NF)])
                pl.fills(ins, "out")

            def m_body(b, first, last):
                m_hidden(b, 0)
                if not first:
                    m_project(b.near(-1))
                if not last:
                    m_in(b.near(1))
                m_hidden(b, 1)
                if not last:
                    m_logits(b.near(1))
                m_hidden(b, 2)
                if not last:
                    m_masked(b.near(1))
                m_hidden(b, 3)

            m_in(b0)
            m_logits(b0)
            m_masked(b0)
            over_batches(pe, m_body)
            m_project(b7)


def _layout(inp):
    import numpy as np

    f = lambda a: np.ascontiguousarray(np.asarray(a), dtype=None)

    def ktiles(w):
        k, n = w.shape
        return w.reshape(k // P, P, n).transpose(1, 0, 2)

    def fcols(v):
        return v.reshape(-1, P).T

    a = {k: np.asarray(v) for k, v in inp.items()}
    x, c = a["x"], a["ctx_1024"]
    out = {}
    out["w_in"] = ktiles(a["L0_attn_W_in"])
    out["w_xp"] = ktiles(a["L0_attn_W_xproj"])
    out["w_dt"] = a["L0_attn_W_dt"]
    out["w_o0"] = ktiles(a["L0_attn_W_out"])
    out["w_ch"] = np.stack([ktiles(a[f"L0_xattn_{n}"].T) for n in ("Wi", "Wg", "A", "Bm", "Wo")], axis=1)
    alog = a["L0_attn_A_log"].reshape(ND, P, NS).transpose(1, 2, 0).reshape(P, NS * ND)
    bqkv = a["L1_attn_b_qkv"]
    one = lambda v: np.broadcast_to(v.reshape(1, 1), (P, 1))
    out["cols"] = np.concatenate([
        fcols(a["L0_attn_b_dt"]), alog, fcols(a["L0_attn_D"]), fcols(a["L0_xattn_bi"]), fcols(a["L0_xattn_bg"]),
        fcols(np.repeat(a["L0_xattn_decay"].reshape(-1), D // 16)),
        fcols(a["L1_attn_ln_g"]), fcols(a["L1_attn_ln_b"]), fcols(bqkv[:D]), fcols(bqkv[D:2 * D]),
        fcols(a["L1_xattn_ln_gamma"]), fcols(a["L1_xattn_ln_beta"]),
        one(a["L1_attn_b_ent"]), one(a["L1_xattn_gate"])], axis=1)
    out["rows"] = np.concatenate([a["L0_xattn_bo"], a["L1_attn_b_out"], bqkv[2 * D:], a["L1_xattn_b_out"],
                                  a["L1_ffn_bo"], a["L1_ffn_ln_gamma"], a["L1_ffn_ln_beta"]]).reshape(1, -1)
    out["xT"] = x.reshape(B, NCH, TC, KD, P).transpose(4, 1, 3, 0, 2).reshape(P, NCH, KD, CC)
    out["x_tok"] = x.reshape(4, 2, NCH, TC, D).transpose(2, 1, 3, 0, 4).reshape(NCH, P, 4, D)
    out["ctxT"] = ktiles(c.reshape(T, D).T)
    out["ident"] = np.eye(P, dtype=np.float32)
    q, k = np.arange(P)[:, None], np.arange(P)[None, :]
    out["causal"] = np.where(k > q, np.float32(-1e30), np.float32(0)).astype(np.float32)
    out["w_gate"] = ktiles(a["L0_ffn_w_gate"].T)
    out["w_up"] = ktiles(a["L0_ffn_w_up"].T)
    out["w_down"] = ktiles(a["L0_ffn_w_down"].T)
    wqkv = a["L1_attn_w_qkv"].T
    out["w_qk"] = ktiles(wqkv[:, :2 * D])
    out["w_v"] = ktiles(wqkv[:, 2 * D:])
    out["w_ent"] = fcols(a["L1_attn_w_ent"])
    out["w_o1"] = ktiles(a["L1_attn_w_out"].T)
    out["w_xq"] = ktiles(a["L1_xattn_w_q"])
    out["w_xkv"] = ktiles(a["L1_xattn_w_kv"])
    out["w_o2"] = ktiles(a["L1_xattn_w_out"])
    out["w_r"] = ktiles(a["L1_ffn_W_router"])
    out["w_1"] = ktiles(a["L1_ffn_W1"].reshape(NE * D, F))
    out["b_1"] = a["L1_ffn_b1"]
    out["w_o3"] = ktiles(a["L1_ffn_Wo"])
    out["prio"] = np.broadcast_to(np.arange(NE, 0, -1, dtype=np.float32), (P, 2, NE))
    out["headm"] = (np.arange(P)[:, None] // 16 == np.arange(8)[None, :]).astype(np.float32)
    return {k: f(v) for k, v in out.items()}


def build(nc, arrays):
    dr = {n: nc.dram_tensor("in_" + n, list(a.shape), F32, kind="ExternalInput").ap() for n, a in arrays.items()}
    dr["bcd"] = nc.dram_tensor("bcd", [NCH, 32, CC], F32, kind="Internal").ap()
    dr["out"] = nc.dram_tensor("out", [B, S, D], F32, kind="ExternalOutput").ap()
    build_program(nc, dr)


def kernel(**inputs):
    import concourse.bacc as _bacc
    from concourse.bass_utils import run_bass_kernel_spmd as _run

    nc = _bacc.Bacc("TRN2", target_bir_lowering=False, num_devices=1)
    arrays = _layout(inputs)
    build(nc, arrays)
    r = _run(nc, [{"in_" + n: v for n, v in arrays.items()}], core_ids=[0])
    return r.results[0]["out"]
```
